# Optimizing a Trainium2 kernel written in Bass

```python
import numpy as np
import jax
import jax.numpy as jnp

def _softmax(x, axis=-1):
    return jax.nn.softmax(x, axis=axis)

def _gelu(x):
    return jax.nn.gelu(x, approximate=True)

def _silu(x):
    return jax.nn.silu(x)

def _sigmoid(x):
    return jax.nn.sigmoid(x)

def _layernorm(x, axis=-1, eps=1e-05):
    m = jnp.mean(x, axis=axis, keepdims=True)
    v = jnp.var(x, axis=axis, keepdims=True)
    return (x - m) / jnp.sqrt(v + eps)

def _scatter_add(tgt, idx, src, axis=0):
    return tgt.at[idx].add(src)

def _segment_sum(src, seg, n):
    return jax.ops.segment_sum(src, seg, n)
kernel_name = 'mk_decoder_postln_d1_seqx_r8_62f0ae'

def setup_inputs(seed: int=0):
    np.random.seed(seed)
    _w = jnp.asarray

    def _rec_inputs():
        import jax
        import jax.numpy as jnp
        _rk = jax.random.key(seed)
        x = -0.0003929 + 0.9999 * jax.random.normal(jax.random.fold_in(_rk, 1), (2, 256, 128), jnp.float32)
        _lenS = 256 - jax.random.randint(jax.random.fold_in(_rk, 7), (2,), 0, max(1, 256 // 4) + 1, jnp.int32)
        _lenS2 = 512 - jax.random.randint(jax.random.fold_in(_rk, 8), (2,), 0, max(1, 512 // 4) + 1, jnp.int32)
        _ctx_1024P = jax.random.normal(jax.random.fold_in(_rk, 11), (2, 16, 128), jnp.float32)
        _ctx_1024c = jax.random.dirichlet(jax.random.fold_in(_rk, 511), 0.3 * jnp.ones((16,), jnp.float32), (2, 512))
        _ctx_1024t = jnp.einsum('bsk,bkd->bsd', _ctx_1024c, _ctx_1024P)
        _ctx_1024t = _ctx_1024t * jax.lax.rsqrt(jnp.mean(jnp.square(_ctx_1024t)) + 1e-12) * 0.953939
        ctx_1024 = 4.13588e-05 + 0.999923 * (_ctx_1024t + 0.3 * jax.random.normal(jax.random.fold_in(_rk, 611), (2, 512, 128), jnp.float32))
        return (x, ctx_1024)
    x, ctx_1024 = _rec_inputs()

    def _L0_attn_setup():
        import jax, jax.numpy as jnp
        import numpy as np
        EPS = 1e-06
        ROPE_BASE = 10000.0

        def _rope(t):
            B, T, H, D = t.shape
            half = D // 2
            inv_freq = 1.0 / ROPE_BASE ** (jnp.arange(0, half, dtype=jnp.float32) * 2.0 / D)
            ang = jnp.arange(T, dtype=jnp.float32)[:, None] * inv_freq[None, :]
            cos = jnp.cos(ang)[None, :, None, :]
            sin = jnp.sin(ang)[None, :, None, :]
            x1, x2 = (t[..., :half], t[..., half:])
            return jnp.concatenate([x1 * cos - x2 * sin, x2 * cos + x1 * sin], axis=-1)

        def _rmsnorm(t, w):
            ms = jnp.mean(t * t, axis=-1, keepdims=True)
            return t * jax.lax.rsqrt(ms + EPS) * w
        key = jax.random.key(seed)
        k1, k2, k3 = jax.random.split(key, 3)
        B, T, C, H = (2, 256, 128, 16)
        D = C // H
        s = 1.0 / np.sqrt(C)
        return {'x': jax.random.normal(k1, (B, T, C), dtype=jnp.float32), 'w_qkv': jax.random.normal(k2, (3 * C, C), dtype=jnp.float32) * s, 'w_out': jax.random.normal(k3, (C, C), dtype=jnp.float32) * s, 'q_norm_w': jnp.ones((D,), dtype=jnp.float32), 'k_norm_w': jnp.ones((D,), dtype=jnp.float32)}
    _L0_attn_all = _L0_attn_setup()
    _L0_attn_in = {k: v for k, v in _L0_attn_all.items() if k in ('w_qkv', 'w_out', 'q_norm_w', 'k_norm_w')}
    del _L0_attn_all

    def _L0_xattn_setup():
        import jax, jax.numpy as jnp
        import numpy as np
        H = 128
        B = 8
        L_CHAR = 256
        L_SUB = 128

        def _linear(x, W, b):
            return jnp.einsum('blh,oh->blo', x, W) + b

        def _interp_linear(x, out_len):
            L_in = x.shape[1]
            pos = (jnp.arange(out_len, dtype=x.dtype) + 0.5) * (L_in / out_len) - 0.5
            pos = jnp.clip(pos, 0.0, L_in - 1)
            lo = jnp.floor(pos).astype(jnp.int32)
            hi = jnp.minimum(lo + 1, L_in - 1)
            w = (pos - lo.astype(x.dtype))[None, :, None]
            return x[:, lo] * (1 - w) + x[:, hi] * w
        key = jax.random.key(seed)
        ks = jax.random.split(key, 18)
        s = 0.02
        inp = {'char_emb': jax.random.normal(ks[0], (B, L_CHAR, H), jnp.float32), 'subword_emb': jax.random.normal(ks[1], (B, L_SUB, H), jnp.float32)}
        names = ['Wq_c', 'Wk_s', 'Wv_s', 'Wq_s', 'Wk_c', 'Wv_c']
        for i, n in enumerate(names):
            inp[n] = jax.random.normal(ks[2 + 2 * i], (H, H), jnp.float32) * s
            inp['b' + n[1:]] = jax.random.normal(ks[3 + 2 * i], (H,), jnp.float32) * s
        inp['Wg'] = jax.random.normal(ks[14], (H, 2 * H), jnp.float32) * s
        inp['bg'] = jax.random.normal(ks[15], (H,), jnp.float32) * s
        return inp
    _L0_xattn_all = _L0_xattn_setup()
    _L0_xattn_in = {k: v for k, v in _L0_xattn_all.items() if k in ('Wq_c', 'bq_c', 'Wk_s', 'bk_s', 'Wv_s', 'bv_s', 'Wq_s', 'bq_s', 'Wk_c', 'bk_c', 'Wv_c', 'bv_c', 'Wg', 'bg')}
    del _L0_xattn_all

    def _L0_ffn_setup():
        import jax, jax.numpy as jnp
        import numpy as np
        B, L, D = (2, 128, 128)
        HID, E, K = (256, 8, 2)
        key = jax.random.key(seed)
        ks = jax.random.split(key, 4)
        std = 0.02
        return {'x': jax.random.normal(ks[0], (B, L, D), dtype=jnp.float32), 'router_scale': jnp.ones((D,), dtype=jnp.float32), 'router_w': jax.random.normal(ks[1], (D, E), dtype=jnp.float32) * std, 'gating_w': jax.random.normal(ks[2], (E, 2, HID, D), dtype=jnp.float32) * std, 'linear_w': jax.random.normal(ks[3], (E, HID, D), dtype=jnp.float32) * std, 'per_expert_scale': jnp.ones((E,), dtype=jnp.float32)}
    _L0_ffn_all = _L0_ffn_setup()
    _L0_ffn_in = {k: v for k, v in _L0_ffn_all.items() if k in ('router_scale', 'router_w', 'gating_w', 'linear_w', 'per_expert_scale')}
    del _L0_ffn_all
    return {'x': x, 'ctx_1024': ctx_1024, 'L0_attn_w_qkv': _L0_attn_in['w_qkv'], 'L0_attn_w_out': _L0_attn_in['w_out'], 'L0_attn_q_norm_w': _L0_attn_in['q_norm_w'], 'L0_attn_k_norm_w': _L0_attn_in['k_norm_w'], 'L0_xattn_Wq_c': _L0_xattn_in['Wq_c'], 'L0_xattn_bq_c': _L0_xattn_in['bq_c'], 'L0_xattn_Wk_s': _L0_xattn_in['Wk_s'], 'L0_xattn_bk_s': _L0_xattn_in['bk_s'], 'L0_xattn_Wv_s': _L0_xattn_in['Wv_s'], 'L0_xattn_bv_s': _L0_xattn_in['bv_s'], 'L0_xattn_Wq_s': _L0_xattn_in['Wq_s'], 'L0_xattn_bq_s': _L0_xattn_in['bq_s'], 'L0_xattn_Wk_c': _L0_xattn_in['Wk_c'], 'L0_xattn_bk_c': _L0_xattn_in['bk_c'], 'L0_xattn_Wv_c': _L0_xattn_in['Wv_c'], 'L0_xattn_bv_c': _L0_xattn_in['bv_c'], 'L0_xattn_Wg': _L0_xattn_in['Wg'], 'L0_xattn_bg': _L0_xattn_in['bg'], 'L0_ffn_router_scale': _L0_ffn_in['router_scale'], 'L0_ffn_router_w': _L0_ffn_in['router_w'], 'L0_ffn_gating_w': _L0_ffn_in['gating_w'], 'L0_ffn_linear_w': _L0_ffn_in['linear_w'], 'L0_ffn_per_expert_scale': _L0_ffn_in['per_expert_scale']}

def reference(x, ctx_1024, L0_attn_w_qkv, L0_attn_w_out, L0_attn_q_norm_w, L0_attn_k_norm_w, L0_xattn_Wq_c, L0_xattn_bq_c, L0_xattn_Wk_s, L0_xattn_bk_s, L0_xattn_Wv_s, L0_xattn_bv_s, L0_xattn_Wq_s, L0_xattn_bq_s, L0_xattn_Wk_c, L0_xattn_bk_c, L0_xattn_Wv_c, L0_xattn_bv_c, L0_xattn_Wg, L0_xattn_bg, L0_ffn_router_scale, L0_ffn_router_w, L0_ffn_gating_w, L0_ffn_linear_w, L0_ffn_per_expert_scale):
    import jax
    import jax.numpy as jnp

    def _L0_attn_ref(x, w_qkv, w_out, q_norm_w, k_norm_w):
        import jax, jax.numpy as jnp
        import numpy as np
        EPS = 1e-06
        ROPE_BASE = 10000.0

        def _rope(t):
            B, T, H, D = t.shape
            half = D // 2
            inv_freq = 1.0 / ROPE_BASE ** (jnp.arange(0, half, dtype=jnp.float32) * 2.0 / D)
            ang = jnp.arange(T, dtype=jnp.float32)[:, None] * inv_freq[None, :]
            cos = jnp.cos(ang)[None, :, None, :]
            sin = jnp.sin(ang)[None, :, None, :]
            x1, x2 = (t[..., :half], t[..., half:])
            return jnp.concatenate([x1 * cos - x2 * sin, x2 * cos + x1 * sin], axis=-1)

        def _rmsnorm(t, w):
            ms = jnp.mean(t * t, axis=-1, keepdims=True)
            return t * jax.lax.rsqrt(ms + EPS) * w
        B, T, C = x.shape
        H = 16
        D = C // H
        qkv = x @ w_qkv.T
        q, k, v = jnp.split(qkv, 3, axis=-1)
        q = q.reshape(B, T, H, D)
        k = k.reshape(B, T, H, D)
        v = v.reshape(B, T, H, D)
        q = _rmsnorm(_rope(q), q_norm_w)
        k = _rmsnorm(_rope(k), k_norm_w)
        scale = 1.0 / np.sqrt(D)
        attn = jnp.einsum('bqhd,bkhd->bhqk', q, k) * scale
        causal = jnp.tril(jnp.ones((T, T), dtype=bool))
        attn = jnp.where(causal[None, None], attn, -jnp.inf)
        attn = jax.nn.softmax(attn, axis=-1)
        out = jnp.einsum('bhqk,bkhd->bqhd', attn, v).reshape(B, T, C)
        return out @ w_out.T

    def _L0_xattn_ref(char_emb, subword_emb, Wq_c, bq_c, Wk_s, bk_s, Wv_s, bv_s, Wq_s, bq_s, Wk_c, bk_c, Wv_c, bv_c, Wg, bg):
        import jax, jax.numpy as jnp
        import numpy as np
        H = 128
        B = 8
        L_CHAR = 256
        L_SUB = 128

        def _linear(x, W, b):
            return jnp.einsum('blh,oh->blo', x, W) + b

        def _interp_linear(x, out_len):
            L_in = x.shape[1]
            pos = (jnp.arange(out_len, dtype=x.dtype) + 0.5) * (L_in / out_len) - 0.5
            pos = jnp.clip(pos, 0.0, L_in - 1)
            lo = jnp.floor(pos).astype(jnp.int32)
            hi = jnp.minimum(lo + 1, L_in - 1)
            w = (pos - lo.astype(x.dtype))[None, :, None]
            return x[:, lo] * (1 - w) + x[:, hi] * w
        h = char_emb.shape[-1]
        scale = 1.0 / jnp.sqrt(jnp.asarray(h, char_emb.dtype))
        Q_char = _linear(char_emb, Wq_c, bq_c)
        K_sub = _linear(subword_emb, Wk_s, bk_s)
        V_sub = _linear(subword_emb, Wv_s, bv_s)
        scores = jnp.einsum('bqh,bkh->bqk', Q_char, K_sub) * scale
        char2sub = jnp.einsum('bqk,bkh->bqh', jax.nn.softmax(scores, axis=-1), V_sub)
        Q_sub = _linear(subword_emb, Wq_s, bq_s)
        K_char = _linear(char_emb, Wk_c, bk_c)
        V_char = _linear(char_emb, Wv_c, bv_c)
        scores2 = jnp.einsum('bqh,bkh->bqk', Q_sub, K_char) * scale
        sub2char = jnp.einsum('bqk,bkh->bqh', jax.nn.softmax(scores2, axis=-1), V_char)
        L_char = char_emb.shape[1]
        if sub2char.shape[1] != L_char:
            sub2char = _interp_linear(sub2char, L_char)
        gate_in = jnp.concatenate([char2sub, sub2char], axis=-1)
        gate = jax.nn.sigmoid(jnp.einsum('blh,oh->blo', gate_in, Wg) + bg)
        return gate * char2sub + (1 - gate) * sub2char

    def _L0_ffn_ref(x, router_scale, router_w, gating_w, linear_w, per_expert_scale):
        import jax, jax.numpy as jnp
        import numpy as np
        B, L, D = (2, 128, 128)
        HID, E, K = (256, 8, 2)
        d = x.shape[-1]
        var = jnp.mean(jnp.square(x), axis=-1, keepdims=True)
        r_in = x * jax.lax.rsqrt(var + 1e-06)
        r_in = r_in * jax.lax.rsqrt(jnp.array(d, dtype=r_in.dtype)) * router_scale
        logits = jnp.dot(r_in, router_w).astype(jnp.float32)
        probs = jax.nn.softmax(logits, axis=-1)
        _, top_k_idx = jax.lax.top_k(logits, K)
        indicator = jax.nn.one_hot(top_k_idx, probs.shape[-1], dtype=probs.dtype)
        gate_weights = indicator.sum(axis=-2) * probs
        renorm = jnp.sum(gate_weights, axis=-1, keepdims=True)
        renorm = jnp.where(renorm > 0.0, renorm, 1.0)
        weights = probs / renorm
        top_k_w = jnp.take_along_axis(weights, top_k_idx, axis=-1)
        combine = jnp.einsum('blke,blk->ble', indicator, top_k_w)
        combine = combine * per_expert_scale
        gate0 = jnp.einsum('bld,ehd->bleh', x, gating_w[:, 0])
        gate1 = jnp.einsum('bld,ehd->bleh', x, gating_w[:, 1])
        act = jax.nn.gelu(gate0) * gate1
        out = jnp.einsum('bleh,ehd,ble->bld', act, linear_w, combine)
        return out.astype(x.dtype)
    x = _layernorm(x + _L0_attn_ref(x, L0_attn_w_qkv, L0_attn_w_out, L0_attn_q_norm_w, L0_attn_k_norm_w), axis=-1)
    x = _layernorm(x + _L0_xattn_ref(x, ctx_1024, L0_xattn_Wq_c, L0_xattn_bq_c, L0_xattn_Wk_s, L0_xattn_bk_s, L0_xattn_Wv_s, L0_xattn_bv_s, L0_xattn_Wq_s, L0_xattn_bq_s, L0_xattn_Wk_c, L0_xattn_bk_c, L0_xattn_Wv_c, L0_xattn_bv_c, L0_xattn_Wg, L0_xattn_bg), axis=-1)
    x = _layernorm(x + _L0_ffn_ref(x, L0_ffn_router_scale, L0_ffn_router_w, L0_ffn_gating_w, L0_ffn_linear_w, L0_ffn_per_expert_scale), axis=-1)
    return x

_drawn_inputs = setup_inputs


def setup_inputs(seed=0):
    import zlib

    import numpy as np

    out = dict(_drawn_inputs(seed))
    spreads = {'L0_attn_q_norm_w': (1.0, 0.2),
     'L0_attn_k_norm_w': (1.0, 0.6),
     'L0_ffn_router_scale': (1.0, 0.6),
     'L0_ffn_per_expert_scale': (1.0, 0.6)}
    factors = {'L0_xattn_Wq_c': 8.0,
     'L0_xattn_bq_c': 8.0,
     'L0_xattn_Wk_s': 8.0,
     'L0_xattn_bk_s': 8.0,
     'L0_xattn_bv_s': 5.371,
     'L0_xattn_Wq_s': 8.0,
     'L0_xattn_bq_s': 8.0,
     'L0_xattn_Wk_c': 8.0,
     'L0_xattn_bk_c': 8.0,
     'L0_xattn_Wv_c': 4.843,
     'L0_xattn_bv_c': 5.506,
     'L0_xattn_Wg': 8.0,
     'L0_xattn_bg': 8.0,
     'L0_ffn_router_w': 8.0,
     'L0_ffn_gating_w': 8.0,
     'L0_ffn_linear_w': 8.0}
    for name, (base, spread) in spreads.items():
        noise = np.random.default_rng([zlib.crc32(name.encode()), seed]).standard_normal(out[name].shape)
        drawn = base * np.exp(spread * noise) if base else spread * noise
        out[name] = jnp.asarray(drawn.astype(out[name].dtype))
    for name, factor in factors.items():
        out[name] = (out[name] * factor).astype(out[name].dtype)
    return out
```

```python
from contextlib import ExitStack

import concourse.bass as bass
from concourse import mybir

F32 = mybir.dt.float32
BF16 = mybir.dt.bfloat16
U16 = mybir.dt.uint16
U32 = mybir.dt.uint32
ALU = mybir.AluOpType
ACT = mybir.ActivationFunctionType
AX = mybir.AxisListType

P = 128
B, T, C = 2, 256, 128
H, D = 16, 8
L = 512
E, HID = 8, 256
N = B * T
NT = N // P
HT = HID // P
M = B * H
BLOCKS = 3
PIECES = 3
LOWEST = -1e30
Q_PIECE = (0, 1, 2, 0, 1, 0)
K_PIECE = (0, 0, 0, 1, 1, 2)

CF = {"ident": (0, 128), "cos": (128, 384), "sin": (384, 640), "mean8": (640, 768), "pair": (768, 832)}
CB = {"ident": (0, 128), "mask": (128, 256), "sel_expert": (256, 256 + E * P)}
WX = ["Wq_c", "Wk_s", "Wv_s", "Wq_s", "Wk_c", "Wv_c", "Wg_c", "Wg_s"]
SM = {"bq_c": 0, "bk_s": 1, "bv_s": 2, "bq_s": 3, "bk_c": 4, "bv_c": 5, "bg": 6, "q_norm": 7, "k_norm": 8,
      "router_scale": 9, "router_w": 10, "expert_scale": 18}
SMW = 26


def post_norm_decoder(nc, xT, x_tok, ctxT, w_qkv, w_out, w_x, small, gating, linear, const_f, const_b, out):
    ctx = ExitStack()

    def sb(name, shape, dt=F32):
        return ctx.enter_context(nc.sbuf_tensor(name, shape, dt))

    def sem(name):
        return ctx.enter_context(nc.semaphore(name))

    with ctx:
        xT_s = sb("xT_s", [P, N])
        x_s = sb("x_s", [P, NT, C])
        ctxT_s = sb("ctxT_s", [P, B * L])
        wqkv_s = sb("wqkv_s", [P, 5, P])
        wout_s = sb("wout_s", [P, P])
        wx_s = sb("wx_s", [P, 8, P])
        sm_s = sb("sm_s", [P, SMW])
        gat_s = sb("gat_s", [P, E, 2, HT, P])
        lin_s = sb("lin_s", [P, E, HT, P])
        cf = sb("cf", [P, 832])
        cb = sb("cb", [P, 256 + E * P], BF16)
        eps_rms = sb("eps_rms", [P, 1])
        eps_ln = sb("eps_ln", [P, 1])
        warm = sb("warm", [P, 512], BF16)

        def constf(name):
            return cf[:, CF[name][0]:CF[name][1]]

        def constb(name, rows=P):
            return cb[0:rows, CB[name][0]:CB[name][1]]

        def wx(name):
            return wx_s[:, WX.index(name), :]

        def smcol(name, n=1):
            return sm_s[:, SM[name]:SM[name] + n]

        def diagonal(flat, at):
            return bass.AP(flat.tensor, flat.offset + at, [list(flat.ap[0]), [P + D, H // 2], [1, D]])

        ident = constf("ident")
        identb = constb("ident")
        sel_expert = constb("sel_expert", PIECES * E).rearrange("r (e m) -> r e m", e=E)
        cos = constf("cos").rearrange("p (o t) -> p o t", o=1)
        sin = constf("sin").rearrange("p (o t) -> p o t", o=1)

        arena = sb("arena", [P, 7 * 2 * N])
        at = [0]

        def later(n):
            at[0] += n
            assert at[0] <= 7 * 2 * N
            return arena[:, at[0] - n:at[0]]


        def early(i):
            return arena[:, i * 2 * N:(i + 1) * 2 * N].rearrange("p (i n) -> p i n", i=2)

        sq, lnms, rstd, rot_c, rot_s, rot, qkn = (early(i) for i in range(7))
        res = sb("res", [P, 2, N])
        piece = sb("piece", [P, 2, PIECES, N], BF16)
        Q6 = sb("Q6", [P, H, N], BF16)
        K6 = sb("K6", [P, H // 2, N], BF16)
        VP = sb("VP", [P, NT, H, P])
        nmax = sb("nmax", [P, M, 2])
        probs = sb("probs", [P, 4, BLOCKS * P])
        probsT = sb("probsT", [P, 4, BLOCKS * P])
        lnsum = sb("lnsum", [P, B, T])
        rsum = sb("rsum", [P, B, T])
        attnT = sb("attnT", [P, N])
        qscale = sb("qscale", [P, 1])

        pre = sb("pre", [P, 3, NT, C])
        stats = sb("stats", [P, 3, NT, 6])
        mv = sb("mv", [P, 3, NT, 2])
        rs_ln = sb("rs_ln", [P, 3, NT])
        x1 = sb("x1", [P, NT, C])
        x1T = sb("x1T", [P, N])
        x2 = sb("x2", [P, NT, C])
        x2T = sb("x2T", [P, N])
        y_s = sb("y_s", [P, NT, C])

        KsT = sb("KsT", [P, B, L])
        QsT = sb("QsT", [P, B, L])
        Vs = sb("Vs", [P, B * L // P, C])
        QcT = sb("QcT", [P, N])
        KcT = sb("KcT", [P, N])
        Vc = sb("Vc", [P, NT, C])
        nm1 = sb("nm1", [P, NT])
        sum1 = sb("sum1", [P, NT])
        r1 = sb("r1", [P, NT])
        after = VP[:, :, :, :].rearrange("p (b t) h c -> p b (t h c)", b=B)
        P1 = after[:, :, 0:2 * L].rearrange("p b (t k) -> p b t k", t=2)
        P2 = after[:, :, 2 * L:4 * L].rearrange("p b (t k) -> p b t k", t=4)
        gd = after[:, :, 4 * L:4 * L + T]
        mixT = after[:, :, 4 * L + T:4 * L + 2 * T]
        PT1 = later(2048).rearrange("p (b k q) -> p b k q", b=B, k=4)
        nm2 = sb("nm2", [P, 8])
        sum2 = sb("sum2", [P, 8])
        r2 = sb("r2", [P, 8])
        pair_r = sb("pair_r", [P, 8, 64])
        PT2 = later(1024).rearrange("p (b k q) -> p b k q", b=B, k=2)
        c2s = later(N)
        s2c = later(N)
        diff = res[:, 0, :]
        nbg = sb("nbg", [P, 1])
        hbg = sb("hbg", [P, 1])
        eg = res[:, 1, :]
        eg1 = later(N)
        gate = later(N)

        rw = sb("rw", [P, E])
        nhalf = sb("nhalf", [P, 2])
        sd2 = sb("sd2", [P, NT])
        ms2 = sb("ms2", [P, NT])
        rr2 = sb("rr2", [P, NT])
        logit = sb("logit", [P, NT, E])
        nml = sb("nml", [P, NT])
        shift = sb("shift", [P, NT, E])
        ex = sb("ex", [P, NT, E])
        beats = sb("beats", [P, NT, E, E])
        ties = sb("ties", [P, NT, E, E])
        rank = sb("rank", [P, NT, E])
        lower = sb("lower", [P, E, E])
        gw = sb("gw", [P, NT, E])
        ren = sb("ren", [P, NT])
        renr = sb("renr", [P, NT])
        cw = sb("cw", [P, NT, E])
        comb = sb("comb", [P, NT, E])
        combr = sb("combr", [P, NT, E])
        combp = sb("combp", [P, NT, PIECES, E], BF16)
        combT = sb("combT", [PIECES * E, N], BF16)
        x2c = Q6[:, :, :].rearrange("p h n -> p (h n)").bitcast(F32).rearrange("p (b e n) -> p b e n", b=B, e=E)
        gl = later(1024).rearrange("p (i n) -> p i n", i=4)
        acts = later(1024).rearrange("p (i n) -> p i n", i=4)

        psum = ctx.enter_context(nc.psum_tensor("psum", [P, 8, 512], F32))
        banks = [psum[:, i, :] for i in range(8)]
        XBANKS = ((6, 0, 1), (7, 2, 3))
        FBANKS = (4, 5, 0)
        SPREAD, DOWN = 6, (1, 2)

        def bk(b, i):
            return banks[XBANKS[b]["ABC".index(i)]]

        def score_bank(m):
            return banks[m % 4 if m < H else 2 + m % 2]

        def trans_bank(m):
            return banks[4 + m % 2]

        qs = nc.dram_tensor("q_pieces", [H, PIECES, D, N], BF16).ap()
        ks = nc.dram_tensor("k_rows", [H, len(K_PIECE), D, N], BF16).ap()

        names = """in_x in_wqkv in_small in_cf in_cb in_ctx in_wx in_xtok in_wout in_gat in_lin
            zeroed_q zeroed_k zeroed_v consts eps
            proj vproj sq_done ms_done rs_done rot_done qkn_done p0 p1 p2 r1d r2d q_saved k_saved q6_in k6_in vp_done
            ctx_mm ctx_ev s_done max_done exp_done t_mm t_done_v t_done_a pv_done rsum_done attn_done
            wout_done pre_done mv_done rsln_done xn_done x2n_done xt_mm xt_done x2t_mm x2t_done
            qkc_mm qkc_done vc_mm vc_done s1_mm nm1_done exp1_done p1n_done pt1_mm pt1_done
            s2_mm nm2_done exp2_done pair_done pt2_mm pt2_done c2s_mm s2c_mm c2s_done s2c_done gate_mm eg_done gate_read mix_done
            mix_mm rw_done rr2_done logit_mm logit_done ex_done comb_done combT_mm combT_done bc_mm x2c_done warm_ready
            gates_mm gl_done act_done out_mm y_ready stored chain_v chain_a chain_p""".split()
        S = {n: sem(n) for n in names}
        SCALE = float(D) ** -0.5
        XSCALE = float(C) ** -0.5

        def transposed(m):
            return (S["t_done_a"], m // 4 + 1) if m % 4 == 3 else (S["t_done_v"], m - m // 4 + 1)

        block = ctx.enter_context(nc.Block())

        @block.sync
        def _(sp):
            sp.dma_start(xT_s[:, :], xT).then_inc(S["in_x"], 16)
            sp.dma_start(cf[:, :], const_f).then_inc(S["in_cf"], 16)
            sp.dma_start(ctxT_s[:, :], ctxT).then_inc(S["in_ctx"], 16)
            sp.dma_start(cb[:, :].bitcast(U16), const_b).then_inc(S["in_cb"], 16)
            for n, ready in enumerate(("p0", "p1", "p2")):
                sp.wait_ge(S[ready], 1)
                sp.dma_start(qs[:, n], piece[:, 0, n, :]).then_inc(S["q_saved"], 16)
            sp.wait_ge(S["q_saved"], 3 * 16)
            sp.wait_ge(S["zeroed_q"], 1)
            q_rows = [(0, 3), (3, 2), (5, 1)]
            for odd in range(2):
                src = qs.rearrange("(p o) n d t -> o (n d) p t", o=2)[odd]
                for at, n in q_rows:
                    r0 = 64 * odd + at * D
                    sp.dma_start(Q6[r0:r0 + n * D, odd:H:2, :], src[0:n * D]).then_inc(S["q6_in"], 16)
            sp.wait_ge(S["k6_in"], 2 * 16)
            sp.dma_start(x_s[:, :, :], x_tok).then_inc(S["in_xtok"], 16)
            sp.dma_start(wout_s[:, :], w_out).then_inc(S["in_wout"], 16)
            sp.dma_start(gat_s[:, 0:4], gating[:, 0:4]).then_inc(S["in_gat"], 16)
            sp.dma_start(gat_s[:, 4:8], gating[:, 4:8]).then_inc(S["in_gat"], 16)
            sp.dma_start(lin_s[:, :, :, :], linear).then_inc(S["in_lin"], 16)
            for b in range(B):
                sp.wait_ge(S["y_ready"], 2 * (b + 1))
                sp.dma_start(out[:, 2 * b:2 * b + 2, :], y_s[:, 2 * b:2 * b + 2, :]).then_inc(S["stored"], 16)
            sp.wait_ge(S["stored"], 16 * B)

        @block.gpsimd
        def _(pool):
            chain = [0]

            def link(ins):
                chain[0] += 1
                ins.then_inc(S["chain_p"], 1)
                pool.wait_ge(S["chain_p"], chain[0])

            nc.gpsimd.memset(eps_rms[:, :], 1e-6)
            nc.gpsimd.memset(nhalf[:, :], -0.5)
            nc.gpsimd.memset(eps_ln[:, :], 1e-5).then_inc(S["eps"], 1)
            nc.gpsimd.memset(K6[:, :, :].bitcast(U32), 0).then_inc(S["zeroed_k"], 1)
            nc.gpsimd.memset(VP[:, 0:2, :, :], 0.0)
            link(nc.gpsimd.memset(VP[:, 2:4, :, :], 0.0))
            for half in range(2):
                for t in range(NT):
                    ones = VP[:, t, half * (H // 2):(half + 1) * (H // 2), :].rearrange("p h c -> p (h c)")
                    last = nc.gpsimd.memset(diagonal(ones, 64 * (1 - half)), 1.0)
            last.then_inc(S["zeroed_v"], 1)
            link(nc.gpsimd.memset(lower[:, :, :], 0.0))
            nc.gpsimd.affine_select(out=lower[:, :, :], in_=lower[:, :, :], compare_op=ALU.is_ge, fill=1.0, base=0,
                                    pattern=[[-1, E], [1, E]], channel_multiplier=0).then_inc(S["consts"], 1)
            pool.wait_ge(S["p0"], 2)
            nc.gpsimd.tensor_tensor(res[:, 1, :], qkn[:, 1, :], piece[:, 1, 0, :], ALU.subtract).then_inc(S["r2d"], 1)
            pool.wait_ge(S["p1"], 2)
            pool.wait_ge(S["r2d"], 1)
            nc.gpsimd.tensor_tensor(piece[:, 1, 2, :], res[:, 1, :], piece[:, 1, 1, :], ALU.subtract).then_inc(S["r2d"], 1)

            def rs_norm(i, b):
                t2 = slice(2 * b, 2 * b + 2)
                pool.wait_ge(S["mv_done"], 2 * i + b + 1)
                link(nc.gpsimd.tensor_scalar(sd2[:, t2], mv[:, i, t2, 1], 1e-5, None, ALU.add))
                nc.gpsimd.tensor_tensor(rs_ln[:, i, t2], sd2[:, t2], nhalf[:, :], ALU.pow).then_inc(S["rsln_done"], 1)

            def rms2(b):
                t2 = slice(2 * b, 2 * b + 2)
                pool.wait_ge(S["rsln_done"], 2 + b + 1)
                link(nc.gpsimd.tensor_tensor(sd2[:, t2], mv[:, 1, t2, 1], rs_ln[:, 1, t2], ALU.mult))
                link(nc.gpsimd.tensor_tensor(ms2[:, t2], sd2[:, t2], rs_ln[:, 1, t2], ALU.mult))
                link(nc.gpsimd.tensor_scalar(ms2[:, t2], ms2[:, t2], 1e-6, None, ALU.add))
                nc.gpsimd.tensor_tensor(rr2[:, t2], ms2[:, t2], nhalf[:, :], ALU.pow).then_inc(S["rr2_done"], 1)

            rs_norm(0, 0)
            rs_norm(0, 1)
            rs_norm(1, 0)
            rms2(0)
            rs_norm(1, 1)
            rms2(1)
            rs_norm(2, 0)
            rs_norm(2, 1)

        @block.scalar
        def _(act):
            chain = [0]

            def link(ins):
                chain[0] += 1
                ins.then_inc(S["chain_a"], 1)
                act.wait_ge(S["chain_a"], chain[0])

            A = nc.scalar.activation
            table = nc.scalar.preload_act_table_set
            exp_set, gelu_set = "natural_log_exp_and_others", "gelu_apprx_tanh_and_others"
            table(exp_set)
            act.dma_start(wqkv_s[:, :, :], w_qkv).then_inc(S["in_wqkv"], 16)
            act.dma_start(sm_s[:, :], small).then_inc(S["in_small"], 16)
            act.dma_start(wx_s[:, :, :], w_x).then_inc(S["in_wx"], 16)
            act.wait_ge(S["eps"], 1)
            for i in range(2):
                act.wait_ge(S["proj"], 1 + 2 * i)
                A(sq[:, i, :], banks[2 * i], ACT.Square).then_inc(S["sq_done"], 1)
            for i in range(2):
                act.wait_ge(S["ms_done"], i + 1)
                link(A(lnms[:, i, :], banks[5 + i], ACT.Ln, bias=eps_rms[:, :]))
                A(rstd[:, i, :], lnms[:, i, :], ACT.Exp, scale=-0.5).then_inc(S["rs_done"], 1)
            act.wait_ge(S["qkn_done"], 1)
            A(piece[:, 0, 0, :], qkn[:, 0, :], ACT.Copy).then_inc(S["p0"], 1)
            act.wait_ge(S["qkn_done"], 2)
            A(piece[:, 1, 0, :], qkn[:, 1, :], ACT.Copy).then_inc(S["p0"], 1)

            def save_k(n):
                for row, p in enumerate(K_PIECE):
                    if p == n:
                        act.dma_start(ks[:, row], piece[:, 1, n, :]).then_inc(S["k_saved"], 16)
            act.wait_ge(S["r1d"], 1)
            A(piece[:, 0, 1, :], res[:, 0, :], ACT.Copy).then_inc(S["p1"], 1)
            act.wait_ge(S["r2d"], 1)
            A(piece[:, 1, 1, :], res[:, 1, :], ACT.Copy).then_inc(S["p1"], 1)
            act.wait_ge(S["p0"], 2)
            save_k(0)
            act.wait_ge(S["p1"], 2)
            save_k(1)
            act.wait_ge(S["r2d"], 2)
            save_k(2)
            act.wait_ge(S["k_saved"], 16 * len(K_PIECE))
            act.wait_ge(S["zeroed_k"], 1)
            for odd in range(2):
                src = ks.rearrange("(p o) n d t -> o (n d) p t", o=2)[odd]
                act.dma_start(K6[64 * odd:64 * odd + len(K_PIECE) * D, :, :], src).then_inc(S["k6_in"], 16)
            act.wait_ge(S["ctx_mm"], 1)
            A(KsT[:, 0, :], banks[0], ACT.Identity, bias=smcol("bk_s")).then_inc(S["ctx_ev"], 1)
            act.wait_ge(S["ctx_mm"], 2)
            A(KsT[:, 1, :], banks[1], ACT.Identity, bias=smcol("bk_s")).then_inc(S["ctx_ev"], 1)
            act.wait_ge(S["ctx_mm"], 5)
            A(Vs[:, 0:4, :], banks[4].rearrange("p (t c) -> p t c", t=4), ACT.Copy).then_inc(S["ctx_ev"], 1)
            act.wait_ge(S["ctx_mm"], 6)
            A(Vs[:, 4:8, :], banks[5].rearrange("p (t c) -> p t c", t=4), ACT.Copy).then_inc(S["ctx_ev"], 1)

            def exps(m):
                act.wait_ge(S["max_done"], m + 1)
                if m >= 4:
                    act.wait_ge(S["t_mm"], m - 3)
                A(probs[:, m % 4, 0:P], score_bank(m)[:, 0:P], ACT.Exp, bias=nmax[:, m, 0:1])
                A(probs[:, m % 4, P:3 * P], score_bank(m)[:, P:3 * P], ACT.Exp, bias=nmax[:, m, 1:2]).then_inc(S["exp_done"], 1)

            def trans_out(m):
                act.wait_ge(S["t_mm"], m + 1)
                if m >= 4:
                    act.wait_ge(S["pv_done"], m - 3)
                A(probsT[:, m % 4, :], trans_bank(m)[:, 0:BLOCKS * P], ACT.Copy).then_inc(S["t_done_a"], 1)

            def heads(first, last):
                for m in range(first, last):
                    if m < M:
                        exps(m)
                    if m >= 2 and (m - 2) % 4 == 3:
                        trans_out(m - 2)

            def sums(b):
                act.wait_ge(S["pv_done"], H * (b + 1))
                A(lnsum[0:64, b, :], banks[6 + b][64:128, 0:T], ACT.Ln)
                link(A(lnsum[64:128, b, :], banks[6 + b][0:64, T:2 * T], ACT.Ln))
                A(rsum[:, b, :], lnsum[:, b, :], ACT.Exp, scale=-1.0).then_inc(S["rsum_done"], 1)

            def v_out(b):
                act.wait_ge(S["vc_mm"], b + 1)
                A(Vc[:, 2 * b:2 * b + 2, :], bk(b, "B")[:, 0:T].rearrange("p (t c) -> p t c", t=2), ACT.Copy).then_inc(S["vc_done"], 1)

            def exp1(b):
                for t in (2 * b, 2 * b + 1):
                    if t == 2:
                        act.wait_ge(S["pv_done"], M)
                    act.wait_ge(S["nm1_done"], t + 1)
                    A(P1[:, b, t % 2, :], bk(b, "CB"[t % 2]), ACT.Exp, bias=nm1[:, t:t + 1], accum_out=sum1[:, t:t + 1]).then_inc(S["exp1_done"], 1)

            def exp2(b, half):
                for s in (2 * half, 2 * half + 1):
                    t = 4 * b + s
                    act.wait_ge(S["nm2_done"], 2 * b + half + 1)
                    A(P2[:, b, s, :], bk(b, "AC"[s // 2])[:, (s % 2) * T:(s % 2 + 1) * T], ACT.Exp, bias=nm2[:, t:t + 1],
                      accum_out=sum2[:, t:t + 1]).then_inc(S["exp2_done"], 1)

            def pt1_out(t):
                b = t // 2
                act.wait_ge(S["pt1_mm"], t + 1)
                A(PT1[:, b, :, (t % 2) * P:(t % 2 + 1) * P], bk(b, "BA"[t % 2]).rearrange("p (k q) -> p k q", k=4),
                  ACT.Copy).then_inc(S["pt1_done"], 1)

            def gate_exp(b):
                act.wait_ge(S["gate_mm"], b + 1)
                A(eg[:, b * T:(b + 1) * T], bk(b, "C")[:, 0:T], ACT.Exp, scale=-1.0, bias=nbg[:, :]).then_inc(S["eg_done"], 1)

            def gate_tanh(b):
                act.wait_ge(S["gate_mm"], b + 1)
                A(eg[:, b * T:(b + 1) * T], bk(b, "C")[:, 0:T], ACT.Tanh, scale=0.5, bias=hbg[:, :]).then_inc(S["eg_done"], 1)

            def c2s_out(b):
                act.wait_ge(S["c2s_mm"], b + 1)
                A(c2s[:, b * T:(b + 1) * T], bk(b, "B")[:, 0:T], ACT.Identity, bias=smcol("bv_s")).then_inc(S["c2s_done"], 1)

            def route(b):
                act.wait_ge(S["logit_done"], b + 1)
                A(ex[:, 2 * b:2 * b + 2, :], shift[:, 2 * b:2 * b + 2, :], ACT.Exp).then_inc(S["ex_done"], 1)

            def gelus(first, last):
                for n in range(first, last):
                    gelu(n)

            def gelu(n):
                act.wait_ge(S["gates_mm"], n + 1)
                if n >= 4:
                    act.wait_ge(S["act_done"], n - 3)
                A(gl[:, n % 4, :], banks[FBANKS[n % 3]][:, 0:T], ACT.Gelu_apprx_tanh).then_inc(S["gl_done"], 1)

            heads(0, 19)
            sums(0)
            heads(19, 24)
            v_out(0)
            heads(24, 26)
            exp1(0)
            heads(26, 28)
            exp2(0, 0)
            heads(28, 29)
            exp2(0, 1)
            heads(29, 30)
            pt1_out(0)
            heads(30, 31)
            pt1_out(1)
            heads(31, M + 2)
            c2s_out(0)
            sums(1)
            gate_exp(0)
            v_out(1)
            exp1(1)
            exp2(1, 0)
            exp2(1, 1)
            route(0)
            table(gelu_set)
            pt1_out(2)
            gelus(0, 1)
            pt1_out(3)
            gelus(1, 5)
            c2s_out(1)
            gelus(5, 6)
            gate_tanh(1)
            gelus(6, 12)
            table(exp_set)
            route(1)
            table(gelu_set)
            gelus(12, B * E * HT)

        @block.vector
        def _(dve):
            chain = [0]

            def link(ins):
                chain[0] += 1
                ins.then_inc(S["chain_v"], 1)
                dve.wait_ge(S["chain_v"], chain[0])

            V = nc.vector
            V.memset(warm[:, :], 0.0).then_inc(S["warm_ready"], 1)
            V.memset(Q6[:, :, :].bitcast(U32), 0).then_inc(S["zeroed_q"], 1)
            dve.wait_ge(S["in_small"], 16)
            V.tensor_scalar(nbg[:, :], smcol("bg"), -1.0, None, ALU.mult)
            V.tensor_scalar(hbg[:, :], smcol("bg"), 0.5, None, ALU.mult)
            link(V.tensor_scalar(qscale[:, :], smcol("q_norm"), SCALE, None, ALU.mult))
            V.tensor_scalar(rw[:, :], smcol("router_w", E), smcol("router_scale"), XSCALE, ALU.mult, ALU.mult).then_inc(S["rw_done"], 1)
            dve.wait_ge(S["in_cf"], 16)
            for i in range(2):
                dve.wait_ge(S["proj"], 2 + 2 * i)
                v3 = lambda ap: ap.rearrange("p (b t) -> p b t", b=B)
                V.tensor_tensor(v3(rot_s[:, i, :]), v3(banks[2 * i + 1]), sin.broadcast_to([P, B, T]), ALU.mult)
                dve.wait_ge(S["sq_done"], i + 1)
                link(V.tensor_tensor(v3(rot_c[:, i, :]), v3(banks[2 * i]), cos.broadcast_to([P, B, T]), ALU.mult))
                V.tensor_tensor(rot[:, i, :], rot_c[:, i, :], rot_s[:, i, :], ALU.add).then_inc(S["rot_done"], 1)
            for i, w in enumerate((qscale[:, :], smcol("k_norm"))):
                dve.wait_ge(S["rs_done"], i + 1)
                dve.wait_ge(S["rot_done"], i + 1)
                V.scalar_tensor_tensor(out=qkn[:, i, :], in0=rot[:, i, :], scalar=w, in1=rstd[:, i, :],
                                       op0=ALU.mult, op1=ALU.mult).then_inc(S["qkn_done"], 1)
            dve.wait_ge(S["p0"], 1)
            dve.wait_ge(S["qkn_done"], 1)
            V.tensor_tensor(res[:, 0, :], qkn[:, 0, :], piece[:, 0, 0, :], ALU.subtract).then_inc(S["r1d"], 1)
            dve.wait_ge(S["vproj"], 1)
            dve.wait_ge(S["zeroed_v"], 1)
            for half in range(2):
                for t in range(NT):
                    own = VP[:, t, half * (H // 2):(half + 1) * (H // 2), :].rearrange("p h c -> p (h c)")
                    src = banks[4][:, t * P + half * 64:t * P + half * 64 + 64].rearrange("p (h d) -> p h d", d=D)
                    ins = V.tensor_copy(diagonal(own, 64 * half), src)
            ins.then_inc(S["vp_done"], 1)
            dve.wait_ge(S["p1"], 1)
            dve.wait_ge(S["r1d"], 1)
            V.tensor_tensor(piece[:, 0, 2, :], res[:, 0, :], piece[:, 0, 1, :], ALU.subtract).then_inc(S["p2"], 1)
            for b in range(B):
                dve.wait_ge(S["ctx_mm"], 3 + b)
                V.tensor_scalar(QsT[:, b, :], banks[2 + b], smcol("bq_s"), XSCALE, ALU.add, ALU.mult).then_inc(S["ctx_ev"], 1)

            def maxes(m):
                dve.wait_ge(S["s_done"], m + 1)
                V.tensor_reduce(nmax[:, m, 0:1], score_bank(m)[:, 0:P], AX.X, ALU.max, negate=True)
                V.tensor_reduce(nmax[:, m, 1:2], score_bank(m)[:, P:3 * P], AX.X, ALU.max, negate=True).then_inc(S["max_done"], 1)

            def trans_out(m):
                dve.wait_ge(S["t_mm"], m + 1)
                if m >= 4:
                    dve.wait_ge(S["pv_done"], m - 3)
                V.tensor_copy(probsT[:, m % 4, :], trans_bank(m)[:, 0:BLOCKS * P]).then_inc(S["t_done_v"], 1)

            def heads(first, last):
                for m in range(first, last):
                    if m < M:
                        maxes(m)
                    if m >= 2 and (m - 2) % 4 != 3:
                        trans_out(m - 2)

            def attn_norm(b):
                dve.wait_ge(S["rsum_done"], b + 1)
                c = slice(b * T, (b + 1) * T)
                V.tensor_tensor(attnT[0:64, c], banks[6 + b][0:64, 0:T], rsum[0:64, b, :], ALU.mult)
                V.tensor_tensor(attnT[64:128, c], banks[6 + b][64:128, T:2 * T], rsum[64:128, b, :], ALU.mult).then_inc(S["attn_done"], 1)

            def norm_in(i, b, psum, other, mm, count):
                t2 = slice(2 * b, 2 * b + 2)
                dve.wait_ge(S[mm], count)
                link(V.tensor_tensor(pre[:, i, t2, :], psum, other[:, t2, :], ALU.add))
                for t in (2 * b, 2 * b + 1):
                    ins = V.bn_stats(stats[:, i, t, :], pre[:, i, t, :])
                link(ins)
                for t in (2 * b, 2 * b + 1):
                    ins = V.bn_aggr(mv[:, i, t, :], stats[:, i, t, :])
                ins.then_inc(S["mv_done"], 1)

            def norm_out(i, b, dst, done):
                dve.wait_ge(S["rsln_done"], 2 * i + b + 1)
                dve.wait_ge(S["mv_done"], 2 * i + b + 1)
                for t in (2 * b, 2 * b + 1):
                    V.tensor_scalar(dst[:, t, :], pre[:, i, t, :], mv[:, i, t, 0:1], rs_ln[:, i, t:t + 1],
                                    ALU.subtract, ALU.mult).then_inc(S[done], 1)

            def xT_out(i, b):
                dst = (x1T, x2T)[i]
                dve.wait_ge(S[("xt_mm", "x2t_mm")[i]], b + 1)
                V.tensor_copy(dst[:, b * T:(b + 1) * T], bk(b, "A")[:, 0:T]).then_inc(S[("xt_done", "x2t_done")[i]], 1)

            def qk_out(b):
                dve.wait_ge(S["qkc_mm"], b + 1)
                c = slice(b * T, (b + 1) * T)
                V.tensor_scalar(QcT[:, c], bk(b, "A")[:, 0:T], smcol("bq_c"), XSCALE, ALU.add, ALU.mult)
                V.tensor_scalar(KcT[:, c], bk(b, "A")[:, T:2 * T], smcol("bk_c"), None, ALU.add).then_inc(S["qkc_done"], 1)

            def max1(b):
                for t in (2 * b, 2 * b + 1):
                    dve.wait_ge(S["s1_mm"], t + 1)
                    V.tensor_reduce(nm1[:, t:t + 1], bk(b, "CB"[t % 2]), AX.X, ALU.max, negate=True).then_inc(S["nm1_done"], 1)

            def max2(b, s):
                dve.wait_ge(S["s2_mm"], 2 * b + s + 1)
                V.tensor_reduce(nm2[:, 4 * b + 2 * s:4 * b + 2 * s + 2], bk(b, "AC"[s]).rearrange("p (h k) -> p h k", h=2),
                                AX.X, ALU.max, negate=True).then_inc(S["nm2_done"], 1)

            def p1_norm(b):
                for t in (2 * b, 2 * b + 1):
                    dve.wait_ge(S["exp1_done"], t + 1)
                    link(V.reciprocal(r1[:, t:t + 1], sum1[:, t:t + 1]))
                    V.tensor_scalar(P1[:, b, t % 2, :], P1[:, b, t % 2, :], r1[:, t:t + 1], None, ALU.mult).then_inc(S["p1n_done"], 1)

            def pairs(b):
                dve.wait_ge(S["exp2_done"], 4 * (b + 1))
                link(V.reciprocal(r2[:, 4 * b:4 * b + 4], sum2[:, 4 * b:4 * b + 4]))
                for s in range(4):
                    t = 4 * b + s
                    ins = V.tensor_scalar(pair_r[:, t, :], constf("pair"), r2[:, t:t + 1], None, ALU.mult)
                ins.then_inc(S["pair_done"], 1)

            def pt2_out(b):
                dve.wait_ge(S["pt2_mm"], b + 1)
                V.tensor_copy(PT2[:, b, :, :], bk(b, "C").rearrange("p (k q) -> p k q", k=2)).then_inc(S["pt2_done"], 1)

            def s2c_out(b):
                c = slice(b * T, (b + 1) * T)
                dve.wait_ge(S["s2c_mm"], b + 1)
                V.tensor_scalar(s2c[:, c], bk(b, "A")[:, 0:T], smcol("bv_c"), None, ALU.add).then_inc(S["s2c_done"], 1)
                dve.wait_ge(S["s2c_done"], b + 1)
                dve.wait_ge(S["c2s_done"], b + 1)
                link(V.tensor_tensor(diff[:, c], c2s[:, c], s2c[:, c], ALU.subtract))

            def mix_exp(b):
                c = slice(b * T, (b + 1) * T)
                dve.wait_ge(S["eg_done"], b + 1)
                link(V.tensor_scalar(eg1[:, c], eg[:, c], 1.0, None, ALU.add))
                link(V.reciprocal(gate[:, c], eg1[:, c]))
                link(V.tensor_tensor(gd[:, b, :], gate[:, c], diff[:, c], ALU.mult))
                V.tensor_tensor(mixT[:, b, :], gd[:, b, :], s2c[:, c], ALU.add).then_inc(S["mix_done"], 1)

            def mix_tanh(b):
                c = slice(b * T, (b + 1) * T)
                link(V.tensor_scalar(eg1[:, c], diff[:, c], 0.5, None, ALU.mult))
                dve.wait_ge(S["eg_done"], b + 1)
                link(V.scalar_tensor_tensor(out=gd[:, b, :], in0=eg[:, c], scalar=1.0, in1=eg1[:, c], op0=ALU.add, op1=ALU.mult))
                V.tensor_tensor(mixT[:, b, :], gd[:, b, :], s2c[:, c], ALU.add).then_inc(S["mix_done"], 1)

            def logits(b):
                t2 = slice(2 * b, 2 * b + 2)
                dve.wait_ge(S["consts"], 1)
                dve.wait_ge(S["logit_mm"], b + 1)
                dve.wait_ge(S["rr2_done"], b + 1)
                for t in (2 * b, 2 * b + 1):
                    ins = V.tensor_scalar(logit[:, t, :], bk(b, "C")[:, (t % 2) * E:(t % 2 + 1) * E], rr2[:, t:t + 1], None, ALU.mult)
                link(ins)
                link(V.tensor_reduce(nml[:, t2], logit[:, t2, :], AX.X, ALU.max, negate=True))
                for t in (2 * b, 2 * b + 1):
                    ins = V.tensor_scalar(shift[:, t, :], logit[:, t, :], nml[:, t:t + 1], None, ALU.add)
                ins.then_inc(S["logit_done"], 1)
                for t in (2 * b, 2 * b + 1):
                    other = logit[:, t, :].rearrange("p (o e) -> p o e", o=1).broadcast_to([P, E, E])
                    own = logit[:, t, :].rearrange("p (e o) -> p e o", o=1).broadcast_to([P, E, E])
                    V.tensor_tensor(beats[:, t, :, :], other, own, ALU.is_gt)
                    ins = V.tensor_tensor(ties[:, t, :, :], other, own, ALU.is_equal)
                link(ins)
                for t in (2 * b, 2 * b + 1):
                    ins = V.tensor_tensor(ties[:, t, :, :], ties[:, t, :, :], lower[:, :, :], ALU.mult)
                link(ins)
                link(V.tensor_tensor(beats[:, t2, :, :], beats[:, t2, :, :], ties[:, t2, :, :], ALU.add))
                link(V.tensor_reduce(rank[:, t2, :], beats[:, t2, :, :], AX.X, ALU.add))

            def combine(b):
                t2 = slice(2 * b, 2 * b + 2)

                def wide(ap):
                    return ap.rearrange("p (t o) -> p t o", o=1).broadcast_to([P, 2, E])

                dve.wait_ge(S["ex_done"], b + 1)
                link(V.scalar_tensor_tensor(out=gw[:, t2, :], in0=rank[:, t2, :], scalar=1.5, in1=ex[:, t2, :],
                                            op0=ALU.is_lt, op1=ALU.mult))
                link(V.tensor_reduce(ren[:, t2], gw[:, t2, :], AX.X, ALU.add))
                link(V.reciprocal(renr[:, t2], ren[:, t2]))
                link(V.tensor_tensor(cw[:, t2, :], gw[:, t2, :], wide(renr[:, t2]), ALU.mult))
                es = smcol("expert_scale", E).rearrange("p (o e) -> p o e", o=1).broadcast_to([P, 2, E])
                link(V.tensor_tensor(comb[:, t2, :], cw[:, t2, :], es, ALU.mult))
                link(V.tensor_copy(combp[:, t2, 0, :], comb[:, t2, :]))
                link(V.tensor_tensor(combr[:, t2, :], comb[:, t2, :], combp[:, t2, 0, :], ALU.subtract))
                link(V.tensor_copy(combp[:, t2, 1, :], combr[:, t2, :]))
                V.tensor_tensor(combp[:, t2, 2, :], combr[:, t2, :], combp[:, t2, 1, :], ALU.subtract).then_inc(S["comb_done"], 1)

            def combT_out(b):
                dve.wait_ge(S["combT_mm"], b + 1)
                V.tensor_copy(combT[:, b * T:(b + 1) * T], bk(b, "B").bitcast(BF16)[0:PIECES * E, 0:T]).then_inc(S["combT_done"], 1)

            pairview = lambda ap: ap[:, 0:T].rearrange("p (t c) -> p t c", t=2)

            def norm1_in(b):
                dve.wait_ge(S["in_xtok"], 16)
                norm_in(0, b, pairview(bk(b, "A")), x_s, "wout_done", b + 1)

            def norm2_in(b):
                norm_in(1, b, pairview(bk(b, "B")), x1, "mix_mm", b + 1)

            def norm3_in(b):
                norm_in(2, b, pairview(banks[DOWN[b]]), x2, "out_mm", E * HT * (b + 1))

            def scaled(m):
                b, e = m // E, m % E
                dve.wait_ge(S["bc_mm"], m + 1)
                dve.wait_ge(S["x2t_done"], b + 1)
                V.tensor_tensor(x2c[:, b, e, :], x2T[:, b * T:(b + 1) * T], banks[SPREAD][:, 0:T], ALU.mult).then_inc(S["x2c_done"], 1)

            def acts_of(n):
                dve.wait_ge(S["gl_done"], n + 1)
                if n >= 4:
                    dve.wait_ge(S["out_mm"], n - 3)
                V.tensor_tensor(acts[:, n % 4, :], banks[FBANKS[n % 3]][:, T:2 * T], gl[:, n % 4, :], ALU.mult).then_inc(S["act_done"], 1)

            def x1_out(b):
                norm_out(0, b, x1, "xn_done")

            def x2_out(b):
                norm_out(1, b, x2, "x2n_done")

            def ffn(first, last):
                for n in range(first, last):
                    if n % HT == 1 and n // HT + 1 != E and n // HT + 1 < B * E:
                        scaled(n // HT + 1)
                    acts_of(n)

            def y_out(b):
                norm_out(2, b, y_s, "y_ready")

            heads(0, 19)
            attn_norm(0)
            heads(19, 21)
            norm1_in(0)
            heads(21, 22)
            x1_out(0)
            heads(22, 23)
            xT_out(0, 0)
            heads(23, 24)
            qk_out(0)
            heads(24, 26)
            max1(0)
            heads(26, 27)
            p1_norm(0)
            max2(0, 0)
            heads(27, 29)
            max2(0, 1)
            heads(29, 30)
            pairs(0)
            heads(30, 32)
            pt2_out(0)
            heads(32, M + 2)
            s2c_out(0)
            attn_norm(1)
            norm1_in(1)
            mix_exp(0)
            x1_out(1)
            norm2_in(0)
            xT_out(0, 1)
            x2_out(0)
            qk_out(1)
            max1(1)
            xT_out(1, 0)
            max2(1, 0)
            logits(0)
            p1_norm(1)
            max2(1, 1)
            combine(0)
            pairs(1)
            combT_out(0)
            scaled(0)
            ffn(0, 3)
            pt2_out(1)
            ffn(3, 5)
            s2c_out(1)
            ffn(5, 6)
            mix_tanh(1)
            ffn(6, 8)
            norm2_in(1)
            ffn(8, 9)
            x2_out(1)
            ffn(9, 10)
            xT_out(1, 1)
            ffn(10, 11)
            logits(1)
            ffn(11, 13)
            combine(1)
            ffn(13, 14)
            combT_out(1)
            ffn(14, 15)
            scaled(E)
            ffn(15, E * HT + 4)
            norm3_in(0)
            y_out(0)
            ffn(E * HT + 4, B * E * HT)
            norm3_in(1)
            y_out(1)

        @block.tensor
        def _(pe):
            def mm(out, lhsT, rhs, start=True, stop=True, **kw):
                return nc.tensor.matmul(out, lhsT, rhs, start=start, stop=stop, **kw)

            pe.wait_ge(S["warm_ready"], 1)
            for _ in range(8):
                mm(banks[7], warm[:, 0:P], warm[:, :])
            pe.wait_ge(S["in_x"], 16)
            pe.wait_ge(S["in_wqkv"], 16)
            for i in range(4):
                mm(banks[i], wqkv_s[:, i, :], xT_s[:, :]).then_inc(S["proj"], 1)
            for t in range(NT):
                ins = mm(banks[4][:, t * P:(t + 1) * P], xT_s[:, t * P:(t + 1) * P], wqkv_s[:, 4, :])
            ins.then_inc(S["vproj"], 1)
            pe.wait_ge(S["in_cf"], 16)
            for i in range(2):
                pe.wait_ge(S["sq_done"], i + 1)
                mm(banks[5 + i], constf("mean8"), sq[:, i, :]).then_inc(S["ms_done"], 1)
            pe.wait_ge(S["in_ctx"], 16)
            pe.wait_ge(S["in_wx"], 16)
            pe.wait_ge(S["rot_done"], 2)
            for j, w in enumerate(("Wk_s", "Wq_s")):
                for b in range(B):
                    mm(banks[2 * j + b], wx(w), ctxT_s[:, b * L:(b + 1) * L]).then_inc(S["ctx_mm"], 1)
            pe.wait_ge(S["vp_done"], 1)
            pe.wait_ge(S["rs_done"], 1)
            for b in range(B):
                for t in range(4):
                    k = 4 * b + t
                    ins = mm(banks[4 + b][:, t * P:(t + 1) * P], ctxT_s[:, k * P:(k + 1) * P], wx("Wv_s"))
                ins.then_inc(S["ctx_mm"], 1)

            for _ in range(36):
                mm(banks[7], warm[:, 0:P], warm[:, :])
            mask = constb("mask").rearrange("p (o k) -> p o k", o=1).broadcast_to([P, 2, P])
            pe.wait_ge(S["in_cb"], 16)
            pe.wait_ge(S["q6_in"], 6 * 16)
            pe.wait_ge(S["k6_in"], 2 * 16)
            pe.wait_ge(S["ctx_ev"], 6)

            def scores(m):
                b, h = m // H, m % H
                if m >= H:
                    pe.wait_ge(S["exp_done"], m - 1)
                elif m >= 4:
                    pe.wait_ge(S["exp_done"], m - 3)
                o = score_bank(m)
                q0 = b * T
                diag = o[:, 0:4 * P].rearrange("p (n k) -> p n k", n=2)[:, :, 0:P]
                mm(diag, identb, mask, stop=False, skip_group_check=True)
                mm(o[:, P:3 * P], Q6[:, h, q0 + P:q0 + T], K6[:, h // 2, q0:q0 + T], start=False, stop=False, skip_group_check=True)
                mm(o[:, 0:P], Q6[:, h, q0:q0 + P], K6[:, h // 2, q0:q0 + P], start=False,
                   skip_group_check=True).then_inc(S["s_done"], 1)

            def transposes(m):
                pe.wait_ge(S["exp_done"], m + 1)
                if m >= 2:
                    pe.wait_ge(*transposed(m - 2))
                for i in range(BLOCKS):
                    ins = nc.tensor.transpose(trans_bank(m)[:, i * P:(i + 1) * P], probs[:, m % 4, i * P:(i + 1) * P], ident)
                ins.then_inc(S["t_mm"], 1)

            def values(m):
                b, h = m // H, m % H
                pe.wait_ge(*transposed(m))
                acc = banks[6 + b][:, (h // 8) * T:(h // 8 + 1) * T]
                mm(acc, VP[:, 2 * b, h, :], probsT[:, m % 4, 0:T], start=(h % 8 == 0), stop=False, skip_group_check=True)
                mm(acc[:, P:T], VP[:, 2 * b + 1, h, :], probsT[:, m % 4, T:T + P], start=False, stop=(h % 8 == 7),
                   skip_group_check=True).then_inc(S["pv_done"], 1)

            def heads(first, last):
                for m in range(first, last):
                    if m < M:
                        scores(m)
                    if 2 <= m < M + 2:
                        transposes(m - 2)
                    if m >= 3:
                        values(m - 3)

            def attn_out(b):
                pe.wait_ge(S["in_wout"], 16)
                pe.wait_ge(S["attn_done"], b + 1)
                for t in (2 * b, 2 * b + 1):
                    ins = mm(bk(b, "A")[:, (t % 2) * P:(t % 2 + 1) * P], attnT[:, t * P:(t + 1) * P], wout_s[:, :])
                ins.then_inc(S["wout_done"], 1)

            def x_t(i, b):
                src = (x1, x2)[i]
                pe.wait_ge(S[("xn_done", "x2n_done")[i]], 2 * (b + 1))
                for t in (2 * b, 2 * b + 1):
                    ins = nc.tensor.transpose(bk(b, "A")[:, (t % 2) * P:(t % 2 + 1) * P], src[:, t, :], ident)
                ins.then_inc(S[("xt_mm", "x2t_mm")[i]], 1)

            def qk_char(b):
                c = slice(b * T, (b + 1) * T)
                pe.wait_ge(S["xt_done"], b + 1)
                mm(bk(b, "A")[:, 0:T], wx("Wq_c"), x1T[:, c])
                mm(bk(b, "A")[:, T:2 * T], wx("Wk_c"), x1T[:, c]).then_inc(S["qkc_mm"], 1)

            def v_char(b):
                for t in (2 * b, 2 * b + 1):
                    ins = mm(bk(b, "B")[:, (t % 2) * P:(t % 2 + 1) * P], x1T[:, t * P:(t + 1) * P], wx("Wv_c"))
                ins.then_inc(S["vc_mm"], 1)

            def s1(b):
                pe.wait_ge(S["qkc_done"], b + 1)
                for t in (2 * b, 2 * b + 1):
                    if t % 2:
                        pe.wait_ge(S["vc_done"], b + 1)
                    mm(bk(b, "CB"[t % 2]), QcT[:, t * P:(t + 1) * P], KsT[:, b, :]).then_inc(S["s1_mm"], 1)

            def s2(b, half):
                if half:
                    pe.wait_ge(S["exp1_done"], 2 * b + 1)
                for s in (2 * half, 2 * half + 1):
                    ins = mm(bk(b, "AC"[half])[:, (s % 2) * T:(s % 2 + 1) * T], QsT[:, b, s * P:(s + 1) * P], KcT[:, b * T:(b + 1) * T])
                ins.then_inc(S["s2_mm"], 1)

            def pt1(b, q):
                t = 2 * b + q
                pe.wait_ge(S["p1n_done"], t + 1)
                pe.wait_ge(*((S["exp1_done"], 2 * b + 2) if q == 0 else (S["exp2_done"], 4 * b + 2)))
                for k in range(4):
                    ins = nc.tensor.transpose(bk(b, "BA"[q])[:, k * P:(k + 1) * P], P1[:, b, q, k * P:(k + 1) * P], ident)
                ins.then_inc(S["pt1_mm"], 1)

            def pt2(b):
                pe.wait_ge(S["pair_done"], b + 1)
                for k in range(2):
                    for s in range(4):
                        o = k * T + s * 64
                        ins = mm(bk(b, "C")[:, o:o + 64], P2[:, b, s, k * P:(k + 1) * P], pair_r[:, 4 * b + s, :])
                ins.then_inc(S["pt2_mm"], 1)

            def c2s_mm(b):
                pe.wait_ge(S["pt1_done"], 2 * (b + 1))
                for k in range(4):
                    ins = mm(bk(b, "B")[:, 0:T], Vs[:, 4 * b + k, :], PT1[:, b, k, :], start=(k == 0), stop=(k == 3))
                ins.then_inc(S["c2s_mm"], 1)

            def s2c_mm(b):
                pe.wait_ge(S["pt1_done"], 2 * (b + 1))
                pe.wait_ge(S["pt2_done"], b + 1)
                for k in range(2):
                    ins = mm(bk(b, "A")[:, 0:T], Vc[:, 2 * b + k, :], PT2[:, b, k, :], start=(k == 0), stop=(k == 1))
                ins.then_inc(S["s2c_mm"], 1)

            def gate_mm(b):
                c = slice(b * T, (b + 1) * T)
                pe.wait_ge(S["c2s_done"], b + 1)
                mm(bk(b, "C")[:, 0:T], wx("Wg_c"), c2s[:, c], stop=False)
                pe.wait_ge(S["s2c_done"], b + 1)
                mm(bk(b, "C")[:, 0:T], wx("Wg_s"), s2c[:, c], start=False).then_inc(S["gate_mm"], 1)

            def mix_t(b):
                pe.wait_ge(S["mix_done"], b + 1)
                for t in range(2):
                    ins = nc.tensor.transpose(bk(b, "B")[:, t * P:(t + 1) * P], mixT[:, b, t * P:(t + 1) * P], ident)
                ins.then_inc(S["mix_mm"], 1)

            def logit_mm(b):
                pe.wait_ge(S["rw_done"], 1)
                pe.wait_ge(S["x2t_done"], b + 1)
                for t in (2 * b, 2 * b + 1):
                    ins = mm(bk(b, "C")[:, (t % 2) * E:(t % 2 + 1) * E], x2T[:, t * P:(t + 1) * P], rw[:, :])
                ins.then_inc(S["logit_mm"], 1)

            def comb_t(b):
                pe.wait_ge(S["comb_done"], b + 1)
                for t in (2 * b, 2 * b + 1):
                    ins = nc.tensor.transpose(bk(b, "B").bitcast(BF16)[0:PIECES * E, (t % 2) * P:(t % 2 + 1) * P],
                                              combp[:, t, :, :].rearrange("p n e -> p (n e)"), identb)
                ins.then_inc(S["combT_mm"], 1)

            def spread(m):
                b, e = m // E, m % E
                pe.wait_ge(S["combT_done"], b + 1)
                if m >= 1:
                    pe.wait_ge(S["x2c_done"], m)
                mm(banks[SPREAD][:, 0:T], sel_expert[:, e, :], combT[:, b * T:(b + 1) * T]).then_inc(S["bc_mm"], 1)

            def gates(n):
                b, e, ht = n // (E * HT), n // HT % E, n % HT
                if n == 0:
                    pe.wait_ge(S["t_done_v"], M - M // 4)
                    pe.wait_ge(S["t_done_a"], M // 4)
                    pe.wait_ge(S["in_gat"], 32)
                pe.wait_ge(S["x2t_done"], b + 1)
                if n >= 3:
                    pe.wait_ge(S["act_done"], n - 2)
                mm(banks[FBANKS[n % 3]][:, 0:T], gat_s[:, e, 0, ht, :], x2T[:, b * T:(b + 1) * T])
                pe.wait_ge(S["x2c_done"], b * E + e + 1)
                mm(banks[FBANKS[n % 3]][:, T:2 * T], gat_s[:, e, 1, ht, :], x2c[:, b, e, :]).then_inc(S["gates_mm"], 1)

            def down(n):
                b, e, ht = n // (E * HT), n // HT % E, n % HT
                i = n % (E * HT)
                if n == 0:
                    pe.wait_ge(S["in_lin"], 16)
                pe.wait_ge(S["act_done"], n + 1)
                for t in range(2):
                    ins = mm(banks[DOWN[b]][:, t * P:(t + 1) * P], acts[:, n % 4, t * P:(t + 1) * P], lin_s[:, e, ht, :],
                             start=(i == 0 and t == 0), stop=(i == E * HT - 1), skip_group_check=True)
                ins.then_inc(S["out_mm"], 1)

            def ffn(first, last):
                for n in range(first, last):
                    gates(n)
                    if n % HT == 1 and n // HT + 1 != E and n // HT + 1 < B * E:
                        spread(n // HT + 1)
                    if n >= 1:
                        down(n - 1)

            heads(0, 20)
            attn_out(0)
            heads(20, 22)
            x_t(0, 0)
            heads(22, 23)
            qk_char(0)
            v_char(0)
            heads(23, 24)
            s1(0)
            heads(24, 26)
            s2(0, 0)
            heads(26, 27)
            pt1(0, 0)
            s2(0, 1)
            heads(27, 29)
            pt1(0, 1)
            heads(29, 30)
            pt2(0)
            heads(30, 32)
            c2s_mm(0)
            heads(32, 33)
            s2c_mm(0)
            heads(33, M + 3)
            attn_out(1)
            gate_mm(0)
            x_t(0, 1)
            mix_t(0)
            qk_char(1)
            v_char(1)
            x_t(1, 0)
            s1(1)
            s2(1, 0)
            logit_mm(0)
            s2(1, 1)
            pt1(1, 0)
            comb_t(0)
            spread(0)
            ffn(0, 1)
            pt1(1, 1)
            ffn(1, 3)
            pt2(1)
            ffn(3, 5)
            c2s_mm(1)
            s2c_mm(1)
            ffn(5, 6)
            gate_mm(1)
            ffn(6, 8)
            mix_t(1)
            ffn(8, 10)
            x_t(1, 1)
            ffn(10, 11)
            logit_mm(1)
            ffn(11, 14)
            comb_t(1)
            ffn(14, 15)
            spread(E)
            ffn(15, B * E * HT)
            down(B * E * HT - 1)


def _constants():
    import numpy as np

    def bf16_bits(a):
        return (np.ascontiguousarray(a, np.float32).view(np.uint32) >> 16).astype(np.uint16)

    ident = np.eye(P, dtype=np.float32)
    half = D // 2
    inv_freq = (1.0 / np.float32(10000.0) ** (np.arange(half, dtype=np.float32) * np.float32(2.0) / np.float32(D))).astype(np.float32)
    ang = (np.arange(T, dtype=np.float32)[:, None] * inv_freq[None, :]).astype(np.float32)
    c, s = np.cos(ang).T, np.sin(ang).T
    cos = np.tile(np.concatenate([c, c]), (H, 1))
    sin = np.tile(np.concatenate([-s, s]), (H, 1))
    mean8 = np.kron(np.eye(H), np.full((D, D), 1.0 / D))
    pair = np.kron(np.eye(P // 2), np.full((2, 1), 0.5))
    const_f = np.concatenate([ident, cos, sin, mean8, pair], 1).astype(np.float32)
    i = np.arange(P)
    lowest = (np.float32(LOWEST).view(np.uint32) & np.uint32(0xFFFF0000)).view(np.float32)
    mask = np.where(i[:, None] < i[None, :], lowest, np.float32(0))
    sel_expert = np.zeros((P, E, P), np.float32)
    for n in range(PIECES):
        sel_expert[n * E + np.arange(E), np.arange(E)] = 1.0
    const_b = bf16_bits(np.concatenate([ident, mask, sel_expert.reshape(P, -1)], 1))
    return np.ascontiguousarray(const_f), const_b


def kernel(**inputs):
    import numpy as np
    import concourse.bacc as bacc
    from concourse import mybir as mb
    from concourse.bass_utils import run_bass_kernel_spmd as run

    a = {k: np.asarray(v) for k, v in inputs.items()}
    tok = a["x"].reshape(N, C)
    w = a["L0_attn_w_qkv"].reshape(3, H, D, C)
    swapped = np.concatenate([w[:, :, D // 2:], w[:, :, :D // 2]], 2)

    def cols(m):
        return m.reshape(P, C).T

    wx = {n: a["L0_xattn_" + n].T for n in WX if not n.startswith("Wg")}
    wx["Wg_c"], wx["Wg_s"] = a["L0_xattn_Wg"][:, :C].T, a["L0_xattn_Wg"][:, C:].T
    small = [a["L0_xattn_" + n][:, None] for n in ("bq_c", "bk_s", "bv_s", "bq_s", "bk_c", "bv_c", "bg")]
    small += [np.tile(a["L0_attn_q_norm_w"], H)[:, None], np.tile(a["L0_attn_k_norm_w"], H)[:, None]]
    small += [a["L0_ffn_router_scale"][:, None], a["L0_ffn_router_w"]]
    small += [np.broadcast_to(a["L0_ffn_per_expert_scale"], (P, E))]
    const_f, const_b = _constants()
    arrays = {
        "xT": tok.T,
        "x_tok": tok.reshape(NT, P, C).transpose(1, 0, 2),
        "ctxT": a["ctx_1024"].reshape(B * L, C).T,
        "w_qkv": np.stack([cols(w[0]), cols(swapped[0]), cols(w[1]), cols(swapped[1]), cols(w[2])], 1),
        "w_out": a["L0_attn_w_out"].T,
        "w_x": np.stack([wx[n] for n in WX], 1),
        "small": np.concatenate(small, 1),
        "gating": a["L0_ffn_gating_w"].reshape(E, 2, HT, P, C).transpose(4, 0, 1, 2, 3),
        "linear": a["L0_ffn_linear_w"].reshape(E, HT, P, C).transpose(2, 0, 1, 3),
        "const_f": const_f,
        "const_b": const_b,
    }
    arrays = {k: np.ascontiguousarray(v) for k, v in arrays.items()}
    nc = bacc.Bacc("TRN2", target_bir_lowering=False, num_devices=1)
    args = [nc.dram_tensor(k, v.shape, mb.dt.from_np(v.dtype), kind="ExternalInput").ap() for k, v in arrays.items()]
    out = nc.dram_tensor("out", (P, NT, C), mb.dt.float32, kind="ExternalOutput").ap()
    post_norm_decoder(nc, *args, out)
    r = run(nc, [arrays], core_ids=[0])
    y = r.results[0]["out"]
    return np.ascontiguousarray(y.transpose(1, 0, 2)).reshape(B, T, C)
```

```python
from contextlib import ExitStack

import concourse.bass as bass
from concourse import mybir

F32 = mybir.dt.float32
BF16 = mybir.dt.bfloat16
U16 = mybir.dt.uint16
U32 = mybir.dt.uint32
ALU = mybir.AluOpType
ACT = mybir.ActivationFunctionType
AX = mybir.AxisListType

P = 128
B, T, C = 2, 256, 128
H, D = 16, 8
L = 512
E, HID = 8, 256
N = B * T
NT = N // P
HT = HID // P
M = B * H
BLOCKS = 3
PIECES = 3
LOWEST = -1e30
Q_PIECE = (0, 1, 2, 0, 1, 0)
K_PIECE = (0, 0, 0, 1, 1, 2)

CF = {"ident": (0, 128), "cos": (128, 384), "sin": (384, 640), "mean8": (640, 768), "pair": (768, 832)}
CB = {"ident": (0, 128), "mask": (128, 256), "sel_expert": (256, 256 + E * P),
      "sel_rows": (256 + E * P, 256 + E * P + 12 * P)}
CBW = 256 + E * P + 12 * P
WX = ["Wq_c", "Wk_s", "Wv_s", "Wq_s", "Wk_c", "Wv_c", "Wg_c", "Wg_s"]
SM = {"bq_c": 0, "bk_s": 1, "bv_s": 2, "bq_s": 3, "bk_c": 4, "bv_c": 5, "bg": 6, "q_norm": 7, "k_norm": 8,
      "router_scale": 9, "router_w": 10, "expert_scale": 18}
SMW = 26


def post_norm_decoder(nc, xT, x_tok, ctxT, w_qkv, w_out, w_x, small, gating, linear, const_f, const_b, out):
    ctx = ExitStack()

    def sb(name, shape, dt=F32):
        return ctx.enter_context(nc.sbuf_tensor(name, shape, dt))

    def sem(name):
        return ctx.enter_context(nc.semaphore(name))

    with ctx:
        xT_s = sb("xT_s", [P, N])
        x_s = sb("x_s", [P, NT, C])
        ctxT_s = sb("ctxT_s", [P, B * L])
        wqkv_s = sb("wqkv_s", [P, 5, P])
        wout_s = sb("wout_s", [P, P])
        wx_s = sb("wx_s", [P, 8, P])
        sm_s = sb("sm_s", [P, SMW])
        gat_s = sb("gat_s", [P, E, 2, HT, P])
        lin_s = sb("lin_s", [P, E, HT, P])
        cf = sb("cf", [P, 832])
        cb = sb("cb", [P, CBW], BF16)
        eps_rms = sb("eps_rms", [P, 1])
        eps_ln = sb("eps_ln", [P, 1])
        warm = sb("warm", [P, 512], BF16)

        def constf(name):
            return cf[:, CF[name][0]:CF[name][1]]

        def constb(name, rows=P):
            return cb[0:rows, CB[name][0]:CB[name][1]]

        def wx(name):
            return wx_s[:, WX.index(name), :]

        def smcol(name, n=1):
            return sm_s[:, SM[name]:SM[name] + n]

        def diagonal(flat, at):
            return bass.AP(flat.tensor, flat.offset + at, [list(flat.ap[0]), [P + D, H // 2], [1, D]])

        ident = constf("ident")
        identb = constb("ident")
        sel_expert = constb("sel_expert", PIECES * E).rearrange("r (e m) -> r e m", e=E)
        sel_rows = constb("sel_rows").rearrange("r (o i n m) -> r o i n m", o=2, i=2, n=PIECES)
        cos = constf("cos").rearrange("p (o t) -> p o t", o=1)
        sin = constf("sin").rearrange("p (o t) -> p o t", o=1)

        arena = sb("arena", [P, 7 * 2 * N])
        at = [0]

        def later(n):
            at[0] += n
            assert at[0] <= 7 * 2 * N
            return arena[:, at[0] - n:at[0]]


        def early(i):
            return arena[:, i * 2 * N:(i + 1) * 2 * N].rearrange("p (i n) -> p i n", i=2)

        sq, lnms, rstd, rot_c, rot_s, rot, qkn = (early(i) for i in range(7))
        res = sb("res", [P, 2, N])
        piece = sb("piece", [P, 2, PIECES, N], BF16)
        Q6 = sb("Q6", [P, H, N], BF16)
        K6 = sb("K6", [P, H // 2, N], BF16)
        VP = sb("VP", [P, NT, H, P])
        nmax = sb("nmax", [P, M, 2])
        probs = sb("probs", [P, 4, BLOCKS * P])
        probsT = sb("probsT", [P, 4, BLOCKS * P])
        lnsum = sb("lnsum", [P, B, T])
        rsum = sb("rsum", [P, B, T])
        attnT = sb("attnT", [P, N])
        qscale = sb("qscale", [P, 1])

        pre = sb("pre", [P, 3, NT, C])
        stats = sb("stats", [P, 3, NT, 6])
        mv = sb("mv", [P, 3, NT, 2])
        rs_ln = sb("rs_ln", [P, 3, NT])
        x1 = sb("x1", [P, NT, C])
        x1T = sb("x1T", [P, N])
        x2 = sb("x2", [P, NT, C])
        x2T = sb("x2T", [P, N])
        y_s = sb("y_s", [P, NT, C])

        KsT = sb("KsT", [P, B, L])
        QsT = sb("QsT", [P, B, L])
        Vs = sb("Vs", [P, B * L // P, C])
        QcT = sb("QcT", [P, N])
        KcT = sb("KcT", [P, N])
        Vc = sb("Vc", [P, NT, C])
        nm1 = sb("nm1", [P, NT])
        sum1 = sb("sum1", [P, NT])
        r1 = sb("r1", [P, NT])
        after = VP[:, :, :, :].rearrange("p (b t) h c -> p b (t h c)", b=B)
        P1 = after[:, :, 0:2 * L].rearrange("p b (t k) -> p b t k", t=2)
        P2 = after[:, :, 2 * L:4 * L].rearrange("p b (t k) -> p b t k", t=4)
        gd = after[:, :, 4 * L:4 * L + T]
        mixT = after[:, :, 4 * L + T:4 * L + 2 * T]
        PT1 = later(2048).rearrange("p (b k q) -> p b k q", b=B, k=4)
        nm2 = sb("nm2", [P, 8])
        sum2 = sb("sum2", [P, 8])
        r2 = sb("r2", [P, 8])
        pair_r = sb("pair_r", [P, 8, 64])
        PT2 = later(1024).rearrange("p (b k q) -> p b k q", b=B, k=2)
        c2s = later(N)
        s2c = later(N)
        diff = res[:, 0, :]
        nbg = sb("nbg", [P, 1])
        hbg = sb("hbg", [P, 1])
        eg = res[:, 1, :]
        eg1 = later(N)
        gate = later(N)

        rw = sb("rw", [P, E])
        nhalf = sb("nhalf", [P, 2])
        sd2 = sb("sd2", [P, NT])
        ms2 = sb("ms2", [P, NT])
        rr2 = sb("rr2", [P, NT])
        logit = sb("logit", [P, NT, E])
        nml = sb("nml", [P, NT])
        shift = sb("shift", [P, NT, E])
        ex = sb("ex", [P, NT, E])
        beats = sb("beats", [P, NT, E, E])
        ties = sb("ties", [P, NT, E, E])
        rank = sb("rank", [P, NT, E])
        lower = sb("lower", [P, E, E])
        gw = sb("gw", [P, NT, E])
        ren = sb("ren", [P, NT])
        renr = sb("renr", [P, NT])
        cw = sb("cw", [P, NT, E])
        comb = sb("comb", [P, NT, E])
        combr = sb("combr", [P, NT, E])
        combp = sb("combp", [P, NT, PIECES, E], BF16)
        combT = sb("combT", [PIECES * E, N], BF16)
        x2c = Q6[:, :, :].rearrange("p h n -> p (h n)").bitcast(F32).rearrange("p (b e n) -> p b e n", b=B, e=E)
        gl = later(1024).rearrange("p (i n) -> p i n", i=4)
        acts = later(1024).rearrange("p (i n) -> p i n", i=4)

        psum = ctx.enter_context(nc.psum_tensor("psum", [P, 8, 512], F32))
        banks = [psum[:, i, :] for i in range(8)]
        XBANKS = ((6, 0, 1), (7, 2, 3))
        FBANKS = (4, 5, 0)
        SPREAD, DOWN = 6, (1, 2)

        def bk(b, i):
            return banks[XBANKS[b]["ABC".index(i)]]

        def score_bank(m):
            return banks[m % 3 if m < H else 2 + m % 2]

        def trans_bank(m):
            return banks[4 + m % 2]

        qs = nc.dram_tensor("q_pieces", [H, PIECES, D, T], BF16).ap()
        ks = nc.dram_tensor("k_rows", [H, len(K_PIECE), D, T], BF16).ap()

        names = """in_x in_wqkv in_small in_cf in_cb in_ctx in_wx in_xtok in_wout in_gat in_lin
            zeroed_q zeroed_k zeroed_v consts eps
            proj vproj sq_done ms_done rs_done rot_done qkn_done p0 p1 p2 r1d r2d q_saved k_saved q6_in k6_in rows_mm q_rows k_rows vp_done
            ctx_mm ctx_ev s_done max_done exp_done t_mm t_done_v t_done_a pv_done rsum_done attn_done
            wout_done pre_done xn_done x2n_done xt_mm xt_done x2t_mm x2t_done
            qkc_mm qkc_done vc_mm vc_done s1_mm nm1_done exp1_done p1n_done pt1_mm pt1_done
            s2_mm nm2_done exp2_done pair_done pt2_mm pt2_done c2s_mm s2c_mm c2s_done s2c_done gate_mm eg_done gate_read mix_done
            mix_mm rw_done rr2_done logit_mm logit_done ex_done comb_done combT_mm combT_done bc_mm x2c_done warm_ready
            gates_mm gl_done act_done out_mm y_ready stored chain_v chain_a chain_p""".split()
        S = {n: sem(n) for n in names}
        mv_done = [sem("mv_done%d" % i) for i in range(3)]
        rsln_done = [sem("rsln_done%d" % i) for i in range(3)]
        SCALE = float(D) ** -0.5
        XSCALE = float(C) ** -0.5

        def transposed(m):
            return (S["t_done_a"], m // 4 + 1) if m % 4 == 3 else (S["t_done_v"], m - m // 4 + 1)

        block = ctx.enter_context(nc.Block())

        @block.sync
        def _(sp):
            sp.dma_start(xT_s[:, :], xT).then_inc(S["in_x"], 16)
            sp.dma_start(cf[:, :], const_f).then_inc(S["in_cf"], 16)
            sp.dma_start(ctxT_s[:, :], ctxT).then_inc(S["in_ctx"], 16)
            sp.dma_start(cb[:, :].bitcast(U16), const_b).then_inc(S["in_cb"], 16)
            late = slice(T, 2 * T)
            for n, (ready, count) in enumerate((("p0", 2), ("p1", 2), ("p2", 2))):
                sp.wait_ge(S[ready], count)
                sp.dma_start(qs[:, n], piece[:, 0, n, late]).then_inc(S["q_saved"], 16)
                for row, p in enumerate(K_PIECE):
                    if p == n:
                        sp.dma_start(ks[:, row], piece[:, 1, n, late]).then_inc(S["k_saved"], 16)
            sp.wait_ge(S["q_saved"], 3 * 16)
            sp.wait_ge(S["zeroed_q"], 1)
            q_rows = [(0, 3), (3, 2), (5, 1)]
            for odd in range(2):
                src = qs.rearrange("(p o) n d t -> o (n d) p t", o=2)[odd]
                for at, n in q_rows:
                    r0 = 64 * odd + at * D
                    sp.dma_start(Q6[r0:r0 + n * D, odd:H:2, late], src[0:n * D]).then_inc(S["q6_in"], 16)
            sp.wait_ge(S["k_saved"], 16 * len(K_PIECE))
            sp.wait_ge(S["zeroed_k"], 1)
            for odd in range(2):
                src = ks.rearrange("(p o) n d t -> o (n d) p t", o=2)[odd]
                sp.dma_start(K6[64 * odd:64 * odd + len(K_PIECE) * D, :, late], src).then_inc(S["k6_in"], 16)
            sp.dma_start(x_s[:, :, :], x_tok).then_inc(S["in_xtok"], 16)
            sp.dma_start(wout_s[:, :], w_out).then_inc(S["in_wout"], 16)
            sp.dma_start(gat_s[:, 0:4], gating[:, 0:4]).then_inc(S["in_gat"], 16)
            sp.dma_start(gat_s[:, 4:8], gating[:, 4:8]).then_inc(S["in_gat"], 16)
            sp.dma_start(lin_s[:, :, :, :], linear).then_inc(S["in_lin"], 16)
            for b in range(B):
                sp.wait_ge(S["y_ready"], 2 * (b + 1))
                sp.dma_start(out[:, 2 * b:2 * b + 2, :], y_s[:, 2 * b:2 * b + 2, :]).then_inc(S["stored"], 16)
            sp.wait_ge(S["stored"], 16 * B)

        @block.gpsimd
        def _(pool):
            chain = [0]

            def link(ins):
                chain[0] += 1
                ins.then_inc(S["chain_p"], 1)
                pool.wait_ge(S["chain_p"], chain[0])

            nc.gpsimd.memset(eps_rms[:, :], 1e-6)
            nc.gpsimd.memset(nhalf[:, :], -0.5)
            nc.gpsimd.memset(eps_ln[:, :], 1e-5).then_inc(S["eps"], 1)
            nc.gpsimd.memset(K6[:, :, :].bitcast(U32), 0).then_inc(S["zeroed_k"], 1)
            nc.gpsimd.memset(VP[:, 0:2, :, :], 0.0)
            link(nc.gpsimd.memset(VP[:, 2:4, :, :], 0.0))
            for half in range(2):
                for t in range(NT):
                    ones = VP[:, t, half * (H // 2):(half + 1) * (H // 2), :].rearrange("p h c -> p (h c)")
                    last = nc.gpsimd.memset(diagonal(ones, 64 * (1 - half)), 1.0)
            last.then_inc(S["zeroed_v"], 1)
            link(nc.gpsimd.memset(lower[:, :, :], 0.0))
            nc.gpsimd.affine_select(out=lower[:, :, :], in_=lower[:, :, :], compare_op=ALU.is_ge, fill=1.0, base=0,
                                    pattern=[[-1, E], [1, E]], channel_multiplier=0).then_inc(S["consts"], 1)
            pool.wait_ge(S["p0"], 2)
            nc.gpsimd.tensor_tensor(res[:, 1, :], qkn[:, 1, :], piece[:, 1, 0, :], ALU.subtract).then_inc(S["r2d"], 1)
            pool.wait_ge(S["p1"], 2)
            pool.wait_ge(S["r2d"], 1)
            nc.gpsimd.tensor_tensor(piece[:, 1, 2, :], res[:, 1, :], piece[:, 1, 1, :], ALU.subtract).then_inc(S["p2"], 1)

            def rs_norm(i, b):
                t2 = slice(2 * b, 2 * b + 2)
                pool.wait_ge(mv_done[i], b + 1)
                link(nc.gpsimd.tensor_scalar(sd2[:, t2], mv[:, i, t2, 1], 1e-5, None, ALU.add))
                nc.gpsimd.tensor_tensor(rs_ln[:, i, t2], sd2[:, t2], nhalf[:, :], ALU.pow).then_inc(rsln_done[i], 1)

            def rms2(b):
                t2 = slice(2 * b, 2 * b + 2)
                pool.wait_ge(rsln_done[1], b + 1)
                link(nc.gpsimd.tensor_tensor(sd2[:, t2], mv[:, 1, t2, 1], rs_ln[:, 1, t2], ALU.mult))
                link(nc.gpsimd.tensor_tensor(ms2[:, t2], sd2[:, t2], rs_ln[:, 1, t2], ALU.mult))
                link(nc.gpsimd.tensor_scalar(ms2[:, t2], ms2[:, t2], 1e-6, None, ALU.add))
                nc.gpsimd.tensor_tensor(rr2[:, t2], ms2[:, t2], nhalf[:, :], ALU.pow).then_inc(S["rr2_done"], 1)

            rs_norm(0, 0)
            rs_norm(0, 1)
            rs_norm(1, 0)
            rms2(0)
            rs_norm(1, 1)
            rms2(1)
            rs_norm(2, 0)
            rs_norm(2, 1)

        @block.scalar
        def _(act):
            chain = [0]

            def link(ins):
                chain[0] += 1
                ins.then_inc(S["chain_a"], 1)
                act.wait_ge(S["chain_a"], chain[0])

            A = nc.scalar.activation
            table = nc.scalar.preload_act_table_set
            exp_set, gelu_set = "natural_log_exp_and_others", "gelu_apprx_tanh_and_others"
            table(exp_set)
            act.dma_start(wqkv_s[:, :, :], w_qkv).then_inc(S["in_wqkv"], 16)
            act.dma_start(sm_s[:, :], small).then_inc(S["in_small"], 16)
            act.dma_start(wx_s[:, :, :], w_x).then_inc(S["in_wx"], 16)
            act.wait_ge(S["eps"], 1)
            for i in range(2):
                act.wait_ge(S["proj"], 1 + 2 * i)
                A(sq[:, i, :], banks[2 * i], ACT.Square).then_inc(S["sq_done"], 1)
            for i in range(2):
                act.wait_ge(S["ms_done"], i + 1)
                link(A(lnms[:, i, :], banks[5 + i], ACT.Ln, bias=eps_rms[:, :]))
                A(rstd[:, i, :], lnms[:, i, :], ACT.Exp, scale=-0.5).then_inc(S["rs_done"], 1)
            act.wait_ge(S["qkn_done"], 1)
            A(piece[:, 0, 0, :], qkn[:, 0, :], ACT.Copy).then_inc(S["p0"], 1)
            act.wait_ge(S["qkn_done"], 2)
            A(piece[:, 1, 0, :], qkn[:, 1, :], ACT.Copy).then_inc(S["p0"], 1)

            act.wait_ge(S["r1d"], 1)
            A(piece[:, 0, 1, :], res[:, 0, :], ACT.Copy).then_inc(S["p1"], 1)
            act.wait_ge(S["r2d"], 1)
            A(piece[:, 1, 1, :], res[:, 1, :], ACT.Copy).then_inc(S["p1"], 1)
            act.wait_ge(S["ctx_mm"], 1)
            A(KsT[:, 0, :], banks[0], ACT.Identity, bias=smcol("bk_s")).then_inc(S["ctx_ev"], 1)
            act.wait_ge(S["ctx_mm"], 2)
            A(KsT[:, 1, :], banks[1], ACT.Identity, bias=smcol("bk_s")).then_inc(S["ctx_ev"], 1)
            act.wait_ge(S["ctx_mm"], 5)
            A(Vs[:, 0:4, :], banks[4].rearrange("p (t c) -> p t c", t=4), ACT.Copy).then_inc(S["ctx_ev"], 1)
            act.wait_ge(S["ctx_mm"], 6)
            A(Vs[:, 4:8, :], banks[5].rearrange("p (t c) -> p t c", t=4), ACT.Copy).then_inc(S["ctx_ev"], 1)

            def rows_out(p):
                act.wait_ge(S["rows_mm"], p + 1)
                act.wait_ge(S["zeroed_q"], 1)
                A(Q6[0:64, 2 * p, 0:T], banks[7][0:64, 0:T], ACT.Copy)
                A(Q6[64:128, 2 * p + 1, 0:T], banks[7][64:128, 0:T], ACT.Copy).then_inc(S["q_rows"], 1)

            def exps(m):
                act.wait_ge(S["max_done"], m + 1)
                if m >= 4:
                    act.wait_ge(S["t_mm"], m - 3)
                A(probs[:, m % 4, 0:P], score_bank(m)[:, 0:P], ACT.Exp, bias=nmax[:, m, 0:1])
                A(probs[:, m % 4, P:3 * P], score_bank(m)[:, P:3 * P], ACT.Exp, bias=nmax[:, m, 1:2]).then_inc(S["exp_done"], 1)

            def trans_out(m):
                act.wait_ge(S["t_mm"], m + 1)
                if m >= 4:
                    act.wait_ge(S["pv_done"], m - 3)
                A(probsT[:, m % 4, :], trans_bank(m)[:, 0:BLOCKS * P], ACT.Copy).then_inc(S["t_done_a"], 1)

            def heads(first, last):
                for m in range(first, last):
                    if m < H - 2 and m % 2 == 0:
                        rows_out(m // 2 + 1)
                    if m < M:
                        exps(m)
                    if m >= 2 and (m - 2) % 4 == 3:
                        trans_out(m - 2)

            def sums(b):
                act.wait_ge(S["pv_done"], H * (b + 1))
                A(lnsum[0:64, b, :], banks[6 + b][64:128, 0:T], ACT.Ln)
                link(A(lnsum[64:128, b, :], banks[6 + b][0:64, T:2 * T], ACT.Ln))
                A(rsum[:, b, :], lnsum[:, b, :], ACT.Exp, scale=-1.0).then_inc(S["rsum_done"], 1)

            def v_out(b):
                act.wait_ge(S["vc_mm"], b + 1)
                A(Vc[:, 2 * b:2 * b + 2, :], bk(b, "B")[:, 0:T].rearrange("p (t c) -> p t c", t=2), ACT.Copy).then_inc(S["vc_done"], 1)

            def exp1(t):
                b = t // 2
                act.wait_ge(S["nm1_done"], t + 1)
                act.wait_ge(S["pv_done"], H * (b + 1))
                A(P1[:, b, t % 2, :], bk(b, "CB"[t % 2]), ACT.Exp, bias=nm1[:, t:t + 1], accum_out=sum1[:, t:t + 1]).then_inc(S["exp1_done"], 1)

            def exp2(h):
                b = h // 2
                act.wait_ge(S["nm2_done"], h + 1)
                act.wait_ge(S["pv_done"], H * (b + 1))
                for s in (2 * (h % 2), 2 * (h % 2) + 1):
                    t = 4 * b + s
                    A(P2[:, b, s, :], bk(b, "AC"[h % 2])[:, (s % 2) * T:(s % 2 + 1) * T], ACT.Exp, bias=nm2[:, t:t + 1],
                      accum_out=sum2[:, t:t + 1]).then_inc(S["exp2_done"], 1)

            def pt1_out(t):
                b = t // 2
                act.wait_ge(S["pt1_mm"], t + 1)
                A(PT1[:, b, :, (t % 2) * P:(t % 2 + 1) * P], bk(b, "BA"[t % 2]).rearrange("p (k q) -> p k q", k=4),
                  ACT.Copy).then_inc(S["pt1_done"], 1)

            def gate_exp(b):
                act.wait_ge(S["gate_mm"], b + 1)
                A(eg[:, b * T:(b + 1) * T], bk(b, "C")[:, 0:T], ACT.Exp, scale=-1.0, bias=nbg[:, :]).then_inc(S["eg_done"], 1)

            def gate_tanh(b):
                act.wait_ge(S["gate_mm"], b + 1)
                A(eg[:, b * T:(b + 1) * T], bk(b, "C")[:, 0:T], ACT.Tanh, scale=0.5, bias=hbg[:, :]).then_inc(S["eg_done"], 1)

            def c2s_out(b):
                act.wait_ge(S["c2s_mm"], b + 1)
                A(c2s[:, b * T:(b + 1) * T], bk(b, "B")[:, 0:T], ACT.Identity, bias=smcol("bv_s")).then_inc(S["c2s_done"], 1)

            def route(b):
                act.wait_ge(S["logit_done"], b + 1)
                act.wait_ge(S["rr2_done"], b + 1)
                for t in (2 * b, 2 * b + 1):
                    A(ex[:, t, :], shift[:, t, :], ACT.Exp, scale=rr2[:, t:t + 1]).then_inc(S["ex_done"], 1)

            def gelu(n):
                act.wait_ge(S["gates_mm"], n + 1)
                if n >= 4:
                    act.wait_ge(S["act_done"], n - 3)
                A(gl[:, n % 4, :], banks[FBANKS[n % 3]][:, 0:T], ACT.Gelu_apprx_tanh).then_inc(S["gl_done"], 1)

            rows_out(0)
            heads(0, H)
            exps(16)
            trans_out(15)
            exps(17)
            exps(18)
            sums(0)
            exps(19)
            exps(20)
            trans_out(19)
            for m in range(21, 25):
                exps(m)
            trans_out(23)
            for m in range(25, 28):
                exps(m)
            exp2(0)
            exp1(0)
            v_out(0)
            exps(28)
            exps(29)
            trans_out(27)
            exps(30)
            exp2(1)
            exps(31)
            trans_out(31)
            exp1(1)
            sums(1)
            pt1_out(0)
            pt1_out(1)
            c2s_out(0)
            gate_exp(0)
            v_out(1)
            exp2(2)
            exp1(2)
            exp1(3)
            pt1_out(2)
            pt1_out(3)
            route(0)
            exp2(3)
            c2s_out(1)
            table(gelu_set)
            for n in range(0, 3):
                gelu(n)
            gate_tanh(1)
            for n in range(3, 11):
                gelu(n)
            table(exp_set)
            route(1)
            table(gelu_set)
            for n in range(11, 20):
                gelu(n)
            for n in range(20, B * E * HT):
                gelu(n)

        @block.vector
        def _(dve):
            chain = [0]

            def link(ins):
                chain[0] += 1
                ins.then_inc(S["chain_v"], 1)
                dve.wait_ge(S["chain_v"], chain[0])

            V = nc.vector
            V.memset(warm[:, :], 0.0).then_inc(S["warm_ready"], 1)
            V.memset(Q6[:, :, :].bitcast(U32), 0).then_inc(S["zeroed_q"], 1)
            dve.wait_ge(S["in_small"], 16)
            V.tensor_scalar(nbg[:, :], smcol("bg"), -1.0, None, ALU.mult)
            V.tensor_scalar(hbg[:, :], smcol("bg"), 0.5, None, ALU.mult)
            link(V.tensor_scalar(qscale[:, :], smcol("q_norm"), SCALE, None, ALU.mult))
            V.tensor_scalar(rw[:, :], smcol("router_w", E), smcol("router_scale"), XSCALE, ALU.mult, ALU.mult).then_inc(S["rw_done"], 1)
            dve.wait_ge(S["in_cf"], 16)
            for i in range(2):
                dve.wait_ge(S["proj"], 2 + 2 * i)
                v3 = lambda ap: ap.rearrange("p (b t) -> p b t", b=B)
                V.tensor_tensor(v3(rot_s[:, i, :]), v3(banks[2 * i + 1]), sin.broadcast_to([P, B, T]), ALU.mult)
                dve.wait_ge(S["sq_done"], i + 1)
                link(V.tensor_tensor(v3(rot_c[:, i, :]), v3(banks[2 * i]), cos.broadcast_to([P, B, T]), ALU.mult))
                V.tensor_tensor(rot[:, i, :], rot_c[:, i, :], rot_s[:, i, :], ALU.add).then_inc(S["rot_done"], 1)
            for i, w in enumerate((qscale[:, :], smcol("k_norm"))):
                dve.wait_ge(S["rs_done"], i + 1)
                dve.wait_ge(S["rot_done"], i + 1)
                V.scalar_tensor_tensor(out=qkn[:, i, :], in0=rot[:, i, :], scalar=w, in1=rstd[:, i, :],
                                       op0=ALU.mult, op1=ALU.mult).then_inc(S["qkn_done"], 1)
            dve.wait_ge(S["p0"], 1)
            dve.wait_ge(S["qkn_done"], 1)
            V.tensor_tensor(res[:, 0, :], qkn[:, 0, :], piece[:, 0, 0, :], ALU.subtract).then_inc(S["r1d"], 1)
            dve.wait_ge(S["vproj"], 1)
            dve.wait_ge(S["zeroed_v"], 1)
            for half in range(2):
                for t in range(NT):
                    own = VP[:, t, half * (H // 2):(half + 1) * (H // 2), :].rearrange("p h c -> p (h c)")
                    src = banks[4][:, t * P + half * 64:t * P + half * 64 + 64].rearrange("p (h d) -> p h d", d=D)
                    ins = V.tensor_copy(diagonal(own, 64 * half), src)
            ins.then_inc(S["vp_done"], 1)
            dve.wait_ge(S["p1"], 1)
            dve.wait_ge(S["r1d"], 1)
            V.tensor_tensor(piece[:, 0, 2, :], res[:, 0, :], piece[:, 0, 1, :], ALU.subtract).then_inc(S["p2"], 1)
            for b in range(B):
                dve.wait_ge(S["ctx_mm"], 3 + b)
                V.tensor_scalar(QsT[:, b, :], banks[2 + b], smcol("bq_s"), XSCALE, ALU.add, ALU.mult).then_inc(S["ctx_ev"], 1)

            def rows_out(p):
                dve.wait_ge(S["rows_mm"], p + 1)
                dve.wait_ge(S["zeroed_k"], 1)
                V.tensor_copy(K6[:, p, 0:T], banks[3][:, 0:T]).then_inc(S["k_rows"], 1)

            def maxes(m):
                dve.wait_ge(S["s_done"], m + 1)
                V.tensor_reduce(nmax[:, m, 0:1], score_bank(m)[:, 0:P], AX.X, ALU.max, negate=True)
                V.tensor_reduce(nmax[:, m, 1:2], score_bank(m)[:, P:3 * P], AX.X, ALU.max, negate=True).then_inc(S["max_done"], 1)

            def trans_out(m):
                dve.wait_ge(S["t_mm"], m + 1)
                if m >= 4:
                    dve.wait_ge(S["pv_done"], m - 3)
                V.tensor_copy(probsT[:, m % 4, :], trans_bank(m)[:, 0:BLOCKS * P]).then_inc(S["t_done_v"], 1)

            def heads(first, last):
                for m in range(first, last):
                    if m < H - 2 and m % 2 == 0:
                        rows_out(m // 2 + 1)
                    if m < M:
                        maxes(m)
                    if m >= 2 and (m - 2) % 4 != 3:
                        trans_out(m - 2)

            def attn_norm(b):
                dve.wait_ge(S["rsum_done"], b + 1)
                c = slice(b * T, (b + 1) * T)
                V.tensor_tensor(attnT[0:64, c], banks[6 + b][0:64, 0:T], rsum[0:64, b, :], ALU.mult)
                V.tensor_tensor(attnT[64:128, c], banks[6 + b][64:128, T:2 * T], rsum[64:128, b, :], ALU.mult).then_inc(S["attn_done"], 1)

            def norm_in(i, b, psum, other, mm, count):
                t2 = slice(2 * b, 2 * b + 2)
                dve.wait_ge(S[mm], count)
                link(V.tensor_tensor(pre[:, i, t2, :], psum, other[:, t2, :], ALU.add))
                for t in (2 * b, 2 * b + 1):
                    ins = V.bn_stats(stats[:, i, t, :], pre[:, i, t, :])
                link(ins)
                for t in (2 * b, 2 * b + 1):
                    ins = V.bn_aggr(mv[:, i, t, :], stats[:, i, t, :])
                ins.then_inc(mv_done[i], 1)

            def norm_out(i, b, dst, done):
                dve.wait_ge(rsln_done[i], b + 1)
                dve.wait_ge(mv_done[i], b + 1)
                for t in (2 * b, 2 * b + 1):
                    V.tensor_scalar(dst[:, t, :], pre[:, i, t, :], mv[:, i, t, 0:1], rs_ln[:, i, t:t + 1],
                                    ALU.subtract, ALU.mult).then_inc(S[done], 1)

            def xT_out(i, b):
                dst = (x1T, x2T)[i]
                dve.wait_ge(S[("xt_mm", "x2t_mm")[i]], b + 1)
                V.tensor_copy(dst[:, b * T:(b + 1) * T], bk(b, "A")[:, 0:T]).then_inc(S[("xt_done", "x2t_done")[i]], 1)

            def qk_out(b):
                dve.wait_ge(S["qkc_mm"], b + 1)
                c = slice(b * T, (b + 1) * T)
                V.tensor_scalar(QcT[:, c], bk(b, "A")[:, 0:T], smcol("bq_c"), XSCALE, ALU.add, ALU.mult)
                V.tensor_scalar(KcT[:, c], bk(b, "A")[:, T:2 * T], smcol("bk_c"), None, ALU.add).then_inc(S["qkc_done"], 1)

            def max1(t):
                dve.wait_ge(S["s1_mm"], t + 1)
                V.tensor_reduce(nm1[:, t:t + 1], bk(t // 2, "CB"[t % 2]), AX.X, ALU.max, negate=True).then_inc(S["nm1_done"], 1)

            def max2(h):
                b = h // 2
                dve.wait_ge(S["s2_mm"], h + 1)
                V.tensor_reduce(nm2[:, 2 * h:2 * h + 2], bk(b, "AC"[h % 2]).rearrange("p (h k) -> p h k", h=2),
                                AX.X, ALU.max, negate=True).then_inc(S["nm2_done"], 1)

            def p1_norm(t):
                dve.wait_ge(S["exp1_done"], t + 1)
                link(V.reciprocal(r1[:, t:t + 1], sum1[:, t:t + 1]))
                p = P1[:, t // 2, t % 2, :]
                V.tensor_scalar(p, p, r1[:, t:t + 1], None, ALU.mult).then_inc(S["p1n_done"], 1)

            def pairs(b):
                dve.wait_ge(S["exp2_done"], 4 * (b + 1))
                link(V.reciprocal(r2[:, 4 * b:4 * b + 4], sum2[:, 4 * b:4 * b + 4]))
                for s in range(4):
                    t = 4 * b + s
                    ins = V.tensor_scalar(pair_r[:, t, :], constf("pair"), r2[:, t:t + 1], None, ALU.mult)
                ins.then_inc(S["pair_done"], 1)

            def pt2_out(b):
                dve.wait_ge(S["pt2_mm"], b + 1)
                V.tensor_copy(PT2[:, b, :, :], bk(b, "C").rearrange("p (k q) -> p k q", k=2)).then_inc(S["pt2_done"], 1)

            def s2c_out(b):
                c = slice(b * T, (b + 1) * T)
                dve.wait_ge(S["s2c_mm"], b + 1)
                V.tensor_scalar(s2c[:, c], bk(b, "A")[:, 0:T], smcol("bv_c"), None, ALU.add).then_inc(S["s2c_done"], 1)
                dve.wait_ge(S["s2c_done"], b + 1)
                dve.wait_ge(S["c2s_done"], b + 1)
                link(V.tensor_tensor(diff[:, c], c2s[:, c], s2c[:, c], ALU.subtract))

            def mix_exp(b):
                c = slice(b * T, (b + 1) * T)
                dve.wait_ge(S["eg_done"], b + 1)
                link(V.tensor_scalar(eg1[:, c], eg[:, c], 1.0, None, ALU.add))
                link(V.reciprocal(gate[:, c], eg1[:, c]))
                link(V.tensor_tensor(gd[:, b, :], gate[:, c], diff[:, c], ALU.mult))
                V.tensor_tensor(mixT[:, b, :], gd[:, b, :], s2c[:, c], ALU.add).then_inc(S["mix_done"], 1)

            def mix_tanh(b):
                c = slice(b * T, (b + 1) * T)
                link(V.tensor_scalar(eg1[:, c], diff[:, c], 0.5, None, ALU.mult))
                dve.wait_ge(S["eg_done"], b + 1)
                link(V.scalar_tensor_tensor(out=gd[:, b, :], in0=eg[:, c], scalar=1.0, in1=eg1[:, c], op0=ALU.add, op1=ALU.mult))
                V.tensor_tensor(mixT[:, b, :], gd[:, b, :], s2c[:, c], ALU.add).then_inc(S["mix_done"], 1)

            def logits(b):
                t2 = slice(2 * b, 2 * b + 2)
                dve.wait_ge(S["consts"], 1)
                dve.wait_ge(S["logit_mm"], b + 1)
                link(V.tensor_copy(logit[:, t2, :], bk(b, "C")[:, 0:2 * E].rearrange("p (t e) -> p t e", t=2)))
                link(V.tensor_reduce(nml[:, t2], logit[:, t2, :], AX.X, ALU.max, negate=True))
                for t in (2 * b, 2 * b + 1):
                    ins = V.tensor_scalar(shift[:, t, :], logit[:, t, :], nml[:, t:t + 1], None, ALU.add)
                ins.then_inc(S["logit_done"], 1)
                for t in (2 * b, 2 * b + 1):
                    other = logit[:, t, :].rearrange("p (o e) -> p o e", o=1).broadcast_to([P, E, E])
                    own = logit[:, t, :].rearrange("p (e o) -> p e o", o=1).broadcast_to([P, E, E])
                    V.tensor_tensor(beats[:, t, :, :], other, own, ALU.is_gt)
                    ins = V.tensor_tensor(ties[:, t, :, :], other, own, ALU.is_equal)
                link(ins)
                for t in (2 * b, 2 * b + 1):
                    ins = V.tensor_tensor(ties[:, t, :, :], ties[:, t, :, :], lower[:, :, :], ALU.mult)
                link(ins)
                link(V.tensor_tensor(beats[:, t2, :, :], beats[:, t2, :, :], ties[:, t2, :, :], ALU.add))
                link(V.tensor_reduce(rank[:, t2, :], beats[:, t2, :, :], AX.X, ALU.add))

            def combine(b):
                t2 = slice(2 * b, 2 * b + 2)

                def wide(ap):
                    return ap.rearrange("p (t o) -> p t o", o=1).broadcast_to([P, 2, E])

                dve.wait_ge(S["ex_done"], 2 * (b + 1))
                link(V.scalar_tensor_tensor(out=gw[:, t2, :], in0=rank[:, t2, :], scalar=1.5, in1=ex[:, t2, :],
                                            op0=ALU.is_lt, op1=ALU.mult))
                es = smcol("expert_scale", E).rearrange("p (o e) -> p o e", o=1).broadcast_to([P, 2, E])
                V.tensor_tensor(cw[:, t2, :], gw[:, t2, :], es, ALU.mult)
                link(V.tensor_reduce(ren[:, t2], gw[:, t2, :], AX.X, ALU.add))
                link(V.reciprocal(renr[:, t2], ren[:, t2]))
                link(V.tensor_tensor(comb[:, t2, :], cw[:, t2, :], wide(renr[:, t2]), ALU.mult))
                link(V.tensor_copy(combp[:, t2, 0, :], comb[:, t2, :]))
                link(V.tensor_tensor(combr[:, t2, :], comb[:, t2, :], combp[:, t2, 0, :], ALU.subtract))
                link(V.tensor_copy(combp[:, t2, 1, :], combr[:, t2, :]))
                V.tensor_tensor(combp[:, t2, 2, :], combr[:, t2, :], combp[:, t2, 1, :], ALU.subtract).then_inc(S["comb_done"], 1)

            def combT_out(b):
                dve.wait_ge(S["combT_mm"], b + 1)
                V.tensor_copy(combT[:, b * T:(b + 1) * T], bk(b, "B").bitcast(BF16)[0:PIECES * E, 0:T]).then_inc(S["combT_done"], 1)

            pairview = lambda ap: ap[:, 0:T].rearrange("p (t c) -> p t c", t=2)

            def norm1_in(b):
                dve.wait_ge(S["in_xtok"], 16)
                norm_in(0, b, pairview(bk(b, "A")), x_s, "wout_done", b + 1)

            def norm2_in(b):
                norm_in(1, b, pairview(bk(b, "B")), x1, "mix_mm", b + 1)

            def norm3_in(b):
                norm_in(2, b, pairview(banks[DOWN[b]]), x2, "out_mm", E * HT * (b + 1))

            def scaled(m):
                b, e = m // E, m % E
                dve.wait_ge(S["bc_mm"], m + 1)
                dve.wait_ge(S["x2t_done"], b + 1)
                V.tensor_tensor(x2c[:, b, e, :], x2T[:, b * T:(b + 1) * T], banks[SPREAD][:, 0:T], ALU.mult).then_inc(S["x2c_done"], 1)

            def acts_of(n):
                dve.wait_ge(S["gl_done"], n + 1)
                if n >= 4:
                    dve.wait_ge(S["out_mm"], n - 3)
                V.tensor_tensor(acts[:, n % 4, :], banks[FBANKS[n % 3]][:, T:2 * T], gl[:, n % 4, :], ALU.mult).then_inc(S["act_done"], 1)

            def x1_out(b):
                norm_out(0, b, x1, "xn_done")

            def x2_out(b):
                norm_out(1, b, x2, "x2n_done")

            def ffn(first, last):
                for n in range(first, last):
                    if n % HT == 1 and n // HT + 1 < B * E:
                        scaled(n // HT + 1)
                    acts_of(n)

            def y_out(b):
                norm_out(2, b, y_s, "y_ready")

            rows_out(0)
            heads(0, H)
            trans_out(14)
            for m in range(16, 19):
                maxes(m)
            trans_out(16)
            trans_out(17)
            maxes(19)
            attn_norm(0)
            maxes(20)
            trans_out(18)
            maxes(21)
            norm1_in(0)
            maxes(22)
            trans_out(20)
            maxes(23)
            trans_out(21)
            x1_out(0)
            maxes(24)
            trans_out(22)
            maxes(25)
            xT_out(0, 0)
            maxes(26)
            qk_out(0)
            maxes(27)
            maxes(28)
            max2(0)
            max1(0)
            trans_out(24)
            trans_out(25)
            maxes(29)
            trans_out(26)
            p1_norm(0)
            maxes(30)
            trans_out(28)
            trans_out(29)
            max2(1)
            maxes(31)
            trans_out(30)
            pairs(0)
            max1(1)
            p1_norm(1)
            attn_norm(1)
            pt2_out(0)
            norm1_in(1)
            s2c_out(0)
            x1_out(1)
            xT_out(0, 1)
            mix_exp(0)
            qk_out(1)
            norm2_in(0)
            max2(2)
            max1(2)
            x2_out(0)
            max1(3)
            xT_out(1, 0)
            p1_norm(2)
            p1_norm(3)
            logits(0)
            max2(3)
            combine(0)
            pairs(1)
            combT_out(0)
            pt2_out(1)
            scaled(0)
            s2c_out(1)
            scaled(1)
            scaled(2)
            acts_of(0)
            acts_of(1)
            scaled(3)
            acts_of(2)
            mix_tanh(1)
            acts_of(3)
            acts_of(4)
            norm2_in(1)
            scaled(4)
            acts_of(5)
            scaled(5)
            x2_out(1)
            xT_out(1, 1)
            scaled(6)
            acts_of(6)
            acts_of(7)
            logits(1)
            for n in range(8, 11):
                acts_of(n)
            scaled(7)
            combine(1)
            acts_of(11)
            acts_of(12)
            combT_out(1)
            acts_of(13)
            scaled(8)
            acts_of(14)
            scaled(9)
            acts_of(15)
            scaled(10)
            for n in range(16, 19):
                acts_of(n)
            norm3_in(0)
            acts_of(19)
            y_out(0)
            ffn(20, B * E * HT)
            norm3_in(1)
            y_out(1)

        @block.tensor
        def _(pe):
            def mm(out, lhsT, rhs, start=True, stop=True, **kw):
                return nc.tensor.matmul(out, lhsT, rhs, start=start, stop=stop, **kw)

            pe.wait_ge(S["warm_ready"], 1)
            for _ in range(8):
                mm(banks[7], warm[:, 0:P], warm[:, :])
            pe.wait_ge(S["in_x"], 16)
            pe.wait_ge(S["in_wqkv"], 16)
            for i in range(4):
                mm(banks[i], wqkv_s[:, i, :], xT_s[:, :]).then_inc(S["proj"], 1)
            for t in range(NT):
                ins = mm(banks[4][:, t * P:(t + 1) * P], xT_s[:, t * P:(t + 1) * P], wqkv_s[:, 4, :])
            ins.then_inc(S["vproj"], 1)
            pe.wait_ge(S["in_cf"], 16)
            for i in range(2):
                pe.wait_ge(S["sq_done"], i + 1)
                mm(banks[5 + i], constf("mean8"), sq[:, i, :]).then_inc(S["ms_done"], 1)
            pe.wait_ge(S["in_ctx"], 16)
            pe.wait_ge(S["in_wx"], 16)
            pe.wait_ge(S["rot_done"], 2)
            for j, w in enumerate(("Wk_s", "Wq_s")):
                for b in range(B):
                    mm(banks[2 * j + b], wx(w), ctxT_s[:, b * L:(b + 1) * L]).then_inc(S["ctx_mm"], 1)
            pe.wait_ge(S["vp_done"], 1)
            pe.wait_ge(S["rs_done"], 1)
            for b in range(B):
                for t in range(4):
                    k = 4 * b + t
                    ins = mm(banks[4 + b][:, t * P:(t + 1) * P], ctxT_s[:, k * P:(k + 1) * P], wx("Wv_s"))
                ins.then_inc(S["ctx_mm"], 1)

            mask = constb("mask").rearrange("p (o k) -> p o k", o=1).broadcast_to([P, 2, P])
            pe.wait_ge(S["in_cb"], 16)
            pe.wait_ge(S["ctx_ev"], 6)

            def rows(p):
                r = slice(32 * (p // 2), 32 * (p // 2) + 32)
                if p:
                    pe.wait_ge(S["q_rows"], p)
                    pe.wait_ge(S["k_rows"], p)
                for i in range(2):
                    for n in range(PIECES):
                        ins = mm(banks[(7, 3)[i]][:, 0:T], sel_rows[r, p % 2, i, n, :], piece[r, i, n, 0:T],
                                 start=(n == 0), stop=(n == PIECES - 1))
                ins.then_inc(S["rows_mm"], 1)

            def scores(m):
                b, h = m // H, m % H
                if m >= H:
                    pe.wait_ge(S["exp_done"], m - 1)
                elif m >= 3:
                    pe.wait_ge(S["exp_done"], m - 2)
                if b == 0:
                    pe.wait_ge(S["q_rows"], m // 2 + 1)
                    pe.wait_ge(S["k_rows"], m // 2 + 1)
                elif m == H:
                    pe.wait_ge(S["q6_in"], 6 * 16)
                    pe.wait_ge(S["k6_in"], 2 * 16)
                o = score_bank(m)
                q0 = b * T
                diag = o[:, 0:4 * P].rearrange("p (n k) -> p n k", n=2)[:, :, 0:P]
                mm(diag, identb, mask, stop=False, skip_group_check=True)
                mm(o[:, P:3 * P], Q6[:, h, q0 + P:q0 + T], K6[:, h // 2, q0:q0 + T], start=False, stop=False, skip_group_check=True)
                mm(o[:, 0:P], Q6[:, h, q0:q0 + P], K6[:, h // 2, q0:q0 + P], start=False,
                   skip_group_check=True).then_inc(S["s_done"], 1)

            def transposes(m):
                pe.wait_ge(S["exp_done"], m + 1)
                if m >= 2:
                    pe.wait_ge(*transposed(m - 2))
                for i in range(BLOCKS):
                    ins = nc.tensor.transpose(trans_bank(m)[:, i * P:(i + 1) * P], probs[:, m % 4, i * P:(i + 1) * P], ident)
                ins.then_inc(S["t_mm"], 1)

            def values(m):
                b, h = m // H, m % H
                pe.wait_ge(*transposed(m))
                acc = banks[6 + b][:, (h // 8) * T:(h // 8 + 1) * T]
                mm(acc, VP[:, 2 * b, h, :], probsT[:, m % 4, 0:T], start=(h % 8 == 0), stop=False, skip_group_check=True)
                mm(acc[:, P:T], VP[:, 2 * b + 1, h, :], probsT[:, m % 4, T:T + P], start=False, stop=(h % 8 == 7),
                   skip_group_check=True).then_inc(S["pv_done"], 1)

            def heads(first, last):
                for m in range(first, last):
                    if m < H - 2 and m % 2 == 0:
                        rows(m // 2 + 1)
                    if m < M:
                        scores(m)
                    if 2 <= m < M + 2:
                        transposes(m - 2)
                    if m >= 3:
                        values(m - 3)

            def attn_out(b):
                pe.wait_ge(S["in_wout"], 16)
                pe.wait_ge(S["attn_done"], b + 1)
                for t in (2 * b, 2 * b + 1):
                    ins = mm(bk(b, "A")[:, (t % 2) * P:(t % 2 + 1) * P], attnT[:, t * P:(t + 1) * P], wout_s[:, :])
                ins.then_inc(S["wout_done"], 1)

            def x_t(i, b):
                src = (x1, x2)[i]
                pe.wait_ge(S[("xn_done", "x2n_done")[i]], 2 * (b + 1))
                for t in (2 * b, 2 * b + 1):
                    ins = nc.tensor.transpose(bk(b, "A")[:, (t % 2) * P:(t % 2 + 1) * P], src[:, t, :], ident)
                ins.then_inc(S[("xt_mm", "x2t_mm")[i]], 1)

            def qk_char(b):
                c = slice(b * T, (b + 1) * T)
                pe.wait_ge(S["xt_done"], b + 1)
                mm(bk(b, "A")[:, 0:T], wx("Wq_c"), x1T[:, c])
                mm(bk(b, "A")[:, T:2 * T], wx("Wk_c"), x1T[:, c]).then_inc(S["qkc_mm"], 1)

            def v_char(b):
                pe.wait_ge(S["xt_done"], b + 1)
                pe.wait_ge(S["exp_done"], H * (b + 1))
                for t in (2 * b, 2 * b + 1):
                    ins = mm(bk(b, "B")[:, (t % 2) * P:(t % 2 + 1) * P], x1T[:, t * P:(t + 1) * P], wx("Wv_c"))
                ins.then_inc(S["vc_mm"], 1)

            def s1(t):
                b = t // 2
                pe.wait_ge(S["qkc_done"], b + 1)
                pe.wait_ge(S["exp_done"], H * (b + 1))
                if t % 2:
                    pe.wait_ge(S["vc_done"], b + 1)
                mm(bk(b, "CB"[t % 2]), QcT[:, t * P:(t + 1) * P], KsT[:, b, :]).then_inc(S["s1_mm"], 1)

            def s2(h):
                b, half = h // 2, h % 2
                pe.wait_ge(S["qkc_done"], b + 1)
                if half:
                    pe.wait_ge(S["exp1_done"], 2 * b + 1)
                for s in (2 * half, 2 * half + 1):
                    ins = mm(bk(b, "AC"[half])[:, (s % 2) * T:(s % 2 + 1) * T], QsT[:, b, s * P:(s + 1) * P], KcT[:, b * T:(b + 1) * T])
                ins.then_inc(S["s2_mm"], 1)

            def pt1(t):
                b, q = t // 2, t % 2
                pe.wait_ge(S["p1n_done"], t + 1)
                pe.wait_ge(*((S["exp1_done"], 2 * b + 2) if q == 0 else (S["exp2_done"], 4 * b + 2)))
                for k in range(4):
                    ins = nc.tensor.transpose(bk(b, "BA"[q])[:, k * P:(k + 1) * P], P1[:, b, q, k * P:(k + 1) * P], ident)
                ins.then_inc(S["pt1_mm"], 1)

            def pt2(b):
                pe.wait_ge(S["pair_done"], b + 1)
                for k in range(2):
                    for s in range(4):
                        o = k * T + s * 64
                        ins = mm(bk(b, "C")[:, o:o + 64], P2[:, b, s, k * P:(k + 1) * P], pair_r[:, 4 * b + s, :])
                ins.then_inc(S["pt2_mm"], 1)

            def c2s_mm(b):
                pe.wait_ge(S["pt1_done"], 2 * (b + 1))
                for k in range(4):
                    ins = mm(bk(b, "B")[:, 0:T], Vs[:, 4 * b + k, :], PT1[:, b, k, :], start=(k == 0), stop=(k == 3))
                ins.then_inc(S["c2s_mm"], 1)

            def s2c_mm(b):
                pe.wait_ge(S["pt1_done"], 2 * (b + 1))
                pe.wait_ge(S["pt2_done"], b + 1)
                for k in range(2):
                    ins = mm(bk(b, "A")[:, 0:T], Vc[:, 2 * b + k, :], PT2[:, b, k, :], start=(k == 0), stop=(k == 1))
                ins.then_inc(S["s2c_mm"], 1)

            def gate_mm(b):
                c = slice(b * T, (b + 1) * T)
                pe.wait_ge(S["c2s_done"], b + 1)
                mm(bk(b, "C")[:, 0:T], wx("Wg_c"), c2s[:, c], stop=False)
                pe.wait_ge(S["s2c_done"], b + 1)
                mm(bk(b, "C")[:, 0:T], wx("Wg_s"), s2c[:, c], start=False).then_inc(S["gate_mm"], 1)

            def mix_t(b):
                pe.wait_ge(S["mix_done"], b + 1)
                for t in range(2):
                    ins = nc.tensor.transpose(bk(b, "B")[:, t * P:(t + 1) * P], mixT[:, b, t * P:(t + 1) * P], ident)
                ins.then_inc(S["mix_mm"], 1)

            def logit_mm(b):
                pe.wait_ge(S["rw_done"], 1)
                pe.wait_ge(S["x2t_done"], b + 1)
                for t in (2 * b, 2 * b + 1):
                    ins = mm(bk(b, "C")[:, (t % 2) * E:(t % 2 + 1) * E], x2T[:, t * P:(t + 1) * P], rw[:, :])
                ins.then_inc(S["logit_mm"], 1)

            def comb_t(b):
                pe.wait_ge(S["comb_done"], b + 1)
                for t in (2 * b, 2 * b + 1):
                    ins = nc.tensor.transpose(bk(b, "B").bitcast(BF16)[0:PIECES * E, (t % 2) * P:(t % 2 + 1) * P],
                                              combp[:, t, :, :].rearrange("p n e -> p (n e)"), identb)
                ins.then_inc(S["combT_mm"], 1)

            def spread(m):
                b, e = m // E, m % E
                pe.wait_ge(S["combT_done"], b + 1)
                if m >= 1:
                    pe.wait_ge(S["x2c_done"], m)
                mm(banks[SPREAD][:, 0:T], sel_expert[:, e, :], combT[:, b * T:(b + 1) * T]).then_inc(S["bc_mm"], 1)

            def gates(n):
                b, e, ht = n // (E * HT), n // HT % E, n % HT
                if n == 0:
                    pe.wait_ge(S["t_done_v"], M - M // 4)
                    pe.wait_ge(S["t_done_a"], M // 4)
                    pe.wait_ge(S["in_gat"], 32)
                pe.wait_ge(S["x2t_done"], b + 1)
                if n >= 3:
                    pe.wait_ge(S["act_done"], n - 2)
                mm(banks[FBANKS[n % 3]][:, 0:T], gat_s[:, e, 0, ht, :], x2T[:, b * T:(b + 1) * T])
                pe.wait_ge(S["x2c_done"], b * E + e + 1)
                mm(banks[FBANKS[n % 3]][:, T:2 * T], gat_s[:, e, 1, ht, :], x2c[:, b, e, :]).then_inc(S["gates_mm"], 1)

            def down(n):
                b, e, ht = n // (E * HT), n // HT % E, n % HT
                i = n % (E * HT)
                if n == 0:
                    pe.wait_ge(S["in_lin"], 16)
                pe.wait_ge(S["act_done"], n + 1)
                for t in range(2):
                    ins = mm(banks[DOWN[b]][:, t * P:(t + 1) * P], acts[:, n % 4, t * P:(t + 1) * P], lin_s[:, e, ht, :],
                             start=(i == 0 and t == 0), stop=(i == E * HT - 1), skip_group_check=True)
                ins.then_inc(S["out_mm"], 1)

            def ffn(first, last):
                for n in range(first, last):
                    gates(n)
                    if n % HT == 1 and n // HT + 1 < B * E:
                        spread(n // HT + 1)
                    if n >= 1:
                        down(n - 1)

            for _ in range(8):
                mm(banks[6], warm[:, 0:P], warm[:, :])
            pe.wait_ge(S["p2"], 2)
            rows(0)
            heads(0, H)
            transposes(14)
            scores(16)
            values(13)
            transposes(15)
            scores(17)
            values(14)
            scores(18)
            transposes(16)
            values(15)
            transposes(17)
            scores(19)
            values(16)
            transposes(18)
            scores(20)
            values(17)
            scores(21)
            transposes(19)
            attn_out(0)
            values(18)
            scores(22)
            transposes(20)
            values(19)
            scores(23)
            transposes(21)
            values(20)
            scores(24)
            transposes(22)
            values(21)
            scores(25)
            x_t(0, 0)
            transposes(23)
            values(22)
            scores(26)
            qk_char(0)
            values(23)
            scores(27)
            scores(28)
            s2(0)
            s1(0)
            transposes(24)
            transposes(25)
            scores(29)
            v_char(0)
            transposes(26)
            values(24)
            transposes(27)
            scores(30)
            values(25)
            values(26)
            transposes(28)
            transposes(29)
            s2(1)
            scores(31)
            transposes(30)
            values(27)
            values(28)
            s1(1)
            transposes(31)
            for m in range(29, 32):
                values(m)
            pt1(0)
            pt1(1)
            pt2(0)
            attn_out(1)
            c2s_mm(0)
            s2c_mm(0)
            gate_mm(0)
            x_t(0, 1)
            qk_char(1)
            v_char(1)
            mix_t(0)
            s2(2)
            s1(2)
            s1(3)
            x_t(1, 0)
            s2(3)
            logit_mm(0)
            pt1(2)
            pt1(3)
            c2s_mm(1)
            comb_t(0)
            pt2(1)
            spread(0)
            s2c_mm(1)
            spread(1)
            gates(0)
            gates(1)
            spread(2)
            gates(2)
            spread(3)
            gate_mm(1)
            gates(3)
            gates(4)
            down(0)
            mix_t(1)
            spread(4)
            gates(5)
            gates(6)
            down(1)
            spread(5)
            gates(7)
            gates(8)
            x_t(1, 1)
            spread(6)
            down(2)
            down(3)
            logit_mm(1)
            spread(7)
            down(4)
            gates(9)
            gates(10)
            for n in range(5, 8):
                down(n)
            for n in range(11, 14):
                gates(n)
            down(8)
            comb_t(1)
            down(9)
            gates(14)
            spread(8)
            down(10)
            down(11)
            spread(9)
            for n in range(15, 18):
                gates(n)
            spread(10)
            gates(18)
            for n in range(12, 18):
                down(n)
            gates(19)
            down(18)
            ffn(20, B * E * HT)
            down(B * E * HT - 1)


def _constants():
    import numpy as np

    def bf16_bits(a):
        return (np.ascontiguousarray(a, np.float32).view(np.uint32) >> 16).astype(np.uint16)

    ident = np.eye(P, dtype=np.float32)
    half = D // 2
    inv_freq = (1.0 / np.float32(10000.0) ** (np.arange(half, dtype=np.float32) * np.float32(2.0) / np.float32(D))).astype(np.float32)
    ang = (np.arange(T, dtype=np.float32)[:, None] * inv_freq[None, :]).astype(np.float32)
    c, s = np.cos(ang).T, np.sin(ang).T
    cos = np.tile(np.concatenate([c, c]), (H, 1))
    sin = np.tile(np.concatenate([-s, s]), (H, 1))
    mean8 = np.kron(np.eye(H), np.full((D, D), 1.0 / D))
    pair = np.kron(np.eye(P // 2), np.full((2, 1), 0.5))
    const_f = np.concatenate([ident, cos, sin, mean8, pair], 1).astype(np.float32)
    i = np.arange(P)
    lowest = (np.float32(LOWEST).view(np.uint32) & np.uint32(0xFFFF0000)).view(np.float32)
    mask = np.where(i[:, None] < i[None, :], lowest, np.float32(0))
    sel_expert = np.zeros((P, E, P), np.float32)
    for n in range(PIECES):
        sel_expert[n * E + np.arange(E), np.arange(E)] = 1.0
    sel_rows = np.zeros((P, 2, 2, PIECES, P), np.float32)
    for r in range(P):
        pair, odd, d = r // 16, r // D % 2, r % D
        for i, pieces in enumerate((Q_PIECE, K_PIECE)):
            for slot, n in enumerate(pieces):
                sel_rows[r, pair % 2, i, n, 64 * odd + slot * D + d] = 1.0
    const_b = bf16_bits(np.concatenate([ident, mask, sel_expert.reshape(P, -1), sel_rows.reshape(P, -1)], 1))
    return np.ascontiguousarray(const_f), const_b


def kernel(**inputs):
    import numpy as np
    import concourse.bacc as bacc
    from concourse import mybir as mb
    from concourse.bass_utils import run_bass_kernel_spmd as run

    a = {k: np.asarray(v) for k, v in inputs.items()}
    tok = a["x"].reshape(N, C)
    w = a["L0_attn_w_qkv"].reshape(3, H, D, C)
    swapped = np.concatenate([w[:, :, D // 2:], w[:, :, :D // 2]], 2)

    def cols(m):
        return m.reshape(P, C).T

    wx = {n: a["L0_xattn_" + n].T for n in WX if not n.startswith("Wg")}
    wx["Wg_c"], wx["Wg_s"] = a["L0_xattn_Wg"][:, :C].T, a["L0_xattn_Wg"][:, C:].T
    small = [a["L0_xattn_" + n][:, None] for n in ("bq_c", "bk_s", "bv_s", "bq_s", "bk_c", "bv_c", "bg")]
    small += [np.tile(a["L0_attn_q_norm_w"], H)[:, None], np.tile(a["L0_attn_k_norm_w"], H)[:, None]]
    small += [a["L0_ffn_router_scale"][:, None], a["L0_ffn_router_w"]]
    small += [np.broadcast_to(a["L0_ffn_per_expert_scale"], (P, E))]
    const_f, const_b = _constants()
    arrays = {
        "xT": tok.T,
        "x_tok": tok.reshape(NT, P, C).transpose(1, 0, 2),
        "ctxT": a["ctx_1024"].reshape(B * L, C).T,
        "w_qkv": np.stack([cols(w[0]), cols(swapped[0]), cols(w[1]), cols(swapped[1]), cols(w[2])], 1),
        "w_out": a["L0_attn_w_out"].T,
        "w_x": np.stack([wx[n] for n in WX], 1),
        "small": np.concatenate(small, 1),
        "gating": a["L0_ffn_gating_w"].reshape(E, 2, HT, P, C).transpose(4, 0, 1, 2, 3),
        "linear": a["L0_ffn_linear_w"].reshape(E, HT, P, C).transpose(2, 0, 1, 3),
        "const_f": const_f,
        "const_b": const_b,
    }
    arrays = {k: np.ascontiguousarray(v) for k, v in arrays.items()}
    nc = bacc.Bacc("TRN2", target_bir_lowering=False, num_devices=1)
    args = [nc.dram_tensor(k, v.shape, mb.dt.from_np(v.dtype), kind="ExternalInput").ap() for k, v in arrays.items()]
    out = nc.dram_tensor("out", (P, NT, C), mb.dt.float32, kind="ExternalOutput").ap()
    post_norm_decoder(nc, *args, out)
    r = run(nc, [arrays], core_ids=[0])
    y = r.results[0]["out"]
    return np.ascontiguousarray(y.transpose(1, 0, 2)).reshape(B, T, C)
```

```python
from contextlib import ExitStack

import concourse.bass as bass
from concourse import mybir

F32 = mybir.dt.float32
F32R = mybir.dt.float32r
BF16 = mybir.dt.bfloat16
U16 = mybir.dt.uint16
U32 = mybir.dt.uint32
ALU = mybir.AluOpType
ACT = mybir.ActivationFunctionType
AX = mybir.AxisListType

P = 128
B, T, C = 2, 256, 128
H, D = 16, 8
L = 512
E, HID = 8, 256
N = B * T
NT = N // P
HT = HID // P
M = B * H
BLOCKS = 3
RING = 3
NR = 4
PIECES = 3
FORBIDDEN = 1e30
Q_PIECE = (0, 1, 2, 0, 1, 0)
K_PIECE = (0, 0, 0, 1, 1, 2)

CF = {"ident": (0, 128), "cos": (128, 384), "sin": (384, 640), "mean8": (640, 768), "pair": (768, 832), "mask": (832, 832 + 2 * P)}
CFW = 832 + 2 * P
CB = {"ident": (0, P), "sel_expert": (P, P + E * P), "sel_rows": (P + E * P, P + E * P + 12 * P)}
CBW = P + E * P + 12 * P
WX = ["Wq_c", "Wk_s", "Wv_s", "Wq_s", "Wk_c", "Wv_c", "Wg_c", "Wg_s"]
SM = {"bq_c": 0, "bk_s": 1, "bv_s": 2, "bq_s": 3, "bk_c": 4, "bv_c": 5, "bg": 6, "q_norm": 7, "k_norm": 8,
      "router_scale": 9, "router_w": 10, "expert_scale": 18}
SMW = 26


def post_norm_decoder(nc, xT, x_tok, ctxT, w_qkv, w_out, w_x, small, gating, linear, const_f, const_b, out):
    ctx = ExitStack()

    def sb(name, shape, dt=F32):
        return ctx.enter_context(nc.sbuf_tensor(name, shape, dt))

    def sem(name):
        return ctx.enter_context(nc.semaphore(name))

    with ctx:
        xT_s = sb("xT_s", [P, N])
        x_s = sb("x_s", [P, NT, C])
        ctxT_s = sb("ctxT_s", [P, B * L])
        wqkv_s = sb("wqkv_s", [P, 5, P])
        wout_s = sb("wout_s", [P, P])
        wx_s = sb("wx_s", [P, 8, P])
        sm_s = sb("sm_s", [P, SMW])
        gat_hi = sb("gat_hi", [P, E, 2 * HT * P], F32R)
        gat_lo = sb("gat_lo", [P, E, 2 * HT * P], F32R)
        lin_s = sb("lin_s", [P, E, HT, P])
        cf = sb("cf", [P, CFW])
        cb = sb("cb", [P, CBW], BF16)
        eps_rms = sb("eps_rms", [P, 1])
        eps_ln = sb("eps_ln", [P, 1])
        warm = sb("warm", [P, 512], BF16)

        def constf(name):
            return cf[:, CF[name][0]:CF[name][1]]

        def constb(name, rows=P):
            return cb[0:rows, CB[name][0]:CB[name][1]]

        def wx(name):
            return wx_s[:, WX.index(name), :]

        def smcol(name, n=1):
            return sm_s[:, SM[name]:SM[name] + n]

        def diagonal(flat, at):
            return bass.AP(flat.tensor, flat.offset + at, [list(flat.ap[0]), [P + D, H // 2], [1, D]])

        ident = constf("ident")
        identb = constb("ident")
        sel_expert = constb("sel_expert", PIECES * E).rearrange("r (e m) -> r e m", e=E)
        sel_rows = constb("sel_rows").rearrange("r (o i n m) -> r o i n m", o=2, i=2, n=PIECES)

        arena = sb("arena", [P, 9 * N])
        at = [0]

        def later(n):
            at[0] += n
            assert at[0] <= 9 * N
            return arena[:, at[0] - n:at[0]]

        def early(i):
            return arena[:, i * 2 * N:(i + 1) * 2 * N].rearrange("p (i n) -> p i n", i=2)

        sq, rot, rot_s = (early(i) for i in range(3))
        lnms = rstd = sq
        rot_c, qkn = rot, rot_s
        res = sb("res", [P, 2, N])
        piece = sb("piece", [P, 2, PIECES, N], BF16)
        Q6 = sb("Q6", [P, H, N], BF16)
        K6 = sb("K6", [P, H // 2, N], BF16)
        VP = sb("VP", [P, NT, H, P])
        nmax = sb("nmax", [P, M, 2])
        probs = sb("probs", [P, 4, BLOCKS * P])
        probsT = sb("probsT", [P, 4, BLOCKS * P])
        attnT = sb("attnT", [P, N])
        qscale = sb("qscale", [P, 1])

        def after_heads(at, n):
            return Q6[:, :, :].rearrange("p h n -> p (h n)").bitcast(F32)[:, at:at + n]

        pre = sb("pre", [P, NT, C])
        stats = sb("stats", [P, 3, NT, 6])
        mv = sb("mv", [P, 3, NT, 2])
        rs_ln = sb("rs_ln", [P, 3, NT])
        x1 = sb("x1", [P, NT, C])
        x1T = sb("x1T", [P, N])
        x2 = sb("x2", [P, NT, C])
        x2T = sb("x2T", [P, N])
        y_s = x1
        lnsum = x2T[:, :].rearrange("p (b t) -> p b t", b=B)
        rsum = x2[:, :, :].rearrange("p (b t) c -> p b (t c)", b=B)

        KsT = sb("KsT", [P, B, L])
        QsT = sb("QsT", [P, B, L])
        Vs = sb("Vs", [P, B * L // P, C])
        QcT = sb("QcT", [P, N])
        KcT = sb("KcT", [P, N])
        Vc = sb("Vc", [P, NT, C])
        nm1 = sb("nm1", [P, NT])
        sum1 = sb("sum1", [P, NT])
        r1 = sb("r1", [P, NT])
        after = VP[:, :, :, :].rearrange("p (b t) h c -> p b (t h c)", b=B)
        P1 = after[:, :, 0:2 * L].rearrange("p b (t k) -> p b t k", t=2)
        P2 = after[:, :, 2 * L:4 * L].rearrange("p b (t k) -> p b t k", t=4)
        gd = after[:, :, 4 * L:4 * L + T]
        mixT = after[:, :, 4 * L + T:4 * L + 2 * T]
        PT1 = later(2048).rearrange("p (b k q) -> p b k q", b=B, k=4)
        nm2 = sb("nm2", [P, 8])
        sum2 = sb("sum2", [P, 8])
        r2 = sb("r2", [P, 8])
        pair_r = sb("pair_r", [P, 8, 64])
        PT2 = later(1024).rearrange("p (b k q) -> p b k q", b=B, k=2)
        c2s = later(N)
        s2c = later(N)
        diff = res[:, 0, :]
        hbg = sb("hbg", [P, 1])
        eg = res[:, 1, :]
        half_diff = later(N)

        rw = sb("rw", [P, E])
        nhalf = sb("nhalf", [P, 2])
        sd2 = sb("sd2", [P, NT])
        ms2 = sb("ms2", [P, NT])
        rr2 = sb("rr2", [P, NT])
        logit = sb("logit", [P, NT, E])
        nml = sb("nml", [P, NT])
        shift = sb("shift", [P, NT, E])
        ex = sb("ex", [P, NT, E])
        beats, ties = (after_heads(RING * T + i * NT * E * E, NT * E * E).rearrange("p (t i j) -> p t i j", t=NT, i=E)
                       for i in range(2))
        rank = sb("rank", [P, NT, E])
        lower = sb("lower", [P, E, E])
        gw = sb("gw", [P, NT, E])
        ren = sb("ren", [P, NT])
        renr = sb("renr", [P, NT])
        cw = sb("cw", [P, NT, E])
        comb = sb("comb", [P, NT, E])
        combr = sb("combr", [P, NT, E])
        combp = sb("combp", [P, NT, PIECES, E], BF16)
        combT = sb("combT", [PIECES * E, N], BF16)
        x2_hi, x2_lo = (sb(n, [P, B, T], F32R) for n in ("x2_hi", "x2_lo"))
        x2c = after_heads(0, RING * T).rearrange("p (i n) -> p i n", i=RING)
        x2c_hi, x2c_lo = (sb(n, [P, RING, T], F32R) for n in ("x2c_hi", "x2c_lo"))
        gl, acts = (x[:, :, :].rearrange("p i n -> p (i n)")[:, 0:4 * T].rearrange("p (i n) -> p i n", i=4)
                    for x in (probs, probsT))
        raw = piece[:, :, :, :].rearrange("p i n t -> p (i n t)").bitcast(F32).rearrange("p (i n) -> p i n", i=3)

        psum = ctx.enter_context(nc.psum_tensor("psum", [P, 8, 512], F32))
        banks = [psum[:, i, :] for i in range(8)]
        XBANKS = ((6, 0, 1), (7, 2, 3))
        FBANKS = (4, 5, 0)
        SPREAD, DOWN = 6, (1, 2)

        PROJ = ((0, 2), (1, 5))
        MEAN = ((4, 4), (7, 4))

        def bk(b, i):
            return banks[XBANKS[b]["ABC".index(i)]]

        def score_bank(m):
            return banks[m % 3 if m < H else 2 + m % 2]

        def trans_bank(m):
            return banks[4 + m % 2]

        qs = nc.dram_tensor("q_pieces", [H, PIECES, D, N], BF16).ap()
        ks = nc.dram_tensor("k_rows", [H, len(K_PIECE), D, N], BF16).ap()

        names = """in_x in_wqkv in_small in_cf in_cb in_ctx in_wx in_xtok in_wout in_lin
            zeroed_q zeroed_k zeroed_v consts eps
            proj vproj sq_done ms_done rs_done rot_done qkn_done p0 p1 p2q p2k r1q r1k rows_mm q_rows k_rows vp_done
            ctx_mm kv_ev q_ev s_done max_done exp_done t_mm t_done_v t_done_a pv_done rsum_done attn_done
            wout_done xn_done x2n_done xt_mm xt_done x2t_mm x2t_done
            qkc_mm qkc_done vc_mm vc_done s1_mm nm1_done exp1_done p1n_done pt1_mm pt1_done
            s2_mm nm2_done exp2_done pair_done pt2_mm pt2_done c2s_mm s2c_mm c2s_done s2c_done gate_mm eg_done mix_done
            mix_mm rw_done rr2_done logit_mm logit_done ex_done comb_done combT_mm combT_done bc_mm x2c_done
            x2_hi_done x2_lo_done x2c_hi_done x2c_lo_done w_split warm_ready
            gates_mm gl_done act_done out_mm y_ready stored chain_v chain_a chain_p""".split()
        S = {n: sem(n) for n in names}
        q_saved, k_saved, q6_in, k6_in = ([sem(n + "_%d" % b) for b in range(B)] for n in ("q_saved", "k_saved", "q6_in", "k6_in"))
        in_gat = [sem("in_gat%d" % i) for i in range(3)]
        mv_done = [sem("mv_done%d" % i) for i in range(3)]
        rsln_done = [sem("rsln_done%d" % i) for i in range(3)]
        SCALE = float(D) ** -0.5
        XSCALE = float(C) ** -0.5

        def transposed(m):
            return (S["t_done_a"], m // 4 + 1) if m % 4 == 3 else (S["t_done_v"], m - m // 4 + 1)

        block = ctx.enter_context(nc.Block())

        @block.sync
        def _(sp):
            sp.dma_start(xT_s[:, :], xT).then_inc(S["in_x"], 16)
            sp.dma_start(cf[:, :], const_f).then_inc(S["in_cf"], 16)
            sp.dma_start(ctxT_s[:, :], ctxT).then_inc(S["in_ctx"], 16)
            sp.dma_start(cb[:, :].bitcast(U16), const_b).then_inc(S["in_cb"], 16)
            q_rows = [(0, 3), (3, 2), (5, 1)]
            for b in range(B):
                c = slice(b * T, (b + 1) * T)
                p0 = (NR, 0)[b]
                for n in range(PIECES):
                    if n < 2:
                        sp.wait_ge(S[("p0", "p1")[n]], 2 * b + 2)
                    else:
                        sp.wait_ge(S["p2q"], b + 1)
                        sp.wait_ge(S["p2k"], b + 1)
                    sp.dma_start(qs[2 * p0:, n, :, c], piece[16 * p0:, 0, n, c]).then_inc(q_saved[b], 16)
                    for row, p in enumerate(K_PIECE):
                        if p == n:
                            sp.dma_start(ks[2 * p0:, row, :, c], piece[16 * p0:, 1, n, c]).then_inc(k_saved[b], 16)
                sp.wait_ge(q_saved[b], 3 * 16)
                sp.wait_ge(S["zeroed_q"], 1)
                for odd in range(2):
                    src = qs.rearrange("(p o) n d t -> o (n d) p t", o=2)[odd]
                    for at, n in q_rows:
                        r0 = 64 * odd + at * D
                        sp.dma_start(Q6[r0:r0 + n * D, 2 * p0 + odd:H:2, c], src[0:n * D, p0:, c]).then_inc(q6_in[b], 16)
                sp.wait_ge(k_saved[b], len(K_PIECE) * 16)
                sp.wait_ge(S["zeroed_k"], 1)
                for odd in range(2):
                    src = ks.rearrange("(p o) n d t -> o (n d) p t", o=2)[odd]
                    sp.dma_start(K6[64 * odd:64 * odd + len(K_PIECE) * D, p0:, c], src[:, p0:, c]).then_inc(k6_in[b], 16)
            sp.dma_start(x_s[:, :, :], x_tok).then_inc(S["in_xtok"], 16)
            sp.dma_start(wout_s[:, :], w_out).then_inc(S["in_wout"], 16)
            sp.dma_start(lin_s[:, :, :, :], linear).then_inc(S["in_lin"], 16)
            sp.wait_ge(S["rows_mm"], NR)
            for e in range(E):
                if e >= 3:
                    sp.wait_ge(S["w_split"], e - 2)
                sp.dma_start(raw[:, e % 3, :], gating[:, e].rearrange("p i h c -> p (i h c)")).then_inc(in_gat[e % 3], 16)
            for b in range(B):
                sp.wait_ge(S["y_ready"], 2 * (b + 1))
                sp.dma_start(out[:, 2 * b:2 * b + 2, :], y_s[:, 2 * b:2 * b + 2, :]).then_inc(S["stored"], 16)
            sp.wait_ge(S["stored"], 16 * B)

        @block.gpsimd
        def _(pool):
            chain = [0]

            def link(ins):
                chain[0] += 1
                ins.then_inc(S["chain_p"], 1)
                pool.wait_ge(S["chain_p"], chain[0])

            nc.gpsimd.memset(eps_rms[:, :], 1e-6)
            nc.gpsimd.memset(nhalf[:, :], -0.5)
            nc.gpsimd.memset(eps_ln[:, :], 1e-5).then_inc(S["eps"], 1)
            nc.gpsimd.memset(K6[:, :, :].bitcast(U32), 0).then_inc(S["zeroed_k"], 1)
            nc.gpsimd.memset(VP[:, 0:2, :, :], 0.0)
            link(nc.gpsimd.memset(VP[:, 2:4, :, :], 0.0))
            for half in range(2):
                for t in range(NT):
                    ones = VP[:, t, half * (H // 2):(half + 1) * (H // 2), :].rearrange("p h c -> p (h c)")
                    last = nc.gpsimd.memset(diagonal(ones, 64 * (1 - half)), 1.0)
            last.then_inc(S["zeroed_v"], 1)
            link(nc.gpsimd.memset(lower[:, :, :], 0.0))
            nc.gpsimd.affine_select(out=lower[:, :, :], in_=lower[:, :, :], compare_op=ALU.is_ge, fill=1.0, base=0,
                                    pattern=[[-1, E], [1, E]], channel_multiplier=0).then_inc(S["consts"], 1)
            for b in range(B):
                c = slice(b * T, (b + 1) * T)
                pool.wait_ge(S["p0"], 2 * b + 2)
                nc.gpsimd.tensor_tensor(res[:, 1, c], qkn[:, 1, c], piece[:, 1, 0, c], ALU.subtract).then_inc(S["r1k"], 1)
                pool.wait_ge(S["p1"], 2 * b + 2)
                pool.wait_ge(S["r1k"], b + 1)
                nc.gpsimd.tensor_tensor(piece[:, 1, 2, c], res[:, 1, c], piece[:, 1, 1, c], ALU.subtract).then_inc(S["p2k"], 1)

            def rs_norm(i, b):
                t2 = slice(2 * b, 2 * b + 2)
                pool.wait_ge(mv_done[i], b + 1)
                link(nc.gpsimd.tensor_scalar(sd2[:, t2], mv[:, i, t2, 1], 1e-5, None, ALU.add))
                nc.gpsimd.tensor_tensor(rs_ln[:, i, t2], sd2[:, t2], nhalf[:, :], ALU.pow).then_inc(rsln_done[i], 1)

            def split_weights(e):
                pool.wait_ge(in_gat[e % 3], 16 * (e // 3 + 1))
                link(nc.gpsimd.tensor_copy(gat_hi[:, e, :], raw[:, e % 3, :]))
                nc.gpsimd.tensor_tensor(gat_lo[:, e, :], raw[:, e % 3, :], gat_hi[:, e, :].bitcast(F32), ALU.subtract).then_inc(S["w_split"], 1)

            def rms2(b):
                t2 = slice(2 * b, 2 * b + 2)
                pool.wait_ge(rsln_done[1], b + 1)
                link(nc.gpsimd.tensor_tensor(sd2[:, t2], mv[:, 1, t2, 1], rs_ln[:, 1, t2], ALU.mult))
                link(nc.gpsimd.tensor_tensor(ms2[:, t2], sd2[:, t2], rs_ln[:, 1, t2], ALU.mult))
                link(nc.gpsimd.tensor_scalar(ms2[:, t2], ms2[:, t2], 1e-6, None, ALU.add))
                nc.gpsimd.tensor_tensor(rr2[:, t2], ms2[:, t2], nhalf[:, :], ALU.pow).then_inc(S["rr2_done"], 1)

            for m in range(0, 2):
                split_weights(m)
            rs_norm(0, 0)
            for m in range(2, 8):
                split_weights(m)
            rs_norm(0, 1)
            rs_norm(1, 0)
            rms2(0)
            rs_norm(1, 1)
            rms2(1)
            rs_norm(2, 0)
            rs_norm(2, 1)

        @block.scalar
        def _(act):
            chain = [0]

            def link(ins):
                chain[0] += 1
                ins.then_inc(S["chain_a"], 1)
                act.wait_ge(S["chain_a"], chain[0])

            A = nc.scalar.activation
            table = nc.scalar.preload_act_table_set
            exp_set, tanh_set, gelu_set = "natural_log_exp_and_others", "exp_and_others", "gelu_apprx_tanh_and_others"
            table(exp_set)
            act.dma_start(wqkv_s[:, :, :], w_qkv).then_inc(S["in_wqkv"], 16)
            act.dma_start(sm_s[:, :], small).then_inc(S["in_small"], 16)
            act.dma_start(wx_s[:, :, :], w_x).then_inc(S["in_wx"], 16)
            act.wait_ge(S["eps"], 1)

            def square(i, b):
                act.wait_ge(S["proj"], 2 * b + i + 1)
                A(sq[:, i, b * T:(b + 1) * T], banks[PROJ[i][b]][:, 0:T], ACT.Square).then_inc(S["sq_done"], 1)

            def rstd_of(i, b):
                c = slice(b * T, (b + 1) * T)
                act.wait_ge(S["ms_done"], 2 * b + i + 1)
                link(A(lnms[:, i, c], banks[MEAN[i][b]][:, 0:T], ACT.Ln, bias=eps_rms[:, :]))
                A(rstd[:, i, c], lnms[:, i, c], ACT.Exp, scale=-0.5).then_inc(S["rs_done"], 1)

            def piece0(i, b):
                c = slice(b * T, (b + 1) * T)
                act.wait_ge(S["qkn_done"], 2 * b + i + 1)
                A(piece[:, i, 0, c], qkn[:, i, c], ACT.Copy).then_inc(S["p0"], 1)

            def piece1(i, b):
                c = slice(b * T, (b + 1) * T)
                act.wait_ge(S[("r1q", "r1k")[i]], b + 1)
                A(piece[:, i, 1, c], res[:, i, c], ACT.Copy).then_inc(S["p1"], 1)

            def ctx_k_out(b):
                act.wait_ge(S["ctx_mm"], 3 * b + 1)
                A(KsT[:, b, :], bk(b, "C"), ACT.Identity, bias=smcol("bk_s")).then_inc(S["kv_ev"], 1)

            def ctx_v_out(b):
                act.wait_ge(S["ctx_mm"], 3 * b + 3)
                A(Vs[:, 4 * b:4 * b + 4, :], bk(b, "C").rearrange("p (t c) -> p t c", t=4), ACT.Copy).then_inc(S["kv_ev"], 1)

            def rows_out(p):
                act.wait_ge(S["rows_mm"], p + 1)
                act.wait_ge(S["zeroed_q"], 1)
                A(Q6[0:64, 2 * p, 0:T], banks[7][0:64, 0:T], ACT.Copy)
                A(Q6[64:128, 2 * p + 1, 0:T], banks[7][64:128, 0:T], ACT.Copy).then_inc(S["q_rows"], 1)

            def exps(m):
                act.wait_ge(S["max_done"], m + 1)
                for t, cols in enumerate((slice(0, P), slice(P, 3 * P))):
                    p = probs[:, m % 4, cols]
                    ins = A(p, p, ACT.Exp, scale=-1.0, bias=nmax[:, m, t:t + 1])
                ins.then_inc(S["exp_done"], 1)

            def trans_out(m):
                act.wait_ge(S["t_mm"], m + 1)
                if m >= 4:
                    act.wait_ge(S["pv_done"], m - 3)
                A(probsT[:, m % 4, :], trans_bank(m)[:, 0:BLOCKS * P], ACT.Copy).then_inc(S["t_done_a"], 1)

            def heads(first, last):
                for m in range(first, last):
                    if m < 2 * NR - 2 and m % 2 == 0:
                        rows_out(m // 2 + 1)
                    if m >= 2 and (m - 2) % 4 == 3:
                        trans_out(m - 2)
                    exps(m)

            def sums(b):
                act.wait_ge(S["pv_done"], H * (b + 1))
                A(lnsum[0:64, b, :], banks[6 + b][64:128, 0:T], ACT.Ln)
                link(A(lnsum[64:128, b, :], banks[6 + b][0:64, T:2 * T], ACT.Ln))
                A(rsum[:, b, :], lnsum[:, b, :], ACT.Exp, scale=-1.0).then_inc(S["rsum_done"], 1)

            def v_out(b):
                act.wait_ge(S["vc_mm"], b + 1)
                A(Vc[:, 2 * b:2 * b + 2, :], bk(b, "B")[:, 0:T].rearrange("p (t c) -> p t c", t=2), ACT.Copy).then_inc(S["vc_done"], 1)

            def exp1(t):
                b = t // 2
                act.wait_ge(S["nm1_done"], t + 1)
                act.wait_ge(S["pv_done"], H * (b + 1))
                A(P1[:, b, t % 2, :], bk(b, "CB"[t % 2]), ACT.Exp, bias=nm1[:, t:t + 1], accum_out=sum1[:, t:t + 1]).then_inc(S["exp1_done"], 1)

            def exp2(h):
                b = h // 2
                act.wait_ge(S["nm2_done"], h + 1)
                act.wait_ge(S["pv_done"], H * (b + 1))
                for s in (2 * (h % 2), 2 * (h % 2) + 1):
                    t = 4 * b + s
                    A(P2[:, b, s, :], bk(b, "AC"[h % 2])[:, (s % 2) * T:(s % 2 + 1) * T], ACT.Exp, bias=nm2[:, t:t + 1],
                      accum_out=sum2[:, t:t + 1]).then_inc(S["exp2_done"], 1)

            def pt1_out(t):
                b = t // 2
                act.wait_ge(S["pt1_mm"], t + 1)
                A(PT1[:, b, :, (t % 2) * P:(t % 2 + 1) * P], bk(b, "BA"[t % 2]).rearrange("p (k q) -> p k q", k=4),
                  ACT.Copy).then_inc(S["pt1_done"], 1)

            def gate_of(b):
                act.wait_ge(S["gate_mm"], b + 1)
                A(eg[:, b * T:(b + 1) * T], bk(b, "C")[:, 0:T], ACT.Tanh, scale=0.5, bias=hbg[:, :]).then_inc(S["eg_done"], 1)

            def c2s_out(b):
                act.wait_ge(S["c2s_mm"], b + 1)
                A(c2s[:, b * T:(b + 1) * T], bk(b, "B")[:, 0:T], ACT.Identity, bias=smcol("bv_s")).then_inc(S["c2s_done"], 1)

            def route(b):
                act.wait_ge(S["logit_done"], b + 1)
                act.wait_ge(S["rr2_done"], b + 1)
                for t in (2 * b, 2 * b + 1):
                    A(ex[:, t, :], shift[:, t, :], ACT.Exp, scale=rr2[:, t:t + 1]).then_inc(S["ex_done"], 1)

            def x2_hi_of(b):
                act.wait_ge(S["x2t_done"], b + 1)
                A(x2_hi[:, b, :], x2T[:, b * T:(b + 1) * T], ACT.Copy).then_inc(S["x2_hi_done"], 1)

            def x2c_hi_of(m):
                act.wait_ge(S["x2c_done"], m + 1)
                if m >= RING:
                    act.wait_ge(S["gates_mm"], HT * (m - RING + 1))
                A(x2c_hi[:, m % RING, :], x2c[:, m % RING, :], ACT.Copy).then_inc(S["x2c_hi_done"], 1)

            def gelu(n):
                act.wait_ge(S["gates_mm"], n + 1)
                if n >= 4:
                    act.wait_ge(S["act_done"], n - 3)
                A(gl[:, n % 4, :], banks[FBANKS[n % 3]][:, 0:T], ACT.Gelu_apprx_tanh).then_inc(S["gl_done"], 1)

            square(0, 0)
            square(1, 0)
            rstd_of(0, 0)
            rstd_of(1, 0)
            piece0(0, 0)
            piece0(1, 0)
            square(0, 1)
            piece1(0, 0)
            square(1, 1)
            piece1(1, 0)
            rstd_of(0, 1)
            rstd_of(1, 1)
            rows_out(0)
            heads(0, 2)
            piece0(0, 1)
            piece0(1, 1)
            heads(2, 4)
            piece1(0, 1)
            piece1(1, 1)
            heads(4, H)
            exps(16)
            exps(17)
            trans_out(15)
            exps(18)
            exps(19)
            ctx_k_out(0)
            sums(0)
            exps(20)
            ctx_v_out(0)
            trans_out(19)
            for m in range(21, 25):
                exps(m)
            trans_out(23)
            for m in range(25, 28):
                exps(m)
            v_out(0)
            for m in range(28, 31):
                exps(m)
            exp1(0)
            exp2(0)
            trans_out(27)
            exps(31)
            exp1(1)
            exp2(1)
            ctx_k_out(1)
            pt1_out(0)
            trans_out(31)
            pt1_out(1)
            sums(1)
            c2s_out(0)
            ctx_v_out(1)
            table(tanh_set)
            gate_of(0)
            v_out(1)
            exp2(2)
            exp1(2)
            exp1(3)
            x2_hi_of(0)
            pt1_out(2)
            exp2(3)
            pt1_out(3)
            route(0)
            c2s_out(1)
            x2c_hi_of(0)
            gate_of(1)
            x2c_hi_of(1)
            table(gelu_set)
            gelu(0)
            x2c_hi_of(2)
            gelu(1)
            gelu(2)
            x2c_hi_of(3)
            gelu(3)
            x2c_hi_of(4)
            gelu(4)
            gelu(5)
            x2c_hi_of(5)
            gelu(6)
            gelu(7)
            x2_hi_of(1)
            x2c_hi_of(6)
            for n in range(8, 11):
                gelu(n)
            table(tanh_set)
            route(1)
            x2c_hi_of(7)
            table(gelu_set)
            for n in range(11, 14):
                gelu(n)
            x2c_hi_of(8)
            gelu(14)
            gelu(15)
            x2c_hi_of(9)
            gelu(16)
            x2c_hi_of(10)
            for n in range(17, 20):
                gelu(n)
            for n in range(20, B * E * HT):
                if n % HT == 0 and n // HT + 1 < B * E:
                    x2c_hi_of(n // HT + 1)
                gelu(n)

        @block.vector
        def _(dve):
            chain = [0]

            def link(ins):
                chain[0] += 1
                ins.then_inc(S["chain_v"], 1)
                dve.wait_ge(S["chain_v"], chain[0])

            V = nc.vector
            mask = constf("mask")
            V.memset(warm[:, :], 0.0).then_inc(S["warm_ready"], 1)
            V.memset(Q6[:, :, :].bitcast(U32), 0).then_inc(S["zeroed_q"], 1)
            dve.wait_ge(S["in_small"], 16)
            V.tensor_scalar(hbg[:, :], smcol("bg"), 0.5, None, ALU.mult)
            link(V.tensor_scalar(qscale[:, :], smcol("q_norm"), -SCALE, None, ALU.mult))
            V.tensor_scalar(rw[:, :], smcol("router_w", E), smcol("router_scale"), XSCALE, ALU.mult, ALU.mult).then_inc(S["rw_done"], 1)
            dve.wait_ge(S["in_cf"], 16)

            def rotate(i, b):
                c = slice(b * T, (b + 1) * T)
                dve.wait_ge(S["proj"], 2 * b + i + 1)
                dve.wait_ge(S["sq_done"], 2 * b + i + 1)
                own = banks[PROJ[i][b]]
                V.tensor_tensor(rot_s[:, i, c], own[:, T:2 * T], constf("sin"), ALU.mult)
                link(V.tensor_tensor(rot_c[:, i, c], own[:, 0:T], constf("cos"), ALU.mult))
                V.tensor_tensor(rot[:, i, c], rot_c[:, i, c], rot_s[:, i, c], ALU.add).then_inc(S["rot_done"], 1)

            def normalise(i, b):
                c = slice(b * T, (b + 1) * T)
                dve.wait_ge(S["rs_done"], 2 * b + i + 1)
                dve.wait_ge(S["rot_done"], 2 * b + i + 1)
                V.scalar_tensor_tensor(out=qkn[:, i, c], in0=rot[:, i, c], scalar=(qscale[:, :], smcol("k_norm"))[i],
                                       in1=rstd[:, i, c], op0=ALU.mult, op1=ALU.mult).then_inc(S["qkn_done"], 1)

            def rest1(b):
                c = slice(b * T, (b + 1) * T)
                dve.wait_ge(S["p0"], 2 * b + 1)
                V.tensor_tensor(res[:, 0, c], qkn[:, 0, c], piece[:, 0, 0, c], ALU.subtract).then_inc(S["r1q"], 1)

            def piece2(b):
                c = slice(b * T, (b + 1) * T)
                dve.wait_ge(S["p1"], 2 * b + 1)
                dve.wait_ge(S["r1q"], b + 1)
                V.tensor_tensor(piece[:, 0, 2, c], res[:, 0, c], piece[:, 0, 1, c], ALU.subtract).then_inc(S["p2q"], 1)

            def v_in(b):
                dve.wait_ge(S["vproj"], 1)
                dve.wait_ge(S["zeroed_v"], 1)
                for half in range(2):
                    for t in (2 * b, 2 * b + 1):
                        own = VP[:, t, half * (H // 2):(half + 1) * (H // 2), :].rearrange("p h c -> p (h c)")
                        src = banks[6][:, t * P + half * 64:t * P + half * 64 + 64].rearrange("p (h d) -> p h d", d=D)
                        ins = V.tensor_copy(diagonal(own, 64 * half), src)
                ins.then_inc(S["vp_done"], 1)

            def ctx_q_out(b):
                dve.wait_ge(S["ctx_mm"], 3 * b + 2)
                V.tensor_scalar(QsT[:, b, :], bk(b, "B"), smcol("bq_s"), XSCALE, ALU.add, ALU.mult).then_inc(S["q_ev"], 1)

            def rows_out(p):
                dve.wait_ge(S["rows_mm"], p + 1)
                dve.wait_ge(S["zeroed_k"], 1)
                V.tensor_copy(K6[:, p, 0:T], banks[3][:, 0:T]).then_inc(S["k_rows"], 1)

            def maxes(m):
                dve.wait_ge(S["s_done"], m + 1)
                if m >= 4:
                    dve.wait_ge(S["t_mm"], m - 3)
                for t, cols in enumerate((slice(0, P), slice(P, 3 * P))):
                    ins = V.tensor_tensor_reduce(out=probs[:, m % 4, cols], in0=mask[:, P * (1 - t):], in1=score_bank(m)[:, cols],
                                                 scale=1.0, scalar=FORBIDDEN, op0=ALU.add, op1=ALU.min,
                                                 accum_out=nmax[:, m, t:t + 1])
                ins.then_inc(S["max_done"], 1)

            def trans_out(m):
                dve.wait_ge(S["t_mm"], m + 1)
                if m >= 4:
                    dve.wait_ge(S["pv_done"], m - 3)
                V.tensor_copy(probsT[:, m % 4, :], trans_bank(m)[:, 0:BLOCKS * P]).then_inc(S["t_done_v"], 1)

            def heads(first, last):
                for m in range(first, last):
                    if m < 2 * NR - 2 and m % 2 == 0:
                        rows_out(m // 2 + 1)
                    if m < M:
                        maxes(m)
                    if m >= 2 and (m - 2) % 4 != 3:
                        trans_out(m - 2)

            def attn_norm(b):
                dve.wait_ge(S["rsum_done"], b + 1)
                c = slice(b * T, (b + 1) * T)
                V.tensor_tensor(attnT[0:64, c], banks[6 + b][0:64, 0:T], rsum[0:64, b, :], ALU.mult)
                V.tensor_tensor(attnT[64:128, c], banks[6 + b][64:128, T:2 * T], rsum[64:128, b, :], ALU.mult).then_inc(S["attn_done"], 1)

            def norm_in(i, b, psum, other, mm, count):
                t2 = slice(2 * b, 2 * b + 2)
                dve.wait_ge(S[mm], count)
                link(V.tensor_tensor(pre[:, t2, :], psum, other[:, t2, :], ALU.add))
                for t in (2 * b, 2 * b + 1):
                    ins = V.bn_stats(stats[:, i, t, :], pre[:, t, :])
                link(ins)
                for t in (2 * b, 2 * b + 1):
                    ins = V.bn_aggr(mv[:, i, t, :], stats[:, i, t, :])
                ins.then_inc(mv_done[i], 1)

            def norm_out(i, b, dst, done):
                dve.wait_ge(rsln_done[i], b + 1)
                dve.wait_ge(mv_done[i], b + 1)
                for t in (2 * b, 2 * b + 1):
                    V.tensor_scalar(dst[:, t, :], pre[:, t, :], mv[:, i, t, 0:1], rs_ln[:, i, t:t + 1],
                                    ALU.subtract, ALU.mult).then_inc(S[done], 1)

            def xT_out(i, b):
                dst = (x1T, x2T)[i]
                dve.wait_ge(S[("xt_mm", "x2t_mm")[i]], b + 1)
                V.tensor_copy(dst[:, b * T:(b + 1) * T], bk(b, "A")[:, 0:T]).then_inc(S[("xt_done", "x2t_done")[i]], 1)

            def qk_out(b):
                dve.wait_ge(S["qkc_mm"], b + 1)
                c = slice(b * T, (b + 1) * T)
                V.tensor_scalar(QcT[:, c], bk(b, "A")[:, 0:T], smcol("bq_c"), XSCALE, ALU.add, ALU.mult)
                V.tensor_scalar(KcT[:, c], bk(b, "A")[:, T:2 * T], smcol("bk_c"), None, ALU.add).then_inc(S["qkc_done"], 1)

            def max1(t):
                dve.wait_ge(S["s1_mm"], t + 1)
                V.tensor_reduce(nm1[:, t:t + 1], bk(t // 2, "CB"[t % 2]), AX.X, ALU.max, negate=True).then_inc(S["nm1_done"], 1)

            def max2(h):
                b = h // 2
                dve.wait_ge(S["s2_mm"], h + 1)
                V.tensor_reduce(nm2[:, 2 * h:2 * h + 2], bk(b, "AC"[h % 2]).rearrange("p (h k) -> p h k", h=2),
                                AX.X, ALU.max, negate=True).then_inc(S["nm2_done"], 1)

            def p1_norm(t):
                dve.wait_ge(S["exp1_done"], t + 1)
                link(V.reciprocal(r1[:, t:t + 1], sum1[:, t:t + 1]))
                p = P1[:, t // 2, t % 2, :]
                V.tensor_scalar(p, p, r1[:, t:t + 1], None, ALU.mult).then_inc(S["p1n_done"], 1)

            def pairs(b):
                dve.wait_ge(S["exp2_done"], 4 * (b + 1))
                link(V.reciprocal(r2[:, 4 * b:4 * b + 4], sum2[:, 4 * b:4 * b + 4]))
                for s in range(4):
                    t = 4 * b + s
                    ins = V.tensor_scalar(pair_r[:, t, :], constf("pair"), r2[:, t:t + 1], None, ALU.mult)
                ins.then_inc(S["pair_done"], 1)

            def pt2_out(b):
                dve.wait_ge(S["pt2_mm"], b + 1)
                V.tensor_copy(PT2[:, b, :, :], bk(b, "C").rearrange("p (k q) -> p k q", k=2)).then_inc(S["pt2_done"], 1)

            def s2c_out(b):
                c = slice(b * T, (b + 1) * T)
                dve.wait_ge(S["s2c_mm"], b + 1)
                V.tensor_scalar(s2c[:, c], bk(b, "A")[:, 0:T], smcol("bv_c"), None, ALU.add).then_inc(S["s2c_done"], 1)
                dve.wait_ge(S["s2c_done"], b + 1)
                dve.wait_ge(S["c2s_done"], b + 1)
                link(V.tensor_tensor(diff[:, c], c2s[:, c], s2c[:, c], ALU.subtract))

            def mix(b):
                c = slice(b * T, (b + 1) * T)
                link(V.tensor_scalar(half_diff[:, c], diff[:, c], 0.5, None, ALU.mult))
                dve.wait_ge(S["eg_done"], b + 1)
                link(V.scalar_tensor_tensor(out=gd[:, b, :], in0=eg[:, c], scalar=1.0, in1=half_diff[:, c], op0=ALU.add, op1=ALU.mult))
                V.tensor_tensor(mixT[:, b, :], gd[:, b, :], s2c[:, c], ALU.add).then_inc(S["mix_done"], 1)

            def logits(b):
                t2 = slice(2 * b, 2 * b + 2)
                dve.wait_ge(S["consts"], 1)
                dve.wait_ge(S["logit_mm"], b + 1)
                link(V.tensor_copy(logit[:, t2, :], bk(b, "C")[:, 0:2 * E].rearrange("p (t e) -> p t e", t=2)))
                link(V.tensor_reduce(nml[:, t2], logit[:, t2, :], AX.X, ALU.max, negate=True))
                for t in (2 * b, 2 * b + 1):
                    ins = V.tensor_scalar(shift[:, t, :], logit[:, t, :], nml[:, t:t + 1], None, ALU.add)
                ins.then_inc(S["logit_done"], 1)
                for t in (2 * b, 2 * b + 1):
                    other = logit[:, t, :].rearrange("p (o e) -> p o e", o=1).broadcast_to([P, E, E])
                    own = logit[:, t, :].rearrange("p (e o) -> p e o", o=1).broadcast_to([P, E, E])
                    V.tensor_tensor(beats[:, t, :, :], other, own, ALU.is_gt)
                    ins = V.tensor_tensor(ties[:, t, :, :], other, own, ALU.is_equal)
                link(ins)
                for t in (2 * b, 2 * b + 1):
                    ins = V.tensor_tensor(ties[:, t, :, :], ties[:, t, :, :], lower[:, :, :], ALU.mult)
                link(ins)
                link(V.tensor_tensor(beats[:, t2, :, :], beats[:, t2, :, :], ties[:, t2, :, :], ALU.add))
                link(V.tensor_reduce(rank[:, t2, :], beats[:, t2, :, :], AX.X, ALU.add))

            def combine(b):
                t2 = slice(2 * b, 2 * b + 2)

                def wide(ap):
                    return ap.rearrange("p (t o) -> p t o", o=1).broadcast_to([P, 2, E])

                dve.wait_ge(S["ex_done"], 2 * (b + 1))
                link(V.scalar_tensor_tensor(out=gw[:, t2, :], in0=rank[:, t2, :], scalar=1.5, in1=ex[:, t2, :],
                                            op0=ALU.is_lt, op1=ALU.mult))
                es = smcol("expert_scale", E).rearrange("p (o e) -> p o e", o=1).broadcast_to([P, 2, E])
                V.tensor_tensor(cw[:, t2, :], gw[:, t2, :], es, ALU.mult)
                link(V.tensor_reduce(ren[:, t2], gw[:, t2, :], AX.X, ALU.add))
                link(V.reciprocal(renr[:, t2], ren[:, t2]))
                link(V.tensor_tensor(comb[:, t2, :], cw[:, t2, :], wide(renr[:, t2]), ALU.mult))
                link(V.tensor_copy(combp[:, t2, 0, :], comb[:, t2, :]))
                link(V.tensor_tensor(combr[:, t2, :], comb[:, t2, :], combp[:, t2, 0, :], ALU.subtract))
                link(V.tensor_copy(combp[:, t2, 1, :], combr[:, t2, :]))
                V.tensor_tensor(combp[:, t2, 2, :], combr[:, t2, :], combp[:, t2, 1, :], ALU.subtract).then_inc(S["comb_done"], 1)

            def combT_out(b):
                dve.wait_ge(S["combT_mm"], b + 1)
                V.tensor_copy(combT[:, b * T:(b + 1) * T], bk(b, "B").bitcast(BF16)[0:PIECES * E, 0:T]).then_inc(S["combT_done"], 1)

            pairview = lambda ap: ap[:, 0:T].rearrange("p (t c) -> p t c", t=2)

            def norm1_in(b):
                dve.wait_ge(S["in_xtok"], 16)
                norm_in(0, b, pairview(bk(b, "A")), x_s, "wout_done", b + 1)

            def norm2_in(b):
                norm_in(1, b, pairview(bk(b, "B")), x1, "mix_mm", b + 1)

            def norm3_in(b):
                norm_in(2, b, pairview(banks[DOWN[b]]), x2, "out_mm", E * HT * (b + 1))

            def scaled(m):
                b, e = m // E, m % E
                dve.wait_ge(S["bc_mm"], m + 1)
                dve.wait_ge(S["x2t_done"], b + 1)
                if m >= RING:
                    dve.wait_ge(S["x2c_lo_done"], m - RING + 1)
                V.tensor_tensor(x2c[:, m % RING, :], x2T[:, b * T:(b + 1) * T], banks[SPREAD][:, 0:T], ALU.mult).then_inc(S["x2c_done"], 1)

            def x2_lo_of(b):
                dve.wait_ge(S["x2_hi_done"], b + 1)
                V.tensor_tensor(x2_lo[:, b, :], x2T[:, b * T:(b + 1) * T], x2_hi[:, b, :].bitcast(F32),
                                ALU.subtract).then_inc(S["x2_lo_done"], 1)

            def x2c_lo_of(m):
                dve.wait_ge(S["x2c_hi_done"], m + 1)
                if m >= RING:
                    dve.wait_ge(S["gates_mm"], HT * (m - RING + 1))
                V.tensor_tensor(x2c_lo[:, m % RING, :], x2c[:, m % RING, :], x2c_hi[:, m % RING, :].bitcast(F32),
                                ALU.subtract).then_inc(S["x2c_lo_done"], 1)

            def acts_of(n):
                dve.wait_ge(S["gl_done"], n + 1)
                if n >= 4:
                    dve.wait_ge(S["out_mm"], n - 3)
                V.tensor_tensor(acts[:, n % 4, :], banks[FBANKS[n % 3]][:, T:2 * T], gl[:, n % 4, :], ALU.mult).then_inc(S["act_done"], 1)

            def x1_out(b):
                norm_out(0, b, x1, "xn_done")

            def x2_out(b):
                norm_out(1, b, x2, "x2n_done")

            def ffn(first, last):
                for n in range(first, last):
                    acts_of(n)
                    if n % HT == 1 and n // HT + 2 < B * E:
                        scaled(n // HT + 2)
                    if n % HT == 0 and n // HT + 1 < B * E:
                        x2c_lo_of(n // HT + 1)

            def y_out(b):
                norm_out(2, b, y_s, "y_ready")

            rotate(0, 0)
            rotate(1, 0)
            normalise(0, 0)
            normalise(1, 0)
            rest1(0)
            rotate(0, 1)
            piece2(0)
            rotate(1, 1)
            rows_out(0)
            v_in(0)
            heads(0, 1)
            v_in(1)
            heads(1, 2)
            normalise(0, 1)
            normalise(1, 1)
            heads(2, 3)
            rest1(1)
            heads(3, 5)
            piece2(1)
            heads(5, H)
            maxes(16)
            maxes(17)
            trans_out(14)
            maxes(18)
            maxes(19)
            trans_out(16)
            trans_out(17)
            maxes(20)
            ctx_q_out(0)
            attn_norm(0)
            trans_out(18)
            maxes(21)
            norm1_in(0)
            maxes(22)
            maxes(23)
            trans_out(20)
            trans_out(21)
            maxes(24)
            trans_out(22)
            x1_out(0)
            for m in range(25, 28):
                maxes(m)
            xT_out(0, 0)
            trans_out(24)
            trans_out(25)
            maxes(28)
            trans_out(26)
            maxes(29)
            maxes(30)
            qk_out(0)
            max1(0)
            max2(0)
            p1_norm(0)
            maxes(31)
            max1(1)
            max2(1)
            trans_out(28)
            p1_norm(1)
            trans_out(29)
            pairs(0)
            trans_out(30)
            pt2_out(0)
            attn_norm(1)
            norm1_in(1)
            s2c_out(0)
            ctx_q_out(1)
            x1_out(1)
            xT_out(0, 1)
            mix(0)
            qk_out(1)
            norm2_in(0)
            max2(2)
            max1(2)
            x2_out(0)
            max1(3)
            xT_out(1, 0)
            p1_norm(2)
            p1_norm(3)
            max2(3)
            logits(0)
            pairs(1)
            combine(0)
            pt2_out(1)
            combT_out(0)
            x2_lo_of(0)
            s2c_out(1)
            scaled(0)
            x2c_lo_of(0)
            scaled(1)
            mix(1)
            x2c_lo_of(1)
            scaled(2)
            norm2_in(1)
            for n in range(0, 3):
                acts_of(n)
            scaled(3)
            x2_out(1)
            x2c_lo_of(2)
            x2c_lo_of(3)
            scaled(4)
            acts_of(3)
            scaled(5)
            acts_of(4)
            acts_of(5)
            x2c_lo_of(4)
            x2c_lo_of(5)
            xT_out(1, 1)
            scaled(6)
            acts_of(6)
            acts_of(7)
            logits(1)
            x2c_lo_of(6)
            for n in range(8, 11):
                acts_of(n)
            scaled(7)
            x2_lo_of(1)
            combine(1)
            x2c_lo_of(7)
            acts_of(11)
            combT_out(1)
            acts_of(12)
            acts_of(13)
            scaled(8)
            scaled(9)
            x2c_lo_of(8)
            acts_of(14)
            acts_of(15)
            x2c_lo_of(9)
            scaled(10)
            acts_of(16)
            scaled(11)
            x2c_lo_of(10)
            acts_of(17)
            acts_of(18)
            norm3_in(0)
            acts_of(19)
            y_out(0)
            ffn(20, B * E * HT)
            norm3_in(1)
            y_out(1)

        @block.tensor
        def _(pe):
            def mm(out, lhsT, rhs, start=True, stop=True, **kw):
                return nc.tensor.matmul(out, lhsT, rhs, start=start, stop=stop, **kw)

            pe.wait_ge(S["warm_ready"], 1)
            for _ in range(8):
                mm(banks[7], warm[:, 0:P], warm[:, :])
            pe.wait_ge(S["in_x"], 16)
            pe.wait_ge(S["in_wqkv"], 16)

            def project(i, b):
                c = slice(b * T, (b + 1) * T)
                mm(banks[PROJ[i][b]][:, 0:T], wqkv_s[:, 2 * i, :], xT_s[:, c])
                mm(banks[PROJ[i][b]][:, T:2 * T], wqkv_s[:, 2 * i + 1, :], xT_s[:, c]).then_inc(S["proj"], 1)

            def mean_squares(i, b):
                pe.wait_ge(S["sq_done"], 2 * b + i + 1)
                if b:
                    pe.wait_ge(S["rs_done"], 1 + 2 * i)
                mm(banks[MEAN[i][b]][:, 0:T], constf("mean8"), sq[:, i, b * T:(b + 1) * T]).then_inc(S["ms_done"], 1)

            def ctx_k(b):
                if b == 0:
                    pe.wait_ge(S["in_ctx"], 16)
                    pe.wait_ge(S["in_wx"], 16)
                pe.wait_ge(S["max_done"], H * (b + 1))
                mm(bk(b, "C"), wx("Wk_s"), ctxT_s[:, b * L:(b + 1) * L]).then_inc(S["ctx_mm"], 1)

            def ctx_q(b):
                mm(bk(b, "B"), wx("Wq_s"), ctxT_s[:, b * L:(b + 1) * L]).then_inc(S["ctx_mm"], 1)

            def ctx_v(b):
                pe.wait_ge(S["kv_ev"], 2 * b + 1)
                for t in range(4):
                    k = 4 * b + t
                    ins = mm(bk(b, "C")[:, t * P:(t + 1) * P], ctxT_s[:, k * P:(k + 1) * P], wx("Wv_s"))
                ins.then_inc(S["ctx_mm"], 1)

            project(0, 0)
            project(1, 0)
            pe.wait_ge(S["in_cf"], 16)
            mean_squares(0, 0)
            mean_squares(1, 0)
            project(0, 1)
            project(1, 1)
            for t in range(NT):
                ins = mm(banks[6][:, t * P:(t + 1) * P], xT_s[:, t * P:(t + 1) * P], wqkv_s[:, 4, :])
            ins.then_inc(S["vproj"], 1)
            mean_squares(0, 1)
            mean_squares(1, 1)

            pe.wait_ge(S["in_cb"], 16)

            def rows(p):
                r = slice(32 * (p // 2), 32 * (p // 2) + 32)
                if p:
                    pe.wait_ge(S["q_rows"], p)
                    pe.wait_ge(S["k_rows"], p)
                for i in range(2):
                    for n in range(PIECES):
                        ins = mm(banks[(7, 3)[i]][:, 0:T], sel_rows[r, p % 2, i, n, :], piece[r, i, n, 0:T],
                                 start=(n == 0), stop=(n == PIECES - 1))
                ins.then_inc(S["rows_mm"], 1)

            def scores(m):
                b, h = m // H, m % H
                if m >= H:
                    pe.wait_ge(S["max_done"], m - 1)
                elif m >= 3:
                    pe.wait_ge(S["max_done"], m - 2)
                if m < 2 * NR:
                    pe.wait_ge(S["q_rows"], m // 2 + 1)
                    pe.wait_ge(S["k_rows"], m // 2 + 1)
                elif m == 2 * NR or m == H:
                    pe.wait_ge(q6_in[b], 6 * 16)
                    pe.wait_ge(k6_in[b], 2 * 16)
                if m == 2:
                    pe.wait_ge(S["rot_done"], 3)
                o = score_bank(m)
                q0 = b * T
                mm(o[:, P:3 * P], Q6[:, h, q0 + P:q0 + T], K6[:, h // 2, q0:q0 + T])
                mm(o[:, 0:P], Q6[:, h, q0:q0 + P], K6[:, h // 2, q0:q0 + P]).then_inc(S["s_done"], 1)

            def transposes(m):
                if m == 0:
                    pe.wait_ge(S["rs_done"], 4)
                elif m == 1:
                    pe.wait_ge(S["rot_done"], 4)
                pe.wait_ge(S["exp_done"], m + 1)
                if m >= 2:
                    pe.wait_ge(*transposed(m - 2))
                for i in range(BLOCKS):
                    ins = nc.tensor.transpose(trans_bank(m)[:, i * P:(i + 1) * P], probs[:, m % 4, i * P:(i + 1) * P], ident)
                ins.then_inc(S["t_mm"], 1)

            def values(m):
                b, h = m // H, m % H
                if m == 0:
                    pe.wait_ge(S["vp_done"], 2)
                pe.wait_ge(*transposed(m))
                acc = banks[6 + b][:, (h // 8) * T:(h // 8 + 1) * T]
                mm(acc, VP[:, 2 * b, h, :], probsT[:, m % 4, 0:T], start=(h % 8 == 0), stop=False, skip_group_check=True)
                mm(acc[:, P:T], VP[:, 2 * b + 1, h, :], probsT[:, m % 4, T:T + P], start=False, stop=(h % 8 == 7),
                   skip_group_check=True).then_inc(S["pv_done"], 1)

            def heads(first, last):
                for m in range(first, last):
                    if m < 2 * NR - 2 and m % 2 == 0:
                        rows(m // 2 + 1)
                    if m < M:
                        scores(m)
                    if 2 <= m < M + 2:
                        transposes(m - 2)
                    if m >= 3:
                        values(m - 3)

            def attn_out(b):
                pe.wait_ge(S["in_wout"], 16)
                pe.wait_ge(S["attn_done"], b + 1)
                for t in (2 * b, 2 * b + 1):
                    ins = mm(bk(b, "A")[:, (t % 2) * P:(t % 2 + 1) * P], attnT[:, t * P:(t + 1) * P], wout_s[:, :])
                ins.then_inc(S["wout_done"], 1)

            def x_t(i, b):
                src = (x1, x2)[i]
                pe.wait_ge(S[("xn_done", "x2n_done")[i]], 2 * (b + 1))
                for t in (2 * b, 2 * b + 1):
                    ins = nc.tensor.transpose(bk(b, "A")[:, (t % 2) * P:(t % 2 + 1) * P], src[:, t, :], ident)
                ins.then_inc(S[("xt_mm", "x2t_mm")[i]], 1)

            def qk_char(b):
                c = slice(b * T, (b + 1) * T)
                pe.wait_ge(S["xt_done"], b + 1)
                mm(bk(b, "A")[:, 0:T], wx("Wq_c"), x1T[:, c])
                mm(bk(b, "A")[:, T:2 * T], wx("Wk_c"), x1T[:, c]).then_inc(S["qkc_mm"], 1)

            def v_char(b):
                pe.wait_ge(S["xt_done"], b + 1)
                pe.wait_ge(S["q_ev"], b + 1)
                for t in (2 * b, 2 * b + 1):
                    ins = mm(bk(b, "B")[:, (t % 2) * P:(t % 2 + 1) * P], x1T[:, t * P:(t + 1) * P], wx("Wv_c"))
                ins.then_inc(S["vc_mm"], 1)

            def s1(t):
                b = t // 2
                pe.wait_ge(S["qkc_done"], b + 1)
                pe.wait_ge(S["kv_ev"], 2 * b + 2)
                if t % 2:
                    pe.wait_ge(S["vc_done"], b + 1)
                mm(bk(b, "CB"[t % 2]), QcT[:, t * P:(t + 1) * P], KsT[:, b, :]).then_inc(S["s1_mm"], 1)

            def s2(h):
                b, half = h // 2, h % 2
                pe.wait_ge(S["qkc_done"], b + 1)
                pe.wait_ge(S["q_ev"], b + 1)
                if half:
                    pe.wait_ge(S["exp1_done"], 2 * b + 1)
                for s in (2 * half, 2 * half + 1):
                    ins = mm(bk(b, "AC"[half])[:, (s % 2) * T:(s % 2 + 1) * T], QsT[:, b, s * P:(s + 1) * P], KcT[:, b * T:(b + 1) * T])
                ins.then_inc(S["s2_mm"], 1)

            def pt1(t):
                b, q = t // 2, t % 2
                pe.wait_ge(S["p1n_done"], t + 1)
                pe.wait_ge(*((S["exp1_done"], 2 * b + 2) if q == 0 else (S["exp2_done"], 4 * b + 2)))
                for k in range(4):
                    ins = nc.tensor.transpose(bk(b, "BA"[q])[:, k * P:(k + 1) * P], P1[:, b, q, k * P:(k + 1) * P], ident)
                ins.then_inc(S["pt1_mm"], 1)

            def pt2(b):
                pe.wait_ge(S["pair_done"], b + 1)
                for k in range(2):
                    for s in range(4):
                        o = k * T + s * 64
                        ins = mm(bk(b, "C")[:, o:o + 64], P2[:, b, s, k * P:(k + 1) * P], pair_r[:, 4 * b + s, :])
                ins.then_inc(S["pt2_mm"], 1)

            def c2s_mm(b):
                pe.wait_ge(S["pt1_done"], 2 * (b + 1))
                for k in range(4):
                    ins = mm(bk(b, "B")[:, 0:T], Vs[:, 4 * b + k, :], PT1[:, b, k, :], start=(k == 0), stop=(k == 3))
                ins.then_inc(S["c2s_mm"], 1)

            def s2c_mm(b):
                pe.wait_ge(S["pt1_done"], 2 * (b + 1))
                pe.wait_ge(S["pt2_done"], b + 1)
                for k in range(2):
                    ins = mm(bk(b, "A")[:, 0:T], Vc[:, 2 * b + k, :], PT2[:, b, k, :], start=(k == 0), stop=(k == 1))
                ins.then_inc(S["s2c_mm"], 1)

            def gate_mm(b):
                c = slice(b * T, (b + 1) * T)
                pe.wait_ge(S["c2s_done"], b + 1)
                mm(bk(b, "C")[:, 0:T], wx("Wg_c"), c2s[:, c], stop=False)
                pe.wait_ge(S["s2c_done"], b + 1)
                mm(bk(b, "C")[:, 0:T], wx("Wg_s"), s2c[:, c], start=False).then_inc(S["gate_mm"], 1)

            def mix_t(b):
                pe.wait_ge(S["mix_done"], b + 1)
                for t in range(2):
                    ins = nc.tensor.transpose(bk(b, "B")[:, t * P:(t + 1) * P], mixT[:, b, t * P:(t + 1) * P], ident)
                ins.then_inc(S["mix_mm"], 1)

            def logit_mm(b):
                pe.wait_ge(S["rw_done"], 1)
                pe.wait_ge(S["x2t_done"], b + 1)
                for t in (2 * b, 2 * b + 1):
                    ins = mm(bk(b, "C")[:, (t % 2) * E:(t % 2 + 1) * E], x2T[:, t * P:(t + 1) * P], rw[:, :])
                ins.then_inc(S["logit_mm"], 1)

            def comb_t(b):
                pe.wait_ge(S["comb_done"], b + 1)
                for t in (2 * b, 2 * b + 1):
                    ins = nc.tensor.transpose(bk(b, "B").bitcast(BF16)[0:PIECES * E, (t % 2) * P:(t % 2 + 1) * P],
                                              combp[:, t, :, :].rearrange("p n e -> p (n e)"), identb)
                ins.then_inc(S["combT_mm"], 1)

            def spread(m):
                b, e = m // E, m % E
                pe.wait_ge(S["combT_done"], b + 1)
                if m >= 1:
                    pe.wait_ge(S["x2c_done"], m)
                mm(banks[SPREAD][:, 0:T], sel_expert[:, e, :], combT[:, b * T:(b + 1) * T]).then_inc(S["bc_mm"], 1)

            def by_parts(out, e, i, ht, x_hi, x_lo):
                at = (i * HT + ht) * P
                w_hi, w_lo = gat_hi[:, e, at:at + P], gat_lo[:, e, at:at + P]
                mm(out, w_hi, x_hi, stop=False)
                mm(out, w_hi, x_lo, start=False, stop=False)
                return mm(out, w_lo, x_hi, start=False)

            def gate_a(n):
                b, e, ht = n // (E * HT), n // HT % E, n % HT
                if n == 0:
                    pe.wait_ge(S["t_done_v"], M - M // 4)
                    pe.wait_ge(S["t_done_a"], M // 4)
                if n == 2:
                    pe.wait_ge(S["combT_done"], 1)
                pe.wait_ge(S["x2t_done"], b + 1)
                if n >= 3:
                    pe.wait_ge(S["act_done"], n - 2)
                pe.wait_ge(S["w_split"], e + 1)
                pe.wait_ge(S["x2_lo_done"], b + 1)
                by_parts(banks[FBANKS[n % 3]][:, 0:T], e, 0, ht, x2_hi[:, b, :], x2_lo[:, b, :])

            def gate_b(n):
                b, e, ht = n // (E * HT), n // HT % E, n % HT
                m = b * E + e
                pe.wait_ge(S["x2c_lo_done"], m + 1)
                by_parts(banks[FBANKS[n % 3]][:, T:2 * T], e, 1, ht, x2c_hi[:, m % RING, :], x2c_lo[:, m % RING, :]).then_inc(S["gates_mm"], 1)

            def down(n):
                b, e, ht = n // (E * HT), n // HT % E, n % HT
                i = n % (E * HT)
                if n == 0:
                    pe.wait_ge(S["in_lin"], 16)
                pe.wait_ge(S["act_done"], n + 1)
                for t in range(2):
                    ins = mm(banks[DOWN[b]][:, t * P:(t + 1) * P], acts[:, n % 4, t * P:(t + 1) * P], lin_s[:, e, ht, :],
                             start=(i == 0 and t == 0), stop=(i == E * HT - 1), skip_group_check=True)
                ins.then_inc(S["out_mm"], 1)

            def ffn(first, last):
                for n in range(first, last):
                    gate_a(n)
                    gate_b(n)
                    if n % HT == 1 and n // HT + 2 < B * E:
                        spread(n // HT + 2)
                    if n >= 1:
                        down(n - 1)

            for _ in range(6):
                mm(banks[3][:, 0:480], warm[:, 0:P], warm[:, 0:480])
            pe.wait_ge(S["p2q"], 1)
            pe.wait_ge(S["p2k"], 1)
            rows(0)
            heads(0, H)
            scores(16)
            scores(17)
            transposes(14)
            values(13)
            transposes(15)
            scores(18)
            scores(19)
            ctx_k(0)
            transposes(16)
            transposes(17)
            values(14)
            values(15)
            scores(20)
            ctx_q(0)
            ctx_v(0)
            transposes(18)
            scores(21)
            scores(22)
            transposes(19)
            attn_out(0)
            transposes(20)
            values(16)
            scores(23)
            values(17)
            values(18)
            scores(24)
            transposes(21)
            values(19)
            transposes(22)
            values(20)
            scores(25)
            scores(26)
            transposes(23)
            values(21)
            values(22)
            scores(27)
            values(23)
            x_t(0, 0)
            transposes(24)
            transposes(25)
            scores(28)
            v_char(0)
            transposes(26)
            values(24)
            scores(29)
            scores(30)
            qk_char(0)
            scores(31)
            values(25)
            values(26)
            s1(0)
            s2(0)
            s1(1)
            transposes(27)
            transposes(28)
            s2(1)
            ctx_k(1)
            transposes(29)
            values(27)
            pt1(0)
            transposes(30)
            values(28)
            values(29)
            transposes(31)
            values(30)
            pt1(1)
            values(31)
            pt2(0)
            c2s_mm(0)
            attn_out(1)
            s2c_mm(0)
            ctx_q(1)
            ctx_v(1)
            gate_mm(0)
            x_t(0, 1)
            v_char(1)
            qk_char(1)
            mix_t(0)
            s2(2)
            s1(2)
            s1(3)
            x_t(1, 0)
            s2(3)
            logit_mm(0)
            pt1(2)
            pt1(3)
            c2s_mm(1)
            pt2(1)
            comb_t(0)
            s2c_mm(1)
            spread(0)
            for n in range(0, 3):
                gate_a(n)
            gate_mm(1)
            spread(1)
            gate_b(0)
            gate_b(1)
            spread(2)
            mix_t(1)
            gate_b(2)
            spread(3)
            gate_a(3)
            down(0)
            down(1)
            spread(4)
            gate_a(4)
            gate_a(5)
            for n in range(3, 6):
                gate_b(n)
            spread(5)
            x_t(1, 1)
            down(2)
            gate_a(6)
            gate_b(6)
            gate_a(7)
            spread(6)
            gate_b(7)
            down(3)
            down(4)
            logit_mm(1)
            for n in range(8, 11):
                gate_a(n)
            for n in range(8, 11):
                gate_b(n)
            for n in range(5, 8):
                down(n)
            spread(7)
            gate_a(11)
            down(8)
            down(9)
            gate_b(11)
            down(10)
            gate_a(12)
            gate_a(13)
            gate_b(12)
            gate_b(13)
            comb_t(1)
            down(11)
            spread(8)
            gate_a(14)
            gate_a(15)
            gate_b(14)
            spread(9)
            gate_b(15)
            gate_a(16)
            down(12)
            down(13)
            gate_a(17)
            gate_a(18)
            gate_b(16)
            spread(10)
            down(14)
            gate_b(17)
            spread(11)
            gate_b(18)
            gate_a(19)
            for n in range(15, 19):
                down(n)
            gate_b(19)
            ffn(20, B * E * HT)
            down(B * E * HT - 1)


def _constants():
    import numpy as np

    def bf16_bits(a):
        return (np.ascontiguousarray(a, np.float32).view(np.uint32) >> 16).astype(np.uint16)

    ident = np.eye(P, dtype=np.float32)
    half = D // 2
    inv_freq = (1.0 / np.float32(10000.0) ** (np.arange(half, dtype=np.float32) * np.float32(2.0) / np.float32(D))).astype(np.float32)
    ang = (np.arange(T, dtype=np.float32)[:, None] * inv_freq[None, :]).astype(np.float32)
    c, s = np.cos(ang).T, np.sin(ang).T
    cos = np.tile(np.concatenate([c, c]), (H, 1))
    sin = np.tile(np.concatenate([-s, s]), (H, 1))
    mean8 = np.kron(np.eye(H), np.full((D, D), 1.0 / D))
    pair = np.kron(np.eye(P // 2), np.full((2, 1), 0.5))
    i = np.arange(P)
    mask = np.where(i[:, None] < i[None, :], np.float32(FORBIDDEN), np.float32(0))
    const_f = np.concatenate([ident, cos, sin, mean8, pair, np.zeros((P, P)), mask], 1).astype(np.float32)
    sel_expert = np.zeros((P, E, P), np.float32)
    for n in range(PIECES):
        sel_expert[n * E + np.arange(E), np.arange(E)] = 1.0
    sel_rows = np.zeros((P, 2, 2, PIECES, P), np.float32)
    for r in range(P):
        pair, odd, d = r // 16, r // D % 2, r % D
        for i, pieces in enumerate((Q_PIECE, K_PIECE)):
            for slot, n in enumerate(pieces):
                sel_rows[r, pair % 2, i, n, 64 * odd + slot * D + d] = 1.0
    const_b = bf16_bits(np.concatenate([ident, sel_expert.reshape(P, -1), sel_rows.reshape(P, -1)], 1))
    return np.ascontiguousarray(const_f), const_b


def kernel(**inputs):
    import numpy as np
    import concourse.bacc as bacc
    from concourse import mybir as mb
    from concourse.bass_utils import run_bass_kernel_spmd as run

    a = {k: np.asarray(v) for k, v in inputs.items()}
    tok = a["x"].reshape(N, C)
    w = a["L0_attn_w_qkv"].reshape(3, H, D, C)
    swapped = np.concatenate([w[:, :, D // 2:], w[:, :, :D // 2]], 2)

    def cols(m):
        return m.reshape(P, C).T

    wx = {n: a["L0_xattn_" + n].T for n in WX if not n.startswith("Wg")}
    wx["Wg_c"], wx["Wg_s"] = a["L0_xattn_Wg"][:, :C].T, a["L0_xattn_Wg"][:, C:].T
    small = [a["L0_xattn_" + n][:, None] for n in ("bq_c", "bk_s", "bv_s", "bq_s", "bk_c", "bv_c", "bg")]
    small += [np.tile(a["L0_attn_q_norm_w"], H)[:, None], np.tile(a["L0_attn_k_norm_w"], H)[:, None]]
    small += [a["L0_ffn_router_scale"][:, None], a["L0_ffn_router_w"]]
    small += [np.broadcast_to(a["L0_ffn_per_expert_scale"], (P, E))]
    const_f, const_b = _constants()
    arrays = {
        "xT": tok.T,
        "x_tok": tok.reshape(NT, P, C).transpose(1, 0, 2),
        "ctxT": a["ctx_1024"].reshape(B * L, C).T,
        "w_qkv": np.stack([cols(w[0]), cols(swapped[0]), cols(w[1]), cols(swapped[1]), cols(w[2])], 1),
        "w_out": a["L0_attn_w_out"].T,
        "w_x": np.stack([wx[n] for n in WX], 1),
        "small": np.concatenate(small, 1),
        "gating": a["L0_ffn_gating_w"].reshape(E, 2, HT, P, C).transpose(4, 0, 1, 2, 3),
        "linear": a["L0_ffn_linear_w"].reshape(E, HT, P, C).transpose(2, 0, 1, 3),
        "const_f": const_f,
        "const_b": const_b,
    }
    arrays = {k: np.ascontiguousarray(v) for k, v in arrays.items()}
    nc = bacc.Bacc("TRN2", target_bir_lowering=False, num_devices=1)
    args = [nc.dram_tensor(k, v.shape, mb.dt.from_np(v.dtype), kind="ExternalInput").ap() for k, v in arrays.items()]
    out = nc.dram_tensor("out", (P, NT, C), mb.dt.float32, kind="ExternalOutput").ap()
    post_norm_decoder(nc, *args, out)
    r = run(nc, [arrays], core_ids=[0])
    y = r.results[0]["out"]
    return np.ascontiguousarray(y.transpose(1, 0, 2)).reshape(B, T, C)
```
